# Optimizing a Trainium2 kernel written in Bass

```python
import numpy as np
import jax
import jax.numpy as jnp

def _softmax(x, axis=-1):
    return jax.nn.softmax(x, axis=axis)

def _gelu(x):
    return jax.nn.gelu(x, approximate=True)

def _silu(x):
    return jax.nn.silu(x)

def _sigmoid(x):
    return jax.nn.sigmoid(x)

def _layernorm(x, axis=-1, eps=1e-05):
    m = jnp.mean(x, axis=axis, keepdims=True)
    v = jnp.var(x, axis=axis, keepdims=True)
    return (x - m) / jnp.sqrt(v + eps)

def _scatter_add(tgt, idx, src, axis=0):
    return tgt.at[idx].add(src)

def _segment_sum(src, seg, n):
    return jax.ops.segment_sum(src, seg, n)
kernel_name = 'mk_lm_tower_d2_tok_ids1024_r4_1094bd'

def setup_inputs(seed: int=0):
    np.random.seed(seed)
    _w = jnp.asarray

    def _rec_inputs():
        import jax
        import jax.numpy as jnp
        _rk = jax.random.key(seed)
        x = jax.random.randint(jax.random.fold_in(_rk, 1), (8, 256), 0, 28, jnp.int32)
        mask_BS_i1_0 = jnp.where(jnp.ones((8, 256), dtype=bool), 1, 0).astype(jnp.int32)
        return (x, mask_BS_i1_0)
    x, mask_BS_i1_0 = _rec_inputs()

    def _L0_tok_setup():
        import jax, jax.numpy as jnp
        import numpy as np
        WINDOW_SIZE = 3
        LN_EPS = 1e-05

        def _sliding_window_features(base_pca, mask_f):
            B, S, F = base_pca.shape
            h = WINDOW_SIZE // 2
            idx = jnp.arange(S)
            start = jnp.maximum(idx - h, 0)
            end = jnp.minimum(idx + h + 1, S)
            masked = base_pca * mask_f[..., None]
            csum = jnp.pad(jnp.cumsum(masked, axis=1), ((0, 0), (1, 0), (0, 0)))
            wsum = csum[:, end, :] - csum[:, start, :]
            mcs = jnp.pad(jnp.cumsum(mask_f, axis=1), ((0, 0), (1, 0)))
            lengths = jnp.maximum(mcs[:, end] - mcs[:, start], 1.0)
            return wsum / lengths[..., None]
        key = jax.random.key(seed)
        ks = jax.random.split(key, 8)
        B, S, V, E = (8, 1024, 28, 256)
        input_ids = jax.random.randint(ks[0], (B, S), 0, V, dtype=jnp.int64)
        attention_mask = jnp.ones((B, S), dtype=jnp.int32)
        emb = jax.random.normal(ks[1], (V, E), dtype=jnp.float32) * 0.02
        emb = emb.at[0].set(0.0)
        pca_lookup = jax.random.normal(ks[2], (V, 20), dtype=jnp.float32)
        proj_w = jax.random.normal(ks[3], (20, E), dtype=jnp.float32) * 0.2
        proj_b = jnp.zeros((E,), dtype=jnp.float32)
        fus_w = jax.random.normal(ks[4], (2 * E, E), dtype=jnp.float32) * 0.02
        fus_b = jnp.zeros((E,), dtype=jnp.float32)
        ln_g = jnp.ones((E,), dtype=jnp.float32)
        ln_b = jnp.zeros((E,), dtype=jnp.float32)
        return {'input_ids': input_ids, 'attention_mask': attention_mask, 'emb': emb, 'pca_lookup': pca_lookup, 'proj_w': proj_w, 'proj_b': proj_b, 'fus_w': fus_w, 'fus_b': fus_b, 'ln_g': ln_g, 'ln_b': ln_b}
    _L0_tok_all = _L0_tok_setup()
    _L0_tok_in = {k: v for k, v in _L0_tok_all.items() if k in ('emb', 'pca_lookup', 'proj_w', 'proj_b', 'fus_w', 'fus_b', 'ln_g', 'ln_b')}
    del _L0_tok_all

    def _L0_attn_setup():
        import jax, jax.numpy as jnp
        import numpy as np
        D_MODEL = 256
        N_HEADS = 16
        HEAD_DIM = D_MODEL // N_HEADS
        LORA_RANK = 16
        LORA_SCALING = 1.0 / LORA_RANK

        def lora_linear(x, w, a, b):
            return x @ w.T + LORA_SCALING * (x @ a.T @ b.T)
        key = jax.random.key(seed)
        ks = jax.random.split(key, 14)
        B, S = (4, 512)

        def w(k, shape, scale=0.02):
            return jax.random.normal(k, shape, dtype=jnp.float32) * scale
        inp = {'x': jax.random.normal(ks[0], (B, S, D_MODEL), dtype=jnp.float32), 'wq': w(ks[1], (D_MODEL, D_MODEL)), 'aq': w(ks[2], (LORA_RANK, D_MODEL)), 'bq': w(ks[3], (D_MODEL, LORA_RANK)), 'wk': w(ks[4], (D_MODEL, D_MODEL)), 'ak': w(ks[5], (LORA_RANK, D_MODEL)), 'bk': w(ks[6], (D_MODEL, LORA_RANK)), 'wv': w(ks[7], (D_MODEL, D_MODEL)), 'av': w(ks[8], (LORA_RANK, D_MODEL)), 'bv': w(ks[9], (D_MODEL, LORA_RANK)), 'wo': w(ks[10], (D_MODEL, D_MODEL)), 'ao': w(ks[11], (LORA_RANK, D_MODEL)), 'bo': w(ks[12], (D_MODEL, LORA_RANK))}
        return inp
    _L0_attn_all = _L0_attn_setup()
    _L0_attn_in = {k: v for k, v in _L0_attn_all.items() if k in ('wq', 'aq', 'bq', 'wk', 'ak', 'bk', 'wv', 'av', 'bv', 'wo', 'ao', 'bo')}
    del _L0_attn_all

    def _L0_ffn_setup():
        import jax, jax.numpy as jnp
        import numpy as np
        BLOCK = 16
        _GRID = jnp.array([0.0, 0.5, 1.0, 1.5, 2.0, 3.0, 4.0, 6.0], dtype=jnp.float32)
        _MID = jnp.array([0.25, 0.75, 1.25, 1.75, 2.5, 3.5, 5.0], dtype=jnp.float32)

        def fp4_quant_dequant(x):
            shape = x.shape
            xb = x.reshape(shape[:-1] + (shape[-1] // BLOCK, BLOCK))
            scale = jnp.max(jnp.abs(xb), axis=-1, keepdims=True) / 6.0
            scale = jnp.maximum(scale, jnp.float32(1e-12))
            xn = xb / scale
            idx = jnp.searchsorted(_MID, jnp.abs(xn))
            q = _GRID[idx] * jnp.sign(xn) * scale
            return q.reshape(shape)

        def fp4_linear(x, w):
            xq = fp4_quant_dequant(x)
            wq = fp4_quant_dequant(w)
            return jnp.einsum('bsk,nk->bsn', xq, wq)
        key = jax.random.key(seed)
        k1, k2, k3, k4 = jax.random.split(key, 4)
        H, I = (256, 704)
        x = jax.random.normal(k1, (4, 1024, H), dtype=jnp.float32)
        w_gate = jax.random.normal(k2, (I, H), dtype=jnp.float32) * 0.02
        w_up = jax.random.normal(k3, (I, H), dtype=jnp.float32) * 0.02
        w_down = jax.random.normal(k4, (H, I), dtype=jnp.float32) * 0.02
        return {'x': x, 'w_gate': w_gate, 'w_up': w_up, 'w_down': w_down}
    _L0_ffn_all = _L0_ffn_setup()
    _L0_ffn_in = {k: v for k, v in _L0_ffn_all.items() if k in ('w_gate', 'w_up', 'w_down')}
    del _L0_ffn_all

    def _L1_attn_setup():
        import jax, jax.numpy as jnp
        import numpy as np
        HEADS = 16
        HEAD_DIM = 64
        DIM = 256
        INNER = HEADS * HEAD_DIM
        EPS = 1e-05
        key = jax.random.key(seed)
        ks = jax.random.split(key, 7)
        s_qkv = (2.0 / (DIM + 3 * INNER)) ** 0.5
        s_out = (2.0 / (INNER + DIM)) ** 0.5
        return {'x': jax.random.normal(ks[0], (4, 512, DIM), dtype=jnp.float32), 'w_qkv': jax.random.normal(ks[1], (DIM, 3 * INNER), dtype=jnp.float32) * s_qkv, 'b_qkv': jnp.zeros((3 * INNER,), dtype=jnp.float32), 'w_out': jax.random.normal(ks[2], (INNER, DIM), dtype=jnp.float32) * s_out, 'b_out': jnp.zeros((DIM,), dtype=jnp.float32), 'ln_gamma': jnp.ones((DIM,), dtype=jnp.float32), 'ln_beta': jnp.zeros((DIM,), dtype=jnp.float32)}
    _L1_attn_all = _L1_attn_setup()
    _L1_attn_in = {k: v for k, v in _L1_attn_all.items() if k in ('w_qkv', 'b_qkv', 'w_out', 'b_out', 'ln_gamma', 'ln_beta')}
    del _L1_attn_all

    def _L1_ffn_setup():
        import jax, jax.numpy as jnp
        import numpy as np
        DIM = 256
        DEPTH = 6
        HEADS = 16
        DIM_HEAD = 64
        WINDOW = 64
        INNER = HEADS * DIM_HEAD
        DIM_INNER = int(DIM * 4 * 2 / 3)
        QK_SCALE = 8.0

        def shift_tokens(t):
            a, s = jnp.split(t, 2, -1)
            s = jnp.pad(s, ((0, 0), (1, 0), (0, 0)))[:, :-1]
            return jnp.concatenate([a, s], -1)

        def l2norm(t):
            return t / jnp.maximum(jnp.linalg.norm(t, axis=-1, keepdims=True), 1e-12)

        def rotate_half(x):
            x1, x2 = jnp.split(x, 2, -1)
            return jnp.concatenate([-x2, x1], -1)

        def rotary_tables(n):
            half = jnp.arange(0, DIM_HEAD, 2, dtype=jnp.float32)
            inv_freq = 1.0 / 10000.0 ** (half / DIM_HEAD)
            t = jnp.arange(n, dtype=jnp.float32)
            freqs = t[:, None] * inv_freq[None, :]
            freqs = jnp.concatenate([freqs, freqs], -1)
            base_scale = (half + 0.4 * DIM_HEAD) / (1.4 * DIM_HEAD)
            power = (t - n // 2) / (WINDOW // 2)
            scale = base_scale[None, :] ** power[:, None]
            scale = jnp.concatenate([scale, scale], -1)
            return (freqs, scale)

        def local_attention(q, k, v):
            b, h, n, d = q.shape
            w = WINDOW
            nw = n // w
            bq = q.reshape(b, h, nw, w, d)
            bk = k.reshape(b, h, nw, w, d)
            bv = v.reshape(b, h, nw, w, d)

            def look(t):
                p = jnp.pad(t, ((0, 0), (0, 0), (1, 0), (0, 0), (0, 0)))
                return jnp.concatenate([p[:, :, :nw], p[:, :, 1:]], axis=3)
            bk2, bv2 = (look(bk), look(bv))
            seq = jnp.arange(n).reshape(nw, w)
            seq_p = jnp.pad(seq, ((1, 0), (0, 0)), constant_values=-1)
            jt = jnp.concatenate([seq_p[:nw], seq_p[1:]], axis=1)
            it = seq[:, :, None]
            jb = jt[:, None, :]
            mask = (it < jb) | (it > jb + w) | (jb == -1)
            sim = jnp.einsum('bhwie,bhwje->bhwij', bq, bk2) * QK_SCALE
            sim = jnp.where(mask, -jnp.finfo(sim.dtype).max, sim)
            attn = jax.nn.softmax(sim, -1)
            out = jnp.einsum('bhwij,bhwje->bhwie', attn, bv2)
            return out.reshape(b, h, n, d)

        def attn_layer(x, Wqkv, qs, ksc, Wo):
            b, n, _ = x.shape
            qkv = x @ Wqkv
            q, k, v = jnp.split(qkv, 3, -1)
            sh = lambda t: t.reshape(b, n, HEADS, DIM_HEAD).transpose(0, 2, 1, 3)
            q, k, v = (sh(q), sh(k), sh(v))
            q = l2norm(q) * qs
            k = l2norm(k) * ksc
            freqs, scale = rotary_tables(n)
            cos, sin = (jnp.cos(freqs), jnp.sin(freqs))
            q = q * cos * scale + rotate_half(q) * sin * scale
            inv = 1.0 / scale
            k = k * cos * inv + rotate_half(k) * sin * inv
            out = local_attention(q, k, v)
            out = out.transpose(0, 2, 1, 3).reshape(b, n, INNER)
            return out @ Wo

        def ffn_layer(x, g, bln, W1, b1, W2, b2):
            mu = x.mean(-1, keepdims=True)
            var = ((x - mu) ** 2).mean(-1, keepdims=True)
            xn = (x - mu) / jnp.sqrt(var + 1e-05) * g + bln
            hg = xn @ W1 + b1
            a, gate = jnp.split(hg, 2, -1)
            return a * jax.nn.gelu(gate, approximate=False) @ W2 + b2
        key = jax.random.key(seed)
        ks = jax.random.split(key, 8)
        B, N = (2, 512)
        init = lambda k, shape: jax.random.normal(k, shape, jnp.float32) * 0.02
        return {'x': jax.random.normal(ks[0], (B, N, DIM), jnp.float32), 'Wqkv': init(ks[1], (DEPTH, DIM, 3 * INNER)), 'q_scale': jnp.ones((DEPTH, DIM_HEAD), jnp.float32), 'k_scale': jnp.ones((DEPTH, DIM_HEAD), jnp.float32), 'Wo': init(ks[2], (DEPTH, INNER, DIM)), 'ln_g': jnp.ones((DEPTH, DIM), jnp.float32), 'ln_b': jnp.zeros((DEPTH, DIM), jnp.float32), 'W1': init(ks[3], (DEPTH, DIM, 2 * DIM_INNER)), 'b1': jnp.zeros((DEPTH, 2 * DIM_INNER), jnp.float32), 'W2': init(ks[4], (DEPTH, DIM_INNER, DIM)), 'b2': jnp.zeros((DEPTH, DIM), jnp.float32)}
    _L1_ffn_all = _L1_ffn_setup()
    _L1_ffn_in = {k: v for k, v in _L1_ffn_all.items() if k in ('Wqkv', 'q_scale', 'k_scale', 'Wo', 'ln_g', 'ln_b', 'W1', 'b1', 'W2', 'b2')}
    del _L1_ffn_all
    return {'x': x, 'mask_BS_i1_0': mask_BS_i1_0, 'L0_tok_emb': _L0_tok_in['emb'], 'L0_tok_pca_lookup': _L0_tok_in['pca_lookup'], 'L0_tok_proj_w': _L0_tok_in['proj_w'], 'L0_tok_proj_b': _L0_tok_in['proj_b'], 'L0_tok_fus_w': _L0_tok_in['fus_w'], 'L0_tok_fus_b': _L0_tok_in['fus_b'], 'L0_tok_ln_g': _L0_tok_in['ln_g'], 'L0_tok_ln_b': _L0_tok_in['ln_b'], 'L0_attn_wq': _L0_attn_in['wq'], 'L0_attn_aq': _L0_attn_in['aq'], 'L0_attn_bq': _L0_attn_in['bq'], 'L0_attn_wk': _L0_attn_in['wk'], 'L0_attn_ak': _L0_attn_in['ak'], 'L0_attn_bk': _L0_attn_in['bk'], 'L0_attn_wv': _L0_attn_in['wv'], 'L0_attn_av': _L0_attn_in['av'], 'L0_attn_bv': _L0_attn_in['bv'], 'L0_attn_wo': _L0_attn_in['wo'], 'L0_attn_ao': _L0_attn_in['ao'], 'L0_attn_bo': _L0_attn_in['bo'], 'L0_ffn_w_gate': _L0_ffn_in['w_gate'], 'L0_ffn_w_up': _L0_ffn_in['w_up'], 'L0_ffn_w_down': _L0_ffn_in['w_down'], 'L1_attn_w_qkv': _L1_attn_in['w_qkv'], 'L1_attn_b_qkv': _L1_attn_in['b_qkv'], 'L1_attn_w_out': _L1_attn_in['w_out'], 'L1_attn_b_out': _L1_attn_in['b_out'], 'L1_attn_ln_gamma': _L1_attn_in['ln_gamma'], 'L1_attn_ln_beta': _L1_attn_in['ln_beta'], 'L1_ffn_Wqkv': _L1_ffn_in['Wqkv'], 'L1_ffn_q_scale': _L1_ffn_in['q_scale'], 'L1_ffn_k_scale': _L1_ffn_in['k_scale'], 'L1_ffn_Wo': _L1_ffn_in['Wo'], 'L1_ffn_ln_g': _L1_ffn_in['ln_g'], 'L1_ffn_ln_b': _L1_ffn_in['ln_b'], 'L1_ffn_W1': _L1_ffn_in['W1'], 'L1_ffn_b1': _L1_ffn_in['b1'], 'L1_ffn_W2': _L1_ffn_in['W2'], 'L1_ffn_b2': _L1_ffn_in['b2']}

def reference(x, mask_BS_i1_0, L0_tok_emb, L0_tok_pca_lookup, L0_tok_proj_w, L0_tok_proj_b, L0_tok_fus_w, L0_tok_fus_b, L0_tok_ln_g, L0_tok_ln_b, L0_attn_wq, L0_attn_aq, L0_attn_bq, L0_attn_wk, L0_attn_ak, L0_attn_bk, L0_attn_wv, L0_attn_av, L0_attn_bv, L0_attn_wo, L0_attn_ao, L0_attn_bo, L0_ffn_w_gate, L0_ffn_w_up, L0_ffn_w_down, L1_attn_w_qkv, L1_attn_b_qkv, L1_attn_w_out, L1_attn_b_out, L1_attn_ln_gamma, L1_attn_ln_beta, L1_ffn_Wqkv, L1_ffn_q_scale, L1_ffn_k_scale, L1_ffn_Wo, L1_ffn_ln_g, L1_ffn_ln_b, L1_ffn_W1, L1_ffn_b1, L1_ffn_W2, L1_ffn_b2):
    import jax
    import jax.numpy as jnp

    def _L0_tok_ref(input_ids, attention_mask, emb, pca_lookup, proj_w, proj_b, fus_w, fus_b, ln_g, ln_b):
        import jax, jax.numpy as jnp
        import numpy as np
        WINDOW_SIZE = 3
        LN_EPS = 1e-05

        def _sliding_window_features(base_pca, mask_f):
            B, S, F = base_pca.shape
            h = WINDOW_SIZE // 2
            idx = jnp.arange(S)
            start = jnp.maximum(idx - h, 0)
            end = jnp.minimum(idx + h + 1, S)
            masked = base_pca * mask_f[..., None]
            csum = jnp.pad(jnp.cumsum(masked, axis=1), ((0, 0), (1, 0), (0, 0)))
            wsum = csum[:, end, :] - csum[:, start, :]
            mcs = jnp.pad(jnp.cumsum(mask_f, axis=1), ((0, 0), (1, 0)))
            lengths = jnp.maximum(mcs[:, end] - mcs[:, start], 1.0)
            return wsum / lengths[..., None]
        token_embeds = emb[input_ids]
        base_pca = pca_lookup[input_ids]
        pca_feat = _sliding_window_features(base_pca, attention_mask.astype(jnp.float32))
        cont = pca_feat @ proj_w + proj_b
        combined = jnp.concatenate([token_embeds, cont], axis=-1)
        fused = combined @ fus_w + fus_b
        mu = jnp.mean(fused, axis=-1, keepdims=True)
        var = jnp.mean(jnp.square(fused - mu), axis=-1, keepdims=True)
        return (fused - mu) * jax.lax.rsqrt(var + LN_EPS) * ln_g + ln_b

    def _L0_attn_ref(x, wq, aq, bq, wk, ak, bk, wv, av, bv, wo, ao, bo):
        import jax, jax.numpy as jnp
        import numpy as np
        D_MODEL = 256
        N_HEADS = 16
        HEAD_DIM = D_MODEL // N_HEADS
        LORA_RANK = 16
        LORA_SCALING = 1.0 / LORA_RANK

        def lora_linear(x, w, a, b):
            return x @ w.T + LORA_SCALING * (x @ a.T @ b.T)
        B, S, _ = x.shape

        def split_heads(t):
            return t.reshape(B, S, N_HEADS, HEAD_DIM).transpose(0, 2, 1, 3)
        q = split_heads(lora_linear(x, wq, aq, bq))
        k = split_heads(lora_linear(x, wk, ak, bk))
        v = split_heads(lora_linear(x, wv, av, bv))
        scores = jnp.einsum('bhqd,bhkd->bhqk', q, k) / jnp.sqrt(jnp.float32(HEAD_DIM))
        causal = jnp.tril(jnp.ones((S, S), dtype=bool))
        scores = jnp.where(causal, scores, -jnp.inf)
        attn = jax.nn.softmax(scores, axis=-1)
        ctx = jnp.einsum('bhqk,bhkd->bhqd', attn, v)
        ctx = ctx.transpose(0, 2, 1, 3).reshape(B, S, D_MODEL)
        return lora_linear(ctx, wo, ao, bo)

    def _L0_ffn_ref(x, w_gate, w_up, w_down):
        import jax, jax.numpy as jnp
        import numpy as np
        BLOCK = 16
        _GRID = jnp.array([0.0, 0.5, 1.0, 1.5, 2.0, 3.0, 4.0, 6.0], dtype=jnp.float32)
        _MID = jnp.array([0.25, 0.75, 1.25, 1.75, 2.5, 3.5, 5.0], dtype=jnp.float32)

        def fp4_quant_dequant(x):
            shape = x.shape
            xb = x.reshape(shape[:-1] + (shape[-1] // BLOCK, BLOCK))
            scale = jnp.max(jnp.abs(xb), axis=-1, keepdims=True) / 6.0
            scale = jnp.maximum(scale, jnp.float32(1e-12))
            xn = xb / scale
            idx = jnp.searchsorted(_MID, jnp.abs(xn))
            q = _GRID[idx] * jnp.sign(xn) * scale
            return q.reshape(shape)

        def fp4_linear(x, w):
            xq = fp4_quant_dequant(x)
            wq = fp4_quant_dequant(w)
            return jnp.einsum('bsk,nk->bsn', xq, wq)
        gate = fp4_linear(x, w_gate)
        y = fp4_linear(x, w_up)
        h = jax.nn.silu(gate) * y
        return fp4_linear(h, w_down)

    def _L1_attn_ref(x, w_qkv, b_qkv, w_out, b_out, ln_gamma, ln_beta):
        import jax, jax.numpy as jnp
        import numpy as np
        HEADS = 16
        HEAD_DIM = 64
        DIM = 256
        INNER = HEADS * HEAD_DIM
        EPS = 1e-05
        mu = jnp.mean(x, axis=-1, keepdims=True)
        var = jnp.var(x, axis=-1, keepdims=True)
        xn = (x - mu) * jax.lax.rsqrt(var + EPS) * ln_gamma + ln_beta
        qkv = xn @ w_qkv + b_qkv
        q, k, v = jnp.split(qkv, 3, axis=-1)
        b, l, _ = x.shape

        def heads(t):
            return t.reshape(b, l, HEADS, HEAD_DIM).transpose(0, 2, 1, 3)
        q, k, v = (heads(q), heads(k), heads(v))
        scale = HEAD_DIM ** (-0.5)
        scores = jnp.einsum('bhqd,bhkd->bhqk', q, k) * scale
        att = jax.nn.softmax(scores, axis=-1)
        out = jnp.einsum('bhqk,bhkd->bhqd', att, v)
        out = out.transpose(0, 2, 1, 3).reshape(b, l, INNER)
        return out @ w_out + b_out

    def _L1_ffn_ref(x, Wqkv, q_scale, k_scale, Wo, ln_g, ln_b, W1, b1, W2, b2):
        import jax, jax.numpy as jnp
        import numpy as np
        DIM = 256
        DEPTH = 6
        HEADS = 16
        DIM_HEAD = 64
        WINDOW = 64
        INNER = HEADS * DIM_HEAD
        DIM_INNER = int(DIM * 4 * 2 / 3)
        QK_SCALE = 8.0

        def shift_tokens(t):
            a, s = jnp.split(t, 2, -1)
            s = jnp.pad(s, ((0, 0), (1, 0), (0, 0)))[:, :-1]
            return jnp.concatenate([a, s], -1)

        def l2norm(t):
            return t / jnp.maximum(jnp.linalg.norm(t, axis=-1, keepdims=True), 1e-12)

        def rotate_half(x):
            x1, x2 = jnp.split(x, 2, -1)
            return jnp.concatenate([-x2, x1], -1)

        def rotary_tables(n):
            half = jnp.arange(0, DIM_HEAD, 2, dtype=jnp.float32)
            inv_freq = 1.0 / 10000.0 ** (half / DIM_HEAD)
            t = jnp.arange(n, dtype=jnp.float32)
            freqs = t[:, None] * inv_freq[None, :]
            freqs = jnp.concatenate([freqs, freqs], -1)
            base_scale = (half + 0.4 * DIM_HEAD) / (1.4 * DIM_HEAD)
            power = (t - n // 2) / (WINDOW // 2)
            scale = base_scale[None, :] ** power[:, None]
            scale = jnp.concatenate([scale, scale], -1)
            return (freqs, scale)

        def local_attention(q, k, v):
            b, h, n, d = q.shape
            w = WINDOW
            nw = n // w
            bq = q.reshape(b, h, nw, w, d)
            bk = k.reshape(b, h, nw, w, d)
            bv = v.reshape(b, h, nw, w, d)

            def look(t):
                p = jnp.pad(t, ((0, 0), (0, 0), (1, 0), (0, 0), (0, 0)))
                return jnp.concatenate([p[:, :, :nw], p[:, :, 1:]], axis=3)
            bk2, bv2 = (look(bk), look(bv))
            seq = jnp.arange(n).reshape(nw, w)
            seq_p = jnp.pad(seq, ((1, 0), (0, 0)), constant_values=-1)
            jt = jnp.concatenate([seq_p[:nw], seq_p[1:]], axis=1)
            it = seq[:, :, None]
            jb = jt[:, None, :]
            mask = (it < jb) | (it > jb + w) | (jb == -1)
            sim = jnp.einsum('bhwie,bhwje->bhwij', bq, bk2) * QK_SCALE
            sim = jnp.where(mask, -jnp.finfo(sim.dtype).max, sim)
            attn = jax.nn.softmax(sim, -1)
            out = jnp.einsum('bhwij,bhwje->bhwie', attn, bv2)
            return out.reshape(b, h, n, d)

        def attn_layer(x, Wqkv, qs, ksc, Wo):
            b, n, _ = x.shape
            qkv = x @ Wqkv
            q, k, v = jnp.split(qkv, 3, -1)
            sh = lambda t: t.reshape(b, n, HEADS, DIM_HEAD).transpose(0, 2, 1, 3)
            q, k, v = (sh(q), sh(k), sh(v))
            q = l2norm(q) * qs
            k = l2norm(k) * ksc
            freqs, scale = rotary_tables(n)
            cos, sin = (jnp.cos(freqs), jnp.sin(freqs))
            q = q * cos * scale + rotate_half(q) * sin * scale
            inv = 1.0 / scale
            k = k * cos * inv + rotate_half(k) * sin * inv
            out = local_attention(q, k, v)
            out = out.transpose(0, 2, 1, 3).reshape(b, n, INNER)
            return out @ Wo

        def ffn_layer(x, g, bln, W1, b1, W2, b2):
            mu = x.mean(-1, keepdims=True)
            var = ((x - mu) ** 2).mean(-1, keepdims=True)
            xn = (x - mu) / jnp.sqrt(var + 1e-05) * g + bln
            hg = xn @ W1 + b1
            a, gate = jnp.split(hg, 2, -1)
            return a * jax.nn.gelu(gate, approximate=False) @ W2 + b2
        for i in range(DEPTH):
            x = attn_layer(shift_tokens(x), Wqkv[i], q_scale[i], k_scale[i], Wo[i]) + x
            x = ffn_layer(shift_tokens(x), ln_g[i], ln_b[i], W1[i], b1[i], W2[i], b2[i]) + x
        return x
    h = _L0_tok_ref(x, mask_BS_i1_0, L0_tok_emb, L0_tok_pca_lookup, L0_tok_proj_w, L0_tok_proj_b, L0_tok_fus_w, L0_tok_fus_b, L0_tok_ln_g, L0_tok_ln_b)
    h = h + _L0_attn_ref(_layernorm(h, axis=-1), L0_attn_wq, L0_attn_aq, L0_attn_bq, L0_attn_wk, L0_attn_ak, L0_attn_bk, L0_attn_wv, L0_attn_av, L0_attn_bv, L0_attn_wo, L0_attn_ao, L0_attn_bo)
    h = h + _L0_ffn_ref(_layernorm(h, axis=-1), L0_ffn_w_gate, L0_ffn_w_up, L0_ffn_w_down)
    h = h + _L1_attn_ref(_layernorm(h, axis=-1), L1_attn_w_qkv, L1_attn_b_qkv, L1_attn_w_out, L1_attn_b_out, L1_attn_ln_gamma, L1_attn_ln_beta)
    h = h + _L1_ffn_ref(_layernorm(h, axis=-1), L1_ffn_Wqkv, L1_ffn_q_scale, L1_ffn_k_scale, L1_ffn_Wo, L1_ffn_ln_g, L1_ffn_ln_b, L1_ffn_W1, L1_ffn_b1, L1_ffn_W2, L1_ffn_b2)
    return h

_drawn_inputs = setup_inputs


def setup_inputs(seed=0):
    import zlib

    import numpy as np

    out = dict(_drawn_inputs(seed))
    spreads = {'L0_tok_proj_b': (0.0, 0.1),
     'L0_tok_fus_b': (0.0, 0.1),
     'L0_tok_ln_g': (1.0, 0.2),
     'L0_tok_ln_b': (0.0, 0.1),
     'L1_attn_b_qkv': (0.0, 0.1),
     'L1_attn_b_out': (0.0, 0.1),
     'L1_attn_ln_gamma': (1.0, 0.2),
     'L1_attn_ln_beta': (0.0, 0.1),
     'L1_ffn_q_scale': (1.0, 0.6),
     'L1_ffn_k_scale': (1.0, 0.6),
     'L1_ffn_ln_g': (1.0, 0.6),
     'L1_ffn_ln_b': (0.0, 0.8),
     'L1_ffn_b1': (0.0, 0.486),
     'L1_ffn_b2': (0.0, 0.1)}
    factors = {'L0_attn_wq': 8.0,
     'L0_attn_aq': 64.0,
     'L0_attn_bq': 64.0,
     'L0_attn_wk': 8.0,
     'L0_attn_ak': 64.0,
     'L0_attn_bk': 64.0,
     'L0_attn_av': 8.0,
     'L0_attn_bv': 8.0,
     'L0_attn_ao': 8.0,
     'L0_attn_bo': 8.0}
    for name, (base, spread) in spreads.items():
        noise = np.random.default_rng([zlib.crc32(name.encode()), seed]).standard_normal(out[name].shape)
        drawn = base * np.exp(spread * noise) if base else spread * noise
        out[name] = jnp.asarray(drawn.astype(out[name].dtype))
    for name, factor in factors.items():
        out[name] = (out[name] * factor).astype(out[name].dtype)
    return out
```

```python
from contextlib import ExitStack

import numpy as np
import concourse.bass as bass
from concourse import mybir

F32 = mybir.dt.float32
I32 = mybir.dt.int32
ALU = mybir.AluOpType
ACT = mybir.ActivationFunctionType
AX = mybir.AxisListType

P = 128
B, S, D = 8, 256, 256
KD = D // P
PAD = S + 1
SLOTS = B + 1
H, HD = 16, 64
INNER = H * HD
HG = 4
NG = H // HG
GW = HG * HD
QT = S // P
DEPTH = 6
WINDOW = 64
V, PCA = 28, 20
FF = 682
FT = -(-FF // P)
QF = 704
QFT = -(-QF // P)
BLK = 16
LOW = -1e30
EPS = 1e-5
L0_HD = 16


def wait(eng, sem, value):
    if isinstance(value, int) and value <= 0:
        return
    eng.wait_ge(sem, value)


class Phase:

    def __init__(self, nc, name):
        self.nc, self.name, self.stack, self.sems = nc, name, ExitStack(), []

    def sb(self, name, shape, dt=F32):
        return self.stack.enter_context(self.nc.sbuf_tensor(f"{self.name}_{name}", shape, dt))

    def psum(self, name, shape, dt=F32):
        return self.stack.enter_context(self.nc.psum_tensor(f"{self.name}_{name}", shape, dt))

    def sem(self, name):
        s = self.stack.enter_context(self.nc.semaphore(f"{self.name}_{name}"))
        self.sems.append(s)
        return s

    def close(self):
        for s in self.sems:
            self.nc.sync.sem_clear(s)
        self.nc.all_engine_barrier()
        self.stack.close()


def tokens(x, k, b, n=1, shift=False):
    v = x[:, k, :].rearrange("p (b t) -> p b t", t=PAD)
    at = 0 if shift and k == 1 else 1
    return v[:, bass.ds(b, n), at:at + S]


def layer_norm(nc, name, src, dst, ones, eps, shift=False, gamma=None, beta=None):
    ph = Phase(nc, name)
    sq = ph.sb("sq", [P, KD, B * S])
    std = ph.sb("std", [P, B * S])
    stats = ph.psum("stats", [P, B, 2, S])
    mean_ready, centred, squared = ph.sem("mean_ready"), ph.sem("centred"), ph.sem("squared")
    var_ready, std_ready, rstd_ready = ph.sem("var_ready"), ph.sem("std_ready"), ph.sem("rstd_ready")
    scaled = ph.sem("scaled")

    def psum_at(b, which):
        return stats[:, bass.ds(b, 1), which, :].rearrange("p a t -> p (a t)")

    with nc.Block() as block:
        @block.tensor
        def _(pe):
            with pe.Fori(0, B) as b:
                for k in range(KD):
                    mm = pe.matmul(psum_at(b, 0), ones[:, :], tokens(src, k, b, 1, shift).rearrange("p a t -> p (a t)"),
                                   start=(k == 0), stop=(k == KD - 1))
                mm.then_inc(mean_ready, 1)
            with pe.Fori(0, B) as b:
                pe.wait_ge(squared, b + 1)
                for k in range(KD):
                    mm = pe.matmul(psum_at(b, 1), ones[:, :], sq[:, k, bass.ds(b * S, S)],
                                   start=(k == 0), stop=(k == KD - 1))
                mm.then_inc(var_ready, 1)

        @block.scalar
        def _(act):
            with act.Fori(0, B) as b:
                act.wait_ge(centred, b + 1)
                for k in range(KD):
                    op = act.activation(sq[:, k, bass.ds(b * S, S)], tokens(dst, k, b).rearrange("p a t -> p (a t)"),
                                        ACT.Square)
                op.then_inc(squared, 1)
            with act.Fori(0, B) as b:
                act.wait_ge(var_ready, b + 1)
                act.activation(std[:, bass.ds(b * S, S)], psum_at(b, 1), ACT.Sqrt, bias=eps[:, :]).then_inc(std_ready, 1)
            if gamma is not None:
                with act.Fori(0, B) as b:
                    act.wait_ge(scaled, b + 1)
                    for k in range(KD):
                        view = tokens(dst, k, b).rearrange("p a t -> p (a t)")
                        act.activation(view, view, ACT.Identity, bias=beta[:, k:k + 1], scale=gamma[:, k:k + 1])

        @block.vector
        def _(dve):
            with dve.Fori(0, B) as b:
                dve.wait_ge(mean_ready, b + 1)
                for k in range(KD):
                    op = dve.tensor_tensor(tokens(dst, k, b).rearrange("p a t -> p (a t)"),
                                           tokens(src, k, b, 1, shift).rearrange("p a t -> p (a t)"),
                                           psum_at(b, 0), ALU.subtract)
                op.then_inc(centred, 1)
            with dve.Fori(0, B) as b:
                dve.wait_ge(std_ready, b + 1)
                s = std[:, bass.ds(b * S, S)]
                dve.reciprocal(s, s).then_inc(rstd_ready, 1)
                dve.wait_ge(rstd_ready, b + 1)
                for k in range(KD):
                    view = tokens(dst, k, b).rearrange("p a t -> p (a t)")
                    op = dve.tensor_tensor(view, view, s, ALU.mult)
                op.then_inc(scaled, 1)
    ph.close()


def attention(nc, name, kind, src, res, w_in, w_out, ident, mask, scale, keys, bias_in, bias_out,
              cos, sin, expo, loads):
    ph = Phase(nc, name)
    rope = kind == "rope"
    xs = ph.sb("xs", [P, KD, S])
    qk = ph.sb("qk", [P, QT, 2 * GW])
    qk_rot = ph.sb("qk_rot", [P, QT, 2 * GW]) if rope else None
    sq = ph.sb("sq", [P, QT, 2 * GW]) if rope else None
    ssq = ph.sb("ssq", [P, QT, 2 * HG]) if rope else None
    q_t = ph.sb("q_t", [P, 2, 2, S])
    k_t = ph.sb("k_t", [P, 2, 2, S])
    v_sb = ph.sb("v_sb", [P, 2, QT, GW])
    probs = ph.sb("probs", [P, 4, QT, S])
    probs_t = ph.sb("probs_t", [P, 2, QT, S])
    row_max = ph.sb("row_max", [P, 4, QT])
    neg_max = ph.sb("neg_max", [P, 4, QT])
    row_sum = ph.sb("row_sum", [P, 2, QT * HG])
    inv_sum = ph.sb("inv_sum", [P, QT * HG])
    out = ph.sb("out", [P, QT, GW])
    out_t = ph.sb("out_t", [P, 2, S])

    proj_ps = ph.psum("proj_ps", [P, 2, 512])
    score_ps = ph.psum("score_ps", [P, 2, QT, S])
    probs_t_ps = ph.psum("probs_t_ps", [P, QT, S])
    turn_ps = ph.psum("turn_ps", [P, 2, S])
    val_ps = ph.psum("val_ps", [P, QT, HG, HD])
    out_ps = ph.psum("out_ps", [P, KD, S])

    xs_ready, proj_full, proj_free = ph.sem("xs_ready"), ph.sem("proj_full"), ph.sem("proj_free")
    sq_done, ssq_done, qk_ready, pool_step = ph.sem("sq_done"), ph.sem("ssq_done"), ph.sem("qk_ready"), ph.sem("pool_step")
    turn_full, turn_free = ph.sem("turn_full"), ph.sem("turn_free")
    score_full, score_free, max_ready = ph.sem("score_full"), ph.sem("score_free"), ph.sem("max_ready")
    exp_done, pt_full, pt_ready = ph.sem("exp_done"), ph.sem("pt_full"), ph.sem("pt_ready")
    val_done, inv_ready, out_ready = ph.sem("val_done"), ph.sem("inv_ready"), ph.sem("out_ready")
    dve_hold, pool_hold = ph.sem("dve_hold"), ph.sem("pool_hold")
    wo_done, res_done, loaded, cleared = ph.sem("wo_done"), ph.sem("res_done"), ph.sem("loaded"), ph.sem("cleared")

    def q_fill(G):
        return 0 if isinstance(G, int) and G == 0 else 3 * G - 1

    def k_fill(G):
        return 1 if isinstance(G, int) and G == 0 else 3 * G

    def out_fill(G):
        return 3 * G + 4

    def back(N, forward):
        return not isinstance(N, int) or (N >= 0 and (forward or N < HG * NG * B))

    def blocks():
        return [(kt, qt) for qt in range(QT) for kt in range(QT)
                if keys[qt][0] < (kt + 1) * P and keys[qt][1] > kt * P]

    with nc.Block() as block:
        @block.tensor
        def _(pe):
            def project(G, g, part, batch):
                f = 3 * G + part
                bank = proj_ps[:, (3 * g + part) % 2, :]
                wait(pe, proj_free, f - 1)
                if g == 0 and part == 0:
                    wait(pe, xs_ready, batch + 1)
                if part < 2:
                    for k in range(KD):
                        w = w_in[:, k, 0:2 * INNER].rearrange("p (s n) -> p s n", s=2)[:, :, g * GW:(g + 1) * GW]
                        mm = pe.matmul(bank, xs[:, k, part * P:(part + 1) * P], w, start=(k == 0), stop=(k == KD - 1))
                else:
                    for t in range(QT):
                        for k in range(KD):
                            mm = pe.matmul(bank[:, t * GW:(t + 1) * GW], xs[:, k, t * P:(t + 1) * P],
                                           w_in[:, k, 2 * INNER + g * GW:2 * INNER + (g + 1) * GW],
                                           start=(k == 0), stop=(k == KD - 1))
                mm.then_inc(proj_full, 1)

            def turn(src_tiles, fill):
                wait(pe, turn_free, fill)
                for i, j, tile in src_tiles:
                    mm = pe.transpose(turn_ps[:, i, j * P:(j + 1) * P], tile, ident[:, :])
                mm.then_inc(turn_full, 1)

            def turn_qk(G, which):
                if rope:
                    wait(pe, qk_ready, 2 * G + 2)
                else:
                    wait(pe, proj_free, 3 * G + 2)
                turn([(i, t, qk[:, t, which * GW + i * P:which * GW + (i + 1) * P]) for i in range(2) for t in range(QT)],
                     (q_fill, k_fill)[which](G))

            def scores(N, G, g, j):
                if j == 0:
                    wait(pe, turn_free, k_fill(G) + 1)
                wait(pe, score_free, N - 1)
                r = slice((j % 2) * HD, (j % 2 + 1) * HD)
                for qt in range(QT):
                    a, z = keys[qt]
                    mm = pe.matmul(score_ps[:, j % 2, qt, a:z], q_t[r, g % 2, j // 2, qt * P:(qt + 1) * P],
                                   k_t[r, g % 2, j // 2, a:z], start=True, stop=True)
                mm.then_inc(score_full, 1)

            def turn_probs(N, j):
                wait(pe, exp_done, N + 1)
                wait(pe, pt_ready, N)
                for kt, qt in blocks():
                    mm = pe.transpose(probs_t_ps[:, kt, qt * P:(qt + 1) * P], probs[:, j, qt, kt * P:(kt + 1) * P], ident[:, :])
                mm.then_inc(pt_full, 1)

            def values(N, G, g, j):
                wait(pe, pt_ready, N + 1)
                if j == 0:
                    wait(pe, proj_free, 3 * G + 3)
                    wait(pe, out_ready, G)
                for qt in range(QT):
                    kts = [kt for kt, q in blocks() if q == qt]
                    for kt in kts:
                        mm = pe.matmul(val_ps[:, qt, j, :], probs_t[:, j % 2, kt, qt * P:(qt + 1) * P],
                                       v_sb[:, g % 2, kt, j * HD:(j + 1) * HD], start=(kt == kts[0]), stop=(kt == kts[-1]))
                mm.then_inc(val_done, 1)

            def turn_out(G):
                wait(pe, out_ready, G + 1)
                turn([(i, t, out[:, t, i * P:(i + 1) * P]) for i in range(2) for t in range(QT)], out_fill(G))

            def project_out(G, b, g):
                wait(pe, turn_free, out_fill(G) + 1)
                if g == 0:
                    wait(pe, res_done, b)
                for k in range(2):
                    for m in range(KD):
                        mm = pe.matmul(out_ps[:, m, :], w_out[:, 2 * g + k, m * P:(m + 1) * P], out_t[:, k, :],
                                       start=(g == 0 and k == 0 and m == 0), stop=(g == NG - 1 and k == 1),
                                       skip_group_check=True)
                mm.then_inc(wo_done, 1)

            def body(b, forward=True):
                for g in range(NG):
                    G = NG * b + g
                    gn, gp = (g + 1) % NG, (g - 1) % NG
                    for j in range(HG):
                        N = HG * G + j
                        if forward and j == 3:
                            turn_qk(G + 1, 0)
                        elif forward:
                            scores(N + 1, G, g, j + 1)
                        if back(N - 1, forward):
                            turn_probs(N - 1, (j - 1) % HG)
                        if j == 3 and back(HG * (G - 1), forward):
                            project_out(G - 1, b if g else b - 1, gp)
                        if j == 3 and forward:
                            turn_qk(G + 1, 1)
                        if back(N - 2, forward):
                            values(N - 2, G if j >= 2 else G - 1, g if j >= 2 else gp, (j - 2) % HG)
                        if j == 2 and back(HG * (G - 1), forward):
                            turn_out(G - 1)
                        if j == 3 and forward:
                            scores(N + 1, G + 1, gn, 0)
                        if forward and j == 0:
                            project(G + 1, gn, 0, b + (gn == 0))
                            project(G + 1, gn, 1, b + (gn == 0))
                        if forward and j == 1:
                            project(G + 1, gn, 2, b + (gn == 0))
                    if not forward:
                        break

            for part in range(3):
                project(0, 0, part, 0)
            turn_qk(0, 0)
            turn_qk(0, 1)
            scores(0, 0, 0, 0)
            body(0)
            with pe.Fori(1, B) as b:
                body(b)
            body(B, forward=False)

        @block.scalar
        def _(act):
            def square(G, g, t):
                wait(act, proj_full, 3 * G + t + 1)
                wait(act, ssq_done, 2 * (G - 1) + t + 1)
                act.activation(sq[:, t, :], proj_ps[:, (3 * g + t) % 2, :], ACT.Square).then_inc(sq_done, 1)

            def keep_qk(G, g, which):
                wait(act, turn_full, (q_fill, k_fill)[which](G) + 1)
                wait(act, score_full, HG * (G - 1))
                dst = (q_t, k_t)[which][:, g % 2, :, :]
                act.activation(dst, turn_ps[:, :, :], ACT.Copy).then_inc(turn_free, 1)

            def exps(N, G, g, j):
                wait(act, max_ready, N + 1)
                if j == 0:
                    wait(act, out_ready, G - 1)
                for qt in range(QT):
                    a, z = keys[qt]
                    op = act.activation(probs[:, j, qt, a:z], probs[:, j, qt, a:z], ACT.Exp, bias=neg_max[:, j, qt:qt + 1],
                                        scale=scale, accum_out=row_sum[:, g % 2, qt * HG + j:qt * HG + j + 1])
                op.then_inc(exp_done, 1)

            def keep_probs_t(N, j):
                wait(act, pt_full, N + 1)
                wait(act, val_done, N - 1)
                if len(blocks()) == QT * QT:
                    op = act.activation(probs_t[:, j % 2, :, :], probs_t_ps[:, :, :], ACT.Copy)
                else:
                    act.activation(probs_t[:, j % 2, 0, :], probs_t_ps[:, 0, :], ACT.Copy)
                    op = act.activation(probs_t[:, j % 2, 1, P:S], probs_t_ps[:, 1, P:S], ACT.Copy)
                op.then_inc(pt_ready, 1)

            def keep_out_t(G):
                wait(act, turn_full, out_fill(G) + 1)
                wait(act, wo_done, G)
                act.activation(out_t[:, :, :], turn_ps[:, :, :], ACT.Copy).then_inc(turn_free, 1)

            def body(b, forward=True):
                for g in range(NG):
                    G = NG * b + g
                    gn = (g + 1) % NG
                    for j in range(HG):
                        N = HG * G + j
                        if forward and j == 3:
                            keep_qk(G + 1, gn, 0)
                        if back(N - 1, forward):
                            keep_probs_t(N - 1, (j - 1) % HG)
                        if forward and j == 3:
                            keep_qk(G + 1, gn, 1)
                        if j == 2 and back(HG * (G - 1), forward):
                            if forward:
                                exps(N + 1, G, g, j + 1)
                            keep_out_t(G - 1)
                        elif forward:
                            exps(N + 1, G if j < 3 else G + 1, g if j < 3 else gn, (j + 1) % HG)
                        if forward and rope and j == 0:
                            square(G + 1, gn, 0)
                            square(G + 1, gn, 1)
                    if not forward:
                        break

            if rope:
                square(0, 0, 0)
                square(0, 0, 1)
            keep_qk(0, 0, 0)
            keep_qk(0, 0, 1)
            exps(0, 0, 0, 0)
            body(0)
            with act.Fori(1, B) as b:
                body(b)
            body(B, forward=False)

        @block.vector
        def _(dve):
            def maxima(N, j):
                wait(dve, score_full, N + 1)
                wait(dve, pt_full, N - 3)
                dve.sem_inc(dve_hold, 1)
                for qt in range(QT):
                    a, z = keys[qt]
                    op = dve.tensor_tensor_reduce(probs[:, j, qt, a:z], score_ps[:, j % 2, qt, a:z], mask[:, qt, a:z],
                                                  1.0, -3e38, ALU.add, ALU.max, row_max[:, j, qt:qt + 1])
                op.then_inc(score_free, 1)
                wait(dve, score_free, N + 1)
                dve.tensor_scalar(neg_max[:, j, :], row_max[:, j, :], -scale, None, ALU.mult).then_inc(max_ready, 1)

            def turn_heads(G, g, t):
                bank = proj_ps[:, (3 * g + t) % 2, :]
                if not rope:
                    wait(dve, proj_full, 3 * G + t + 1)
                    wait(dve, turn_full, k_fill(G - 1) + 1)
                    w = bias_in[:, 0:2 * INNER].rearrange("p (s n) -> p s n", s=2)[:, :, g * GW:(g + 1) * GW]
                    dve.tensor_tensor(qk[:, t, :].rearrange("p (s n) -> p s n", s=2), bank.rearrange("p (s n) -> p s n", s=2),
                                      w, ALU.add).then_inc(proj_free, 1)
                    return
                wait(dve, sq_done, 2 * G + t + 1)
                wait(dve, qk_ready, 2 * (G - 1) + t + 1)
                dve.tensor_reduce(ssq[:, t, :], sq[:, t, :].rearrange("p (h d) -> p h d", d=HD), AX.X, ALU.add).then_inc(ssq_done, 1)
                if not (isinstance(G, int) and G == 0):
                    wait(dve, turn_full, k_fill(G - 1) + 1)
                view = lambda x: x.rearrange("p (s h d) -> p s h d", s=2, h=HG)
                table = lambda x, lo, hi: x[:, t, :, lo:hi].unsqueeze(2).broadcast_to([P, 2, HG, hi - lo])
                dve.tensor_tensor(view(qk[:, t, :]), view(bank), table(cos, 0, HD), ALU.mult)
                half = HD // 2
                for lo in (0, half):
                    other = half - lo
                    op = dve.tensor_tensor(view(qk_rot[:, t, :])[:, :, :, lo:lo + half], view(bank)[:, :, :, other:other + half],
                                           table(sin, lo, lo + half), ALU.mult)
                op.then_inc(proj_free, 1)

            def keep_v(G, g):
                wait(dve, proj_full, 3 * G + 3)
                wait(dve, val_done, HG * (G - 1))
                dst = v_sb[:, g % 2, :, :]
                bank = proj_ps[:, (3 * g + 2) % 2, :].rearrange("p (t n) -> p t n", t=QT)
                if rope:
                    op = dve.tensor_copy(dst, bank)
                else:
                    w = bias_in[:, 2 * INNER + g * GW:2 * INNER + (g + 1) * GW].unsqueeze(1).broadcast_to([P, QT, GW])
                    op = dve.tensor_tensor(dst, bank, w, ALU.add)
                op.then_inc(proj_free, 1)

            def norm(G, g):
                wait(dve, val_done, HG * G + HG)
                dve.reciprocal(inv_sum[:, :], row_sum[:, g % 2, :]).then_inc(inv_ready, 1)
                wait(dve, turn_full, out_fill(G - 1) + 1 if not isinstance(G, int) or G else 0)
                dve.wait_ge(inv_ready, G + 1)
                dve.tensor_tensor(out[:, :, :].rearrange("p t (h d) -> p (t h) d", d=HD),
                                  val_ps[:, :, :, :].rearrange("p t h d -> p (t h) d"),
                                  inv_sum[:, :].unsqueeze(2).broadcast_to([P, QT * HG, HD]), ALU.mult).then_inc(out_ready, 1)

            def residual(b):
                wait(dve, wo_done, NG * b + NG)
                for m in range(KD):
                    r = tokens(res, m, b).rearrange("p a t -> p (a t)")
                    op = dve.scalar_tensor_tensor(r, out_ps[:, m, :], bias_out[:, m:m + 1], r, ALU.add, ALU.add)
                op.then_inc(res_done, 1)

            def body(b, forward=True):
                for g in range(NG):
                    G = NG * b + g
                    gn, gp = (g + 1) % NG, (g - 1) % NG
                    for j in range(HG):
                        N = HG * G + j
                        if j == 3 and g == 0 and back(HG * (G - 1), forward):
                            residual(b - 1)
                        if forward:
                            maxima(N + 1, (j + 1) % HG)
                            if j == 0:
                                turn_heads(G + 1, gn, 0)
                                turn_heads(G + 1, gn, 1)
                        if j == 1 and back(HG * (G - 1), forward):
                            norm(G - 1, gp)
                        if forward and j == 1:
                            keep_v(G + 1, gn)
                    if not forward:
                        break

            op = dve.memset(probs[:, :, :, :], 0.0)
            op.then_inc(cleared, 1)
            turn_heads(0, 0, 0)
            turn_heads(0, 0, 1)
            keep_v(0, 0)
            wait(dve, cleared, 1)
            maxima(0, 0)
            body(0)
            with dve.Fori(1, B) as b:
                body(b)
            body(B, forward=False)

        @block.gpsimd
        def _(pool):
            def stage(b):
                wait(pool, proj_full, 3 * NG * b)
                for k in range(KD):
                    op = pool.tensor_copy(xs[:, k, :], tokens(src, k, b, 1, rope).rearrange("p a t -> p (a t)"))
                op.then_inc(xs_ready, 1)

            def scale_heads(G, t):
                step = 3 * (2 * G + t)
                wait(pool, ssq_done, 2 * G + t + 1)
                pool.sem_inc(pool_hold, 1)
                pool.tensor_scalar(ssq[:, t, :], ssq[:, t, :], 1e-24, None, ALU.max).then_inc(pool_step, 1)
                pool.wait_ge(pool_step, step + 1)
                pool.tensor_tensor(ssq[:, t, :], ssq[:, t, :], expo[:, :], ALU.pow).then_inc(pool_step, 1)
                wait(pool, proj_free, 3 * G + t + 1)
                pool.tensor_tensor(qk[:, t, :], qk[:, t, :], qk_rot[:, t, :], ALU.add).then_inc(pool_step, 1)
                pool.wait_ge(pool_step, step + 3)
                view = qk[:, t, :].rearrange("p (h d) -> p h d", d=HD)
                pool.tensor_tensor(view, view, ssq[:, t, :].unsqueeze(2).broadcast_to([P, 2 * HG, HD]), ALU.mult)\
                    .then_inc(qk_ready, 1)

            def body(b):
                for g in range(NG):
                    G = NG * b + g
                    if rope:
                        scale_heads(G + 1, 0)
                        scale_heads(G + 1, 1)
                    if g == NG - 2:
                        stage(b + 1)

            stage(0)
            if rope:
                scale_heads(0, 0)
                scale_heads(0, 1)
            body(0)
            with pool.Fori(1, B) as b:
                body(b)

        @block.sync
        def _(sp):
            for n, (dst, source) in enumerate(loads):
                sp.dma_start(dst, source).then_inc(loaded, 16)
            wait(sp, loaded, 16 * len(loads))
    ph.close()


def feed_forward(nc, name, src, res, w1, b1, w2, b2, loads):
    ph = Phase(nc, name)
    CH = 2 * S
    gate = ph.sb("gate", [P, 2, CH])
    hid = ph.sb("hid", [P, FT, CH])
    up_ps = ph.psum("up_ps", [P, 2, 2, CH])
    down_ps = ph.psum("down_ps", [P, 2, KD, CH])
    up_full, gate_ready, hid_ready = ph.sem("up_full"), ph.sem("gate_ready"), ph.sem("hid_ready")
    down_full, res_done, loaded = ph.sem("down_full"), ph.sem("res_done"), ph.sem("loaded")
    width = [min(P, FF - m * P) for m in range(FT)]

    with nc.Block() as block:
        @block.tensor
        def _(pe):
            def up(c, m):
                wait(pe, hid_ready, FT * c + m - 1)
                for part in (0, 1):
                    for k in range(KD):
                        mm = pe.matmul(up_ps[0:width[m], m % 2, part, :].rearrange("p (b t) -> p b t", t=S),
                                       w1[:, k, part * FF + m * P:part * FF + m * P + width[m]],
                                       tokens(src, k, 2 * c, 2), start=(k == 0), stop=(k == KD - 1))
                mm.then_inc(up_full, 1)

            def down(c, parity, m):
                wait(pe, hid_ready, FT * c + m + 1)
                if m == 0:
                    wait(pe, res_done, c - 1)
                for n in range(KD):
                    mm = pe.matmul(down_ps[:, parity, n, :], w2[0:width[m], m, n * P:(n + 1) * P], hid[0:width[m], m, :],
                                   start=(m == 0), stop=(m == FT - 1))
                if m == FT - 1:
                    mm.then_inc(down_full, 1)

            def body(c, parity):
                for m in range(FT + 2):
                    if m < FT:
                        up(c, m)
                    if m >= 2:
                        down(c, parity, m - 2)

            body(0, 0)
            body(1, 1)
            with pe.Fori(1, B // 4) as c:
                body(2 * c, 0)
                body(2 * c + 1, 1)

        @block.scalar
        def _(act):
            def body(c):
                for m in range(FT):
                    wait(act, up_full, FT * c + m + 1)
                    wait(act, hid_ready, FT * c + m - 1)
                    act.activation(gate[0:width[m], m % 2, :], up_ps[0:width[m], m % 2, 1, :], ACT.Gelu,
                                   bias=b1[0:width[m], FT + m:FT + m + 1]).then_inc(gate_ready, 1)
            body(0)
            with act.Fori(1, B // 2) as c:
                body(c)

        @block.vector
        def _(dve):
            def add(c, parity):
                wait(dve, down_full, c + 1)
                for n in range(KD):
                    r = tokens(res, n, 2 * c, 2)
                    op = dve.scalar_tensor_tensor(r, down_ps[:, parity, n, :].rearrange("p (b t) -> p b t", t=S),
                                                  b2[:, n:n + 1], r, ALU.add, ALU.add)
                op.then_inc(res_done, 1)

            def body(c, parity):
                for m in range(FT):
                    wait(dve, gate_ready, FT * c + m + 1)
                    if m == 0:
                        wait(dve, down_full, c)
                    w = width[m]
                    dve.scalar_tensor_tensor(hid[0:w, m, :], up_ps[0:w, m % 2, 0, :], b1[0:w, m:m + 1],
                                             gate[0:w, m % 2, :], ALU.add, ALU.mult).then_inc(hid_ready, 1)
                add(c, parity)

            body(0, 0)
            body(1, 1)
            with dve.Fori(1, B // 4) as c:
                body(2 * c, 0)
                body(2 * c + 1, 1)

        @block.sync
        def _(sp):
            for dst, source in loads:
                sp.dma_start(dst, source).then_inc(loaded, 16)
            wait(sp, loaded, 16 * len(loads))
    ph.close()


def token_features(nc, consts, dram, emb, pca, proj, proj_b, fus, fus_b, dst, loads):
    ph = Phase(nc, "tok")
    CH = 2 * S
    ids = ph.sb("ids", [V, B * S], I32)
    one_hot = ph.sb("one_hot", [V, B * S])
    mask_i = ph.sb("mask_i", [PCA, B * S], I32)
    mask = ph.sb("mask", [PCA, B, S + 2])
    length = ph.sb("length", [PCA, B, S])
    masked = ph.sb("masked", [PCA, B, S + 2])
    window = ph.sb("window", [PCA, B, S])
    comb = ph.sb("comb", [P, 2 * KD, CH])
    look_ps = ph.psum("look_ps", [P, KD + 1, CH])
    proj_ps = ph.psum("proj_ps", [P, KD, CH])
    fus_ps = ph.psum("fus_ps", [P, KD, CH])
    got_ids, loaded, zeroed, step = ph.sem("got_ids"), ph.sem("loaded"), ph.sem("zeroed"), ph.sem("step")
    looked, kept, windowed, projected = ph.sem("looked"), ph.sem("kept"), ph.sem("windowed"), ph.sem("projected")
    biased, fused, stored, added = ph.sem("biased"), ph.sem("fused"), ph.sem("stored"), ph.sem("added")
    chunk = lambda x, c: x[:, bass.ds(c * CH, CH)]

    with nc.Block() as block:
        @block.sync
        def _(sp):
            sp.dma_start(ids[:, :], dram["x"].unsqueeze(0).broadcast_to([V, B * S])).then_inc(got_ids, 16)
            sp.dma_start(mask_i[:, :], dram["mask"].unsqueeze(0).broadcast_to([PCA, B * S])).then_inc(got_ids, 16)
            for d, source in loads:
                sp.dma_start(d, source).then_inc(loaded, 16)
            wait(sp, loaded, 16 * len(loads))

        @block.vector
        def _(dve):
            dve.memset(mask[:, :, :], 0.0).then_inc(zeroed, 1)
            dve.memset(masked[:, :, :], 0.0).then_inc(zeroed, 1)
            dve.wait_ge(got_ids, 32)
            dve.wait_ge(zeroed, 2)
            dve.tensor_scalar(one_hot[:, :], ids[:, :], consts["iota"][0:V, :], None, ALU.is_equal).then_inc(step, 1)
            dve.tensor_copy(mask[:, :, 1:S + 1], mask_i[:, :].rearrange("p (b t) -> p b t", t=S)).then_inc(step, 1)
            dve.wait_ge(step, 2)
            dve.tensor_tensor(length[:, :, :], mask[:, :, 0:S], mask[:, :, 1:S + 1], ALU.add).then_inc(step, 1)
            dve.wait_ge(step, 3)
            dve.tensor_tensor(length[:, :, :], length[:, :, :], mask[:, :, 2:S + 2], ALU.add).then_inc(step, 1)
            dve.wait_ge(step, 4)
            dve.tensor_scalar(length[:, :, :], length[:, :, :], 1.0, None, ALU.max).then_inc(step, 1)
            dve.wait_ge(step, 5)
            dve.reciprocal(length[:, :, :], length[:, :, :]).then_inc(step, 1)
            dve.wait_ge(step, 6)
            with dve.Fori(0, B // 2) as c:
                two = lambda x, lo=0: x[:, bass.ds(c * 2, 2), lo:lo + S]
                dve.wait_ge(looked, c + 1)
                dve.tensor_tensor(two(masked, 1), look_ps[0:PCA, KD, :].rearrange("p (b t) -> p b t", t=S), two(mask, 1),
                                  ALU.mult).then_inc(added, 1)
                dve.wait_ge(added, 4 * c + 1)
                dve.tensor_tensor(two(window), two(masked, 0), two(masked, 1), ALU.add).then_inc(added, 1)
                dve.wait_ge(added, 4 * c + 2)
                dve.tensor_tensor(two(window), two(window), two(masked, 2), ALU.add).then_inc(added, 1)
                dve.wait_ge(added, 4 * c + 3)
                dve.tensor_tensor(two(window), two(window), two(length), ALU.mult).then_inc(added, 1)
                dve.wait_ge(added, 4 * c + 4)
                dve.sem_inc(windowed, 1)
                dve.wait_ge(fused, c + 1)
                for m in range(KD):
                    op = dve.tensor_scalar(tokens(dst, m, c * 2, 2), fus_ps[:, m, :].rearrange("p (b t) -> p b t", t=S),
                                           fus_b[:, m:m + 1], None, ALU.add)
                op.then_inc(stored, 1)

        @block.scalar
        def _(act):
            with act.Fori(0, B // 2) as c:
                act.wait_ge(looked, c + 1)
                act.activation(comb[:, 0:KD, :], look_ps[:, 0:KD, :], ACT.Copy).then_inc(kept, 1)
                act.wait_ge(projected, c + 1)
                for m in range(KD):
                    op = act.activation(comb[:, KD + m, :], proj_ps[:, m, :], ACT.Identity, bias=proj_b[:, m:m + 1])
                op.then_inc(biased, 1)

        @block.tensor
        def _(pe):
            def chunk_of(c):
                wait(pe, windowed, c)
                for m in range(KD):
                    pe.matmul(look_ps[:, m, :], emb[:, m * P:(m + 1) * P], chunk(one_hot, c), start=True, stop=True)
                pe.matmul(look_ps[:, KD, :], pca[:, :], chunk(one_hot, c), start=True, stop=True).then_inc(looked, 1)
                pe.wait_ge(windowed, c + 1)
                for m in range(KD):
                    mm = pe.matmul(proj_ps[:, m, :], proj[:, m * P:(m + 1) * P],
                                   window[:, bass.ds(c * 2, 2), :].rearrange("p b t -> p (b t)"), start=True, stop=True)
                mm.then_inc(projected, 1)
                pe.wait_ge(biased, c + 1)
                wait(pe, stored, c)
                for m in range(KD):
                    for k in range(2 * KD):
                        mm = pe.matmul(fus_ps[:, m, :], fus[:, k, m * P:(m + 1) * P], comb[:, k, :],
                                       start=(k == 0), stop=(k == 2 * KD - 1))
                mm.then_inc(fused, 1)

            pe.wait_ge(step, 1)
            chunk_of(0)
            with pe.Fori(1, B // 2) as c:
                chunk_of(c)
    ph.close()


def merge_lora(nc, w_in, w_out, a_in, b_in, a_out, b_out):
    ph = Phase(nc, "lora")
    RANK = 16
    ps = ph.psum("ps", [P, 8, 512])
    full, done = ph.sem("full"), ph.sem("done")
    NC = 3 * INNER // 512
    pieces = [(w_in[:, k, n * 512:(n + 1) * 512], a_in[:, n // 2, k * P:(k + 1) * P], b_in[:, n * 512:(n + 1) * 512])
              for k in range(KD) for n in range(NC)]
    pieces += [(w_out[:, k, :], a_out[:, k * P:(k + 1) * P], b_out[:, :]) for k in range(INNER // P)]

    with nc.Block() as block:
        @block.tensor
        def _(pe):
            for n, (w, a, b) in enumerate(pieces):
                wait(pe, done, n - 7)
                pe.matmul(ps[:, n % 8, 0:w.shape[1]], a, b, start=True, stop=True).then_inc(full, 1)

        @block.vector
        def _(dve):
            for n, (w, a, b) in enumerate(pieces):
                dve.wait_ge(full, n + 1)
                dve.scalar_tensor_tensor(w, ps[:, n % 8, 0:w.shape[1]], 1.0 / RANK, w, ALU.mult, ALU.add).then_inc(done, 1)
    ph.close()


class Quantiser:

    STEPS = 14

    def __init__(self, ph, rows, n):
        self.step = ph.sem("quant_step")
        self.mag = ph.sb("mag", [P, rows, n])
        self.sign = ph.sb("sign", [P, rows, n])
        self.level = ph.sb("level", [P, rows, n])
        self.scale = ph.sb("scale", [P, rows * n // BLK])
        self.inverse = ph.sb("inverse", [P, rows * n // BLK])

    def __call__(self, dve, out, mag, sign, level, before):
        n = mag.shape[1]
        sc, inv = self.scale[:, 0:n // BLK], self.inverse[:, 0:n // BLK]
        blocks = lambda x: x.rearrange("p (b e) -> p b e", e=BLK)
        spread = lambda x: x.unsqueeze(2).broadcast_to([P, n // BLK, BLK])
        made = 0

        def then(op):
            nonlocal made
            made += 1
            op.then_inc(self.step, 1)
            dve.wait_ge(self.step, before + made)

        then(dve.tensor_reduce(sc, blocks(mag), AX.X, ALU.max))
        then(dve.tensor_scalar(sc, sc, 1.0 / 6.0, 1e-12, ALU.mult, ALU.max))
        then(dve.reciprocal(inv, sc))
        then(dve.tensor_tensor(blocks(mag), blocks(mag), spread(inv), ALU.mult))
        then(dve.tensor_scalar(level, mag, 5.0, 2.0, ALU.is_gt, ALU.mult))
        then(dve.scalar_tensor_tensor(level, mag, 3.5, level, ALU.is_gt, ALU.add))
        then(dve.scalar_tensor_tensor(level, mag, 2.5, level, ALU.is_gt, ALU.add))
        then(dve.tensor_scalar(level, level, 2.0, None, ALU.mult))
        for threshold in (1.75, 1.25, 0.75, 0.25):
            then(dve.scalar_tensor_tensor(level, mag, threshold, level, ALU.is_gt, ALU.add))
        then(dve.scalar_tensor_tensor(level, level, 0.5, sign, ALU.mult, ALU.mult))
        then(dve.tensor_tensor(blocks(out), blocks(level), spread(sc), ALU.mult))
        assert made == self.STEPS


def quantise_weights(nc, gate_t, up_t, down_t, dram, ident, loads):
    ph = Phase(nc, "qw")
    raw = ph.sb("raw", [P, 3, 6 * D])
    q = Quantiser(ph, 1, 6 * D)
    turn_ps = ph.psum("turn_ps", [P, 2, 512])
    got, abs_ready, sign_ready, ready = ph.sem("got"), ph.sem("abs_ready"), ph.sem("sign_ready"), ph.sem("ready")
    turned, kept, loaded, zeroed = ph.sem("turned"), ph.sem("kept"), ph.sem("loaded"), ph.sem("zeroed")
    full = QF // P
    rest = QF - full * P
    n_of = (6 * D, 6 * D, KD * QF)

    def turns(i):
        if i < 2:
            dst = (gate_t, up_t)[i]
            for t in range(QFT):
                w = P if t < full else rest
                for k in range(KD):
                    yield dst[:, k, t * P:t * P + w], raw[0:w, i, t * D + k * P:t * D + (k + 1) * P], w
        else:
            for m in range(KD):
                for t in range(QFT):
                    w = P if t < full else rest
                    yield down_t[0:w, t, m * P:(m + 1) * P], raw[:, 2, m * QF + t * P:m * QF + t * P + w], w

    with nc.Block() as block:
        @block.sync
        def _(sp):
            sp.wait_ge(zeroed, 1)
            for i, name in enumerate(("w_gate", "w_up")):
                sp.dma_start(raw[:, i, 0:full * D].rearrange("p (t d) -> p t d", d=D),
                             dram[name][0:full * P, :].rearrange("(t p) d -> p t d", p=P)).then_inc(got, 16)
                sp.dma_start(raw[0:rest, i, full * D:QFT * D], dram[name][full * P:QF, :]).then_inc(got, 16)
            sp.dma_start(raw[:, 2, 0:KD * QF].rearrange("p (m n) -> p m n", n=QF),
                         dram["w_down"].rearrange("(m p) n -> p m n", p=P)).then_inc(got, 16)
            for d, source in loads:
                sp.dma_start(d, source).then_inc(loaded, 16)
            wait(sp, loaded, 16 * len(loads))

        @block.scalar
        def _(act):
            act.wait_ge(got, 5 * 16)
            for i in range(3):
                n = n_of[i]
                wait(act, ready, i)
                act.activation(q.mag[:, 0, 0:n], raw[:, i, 0:n], ACT.Abs).then_inc(abs_ready, 1)
                act.activation(q.sign[:, 0, 0:n], raw[:, i, 0:n], ACT.Sign).then_inc(sign_ready, 1)

        @block.vector
        def _(dve):
            dve.memset(raw[:, 0:2, full * D:QFT * D], 0.0).then_inc(zeroed, 1)
            for i in range(3):
                n = n_of[i]
                dve.wait_ge(abs_ready, i + 1)
                dve.wait_ge(sign_ready, i + 1)
                q(dve, raw[:, i, 0:n], q.mag[:, 0, 0:n], q.sign[:, 0, 0:n], q.level[:, 0, 0:n], q.STEPS * i)
                dve.sem_inc(ready, 1)
                f = sum(len(list(turns(a))) for a in range(i))
                for n_, (dst, tile, w) in enumerate(turns(i)):
                    dve.wait_ge(turned, f + n_ + 1)
                    dve.tensor_copy(dst, turn_ps[0:dst.shape[0], (f + n_) % 2, 0:dst.shape[1]]).then_inc(kept, 1)

        @block.tensor
        def _(pe):
            f = 0
            for i in range(3):
                pe.wait_ge(ready, i + 1)
                for dst, tile, w in turns(i):
                    wait(pe, kept, f - 1)
                    rows = tile.shape[0]
                    pe.transpose(turn_ps[0:tile.shape[1], f % 2, 0:rows], tile, ident[0:rows, 0:rows]).then_inc(turned, 1)
                    f += 1
    ph.close()


def quantised_feed_forward(nc, src, res, gate_t, up_t, down_t, ident, loads):
    ph = Phase(nc, "qff")
    HF = QF // 2
    xs = ph.sb("xs", [P, 2, KD, P])
    qx = Quantiser(ph, 1, QF)
    xq = ph.sb("xq", [P, D])
    xq_t = ph.sb("xq_t", [P, KD, P])
    silu = ph.sb("silu", [P, 2, HF])
    hid = ph.sb("hid", [P, QF])
    hq = ph.sb("hq", [P, QF])
    hq_t = ph.sb("hq_t", [P, QFT, P])
    mag_x, sign_x, level_x = ph.sb("mag_x", [P, D]), ph.sb("sign_x", [P, D]), ph.sb("level_x", [P, D])
    gu_ps = ph.psum("gu_ps", [P, 4, 512])
    x_ps = ph.psum("x_ps", [P, 512])
    h_ps = ph.psum("h_ps", [P, 2, 512])
    y_ps = ph.psum("y_ps", [P, KD, P])
    staged, x_turned, x_abs, x_sign, x_quant = (ph.sem(n) for n in ("staged", "x_turned", "x_abs", "x_sign", "x_quant"))
    xq_turned, xq_kept, gu_ready, silu_ready = (ph.sem(n) for n in ("xq_turned", "xq_kept", "gu_ready", "silu_ready"))
    h_ready, h_abs, h_sign, h_quant, hq_turned = (ph.sem(n) for n in ("h_ready", "h_abs", "h_sign", "h_quant", "hq_turned"))
    x_hold = ph.sem("x_hold")
    hq_kept, y_ready, added, loaded = (ph.sem(n) for n in ("hq_kept", "y_ready", "added", "loaded"))
    widths = [min(P, QF - t * P) for t in range(QFT)]
    PER = 2 * Quantiser.STEPS

    with nc.Block() as block:
        @block.sync
        def _(sp):
            for d, source in loads:
                sp.dma_start(d, source).then_inc(loaded, 16)
            wait(sp, loaded, 16 * len(loads))

        @block.gpsimd
        def _(pool):
            def stage(b):
                wait(pool, x_turned, 2 * b)
                for t in range(2):
                    for k in range(KD):
                        op = pool.tensor_copy(xs[:, t, k, :], tokens(src, k, b)[:, :, t * P:(t + 1) * P].rearrange("p a t -> p (a t)"))
                op.then_inc(staged, 1)
            stage(0)
            with pool.Fori(1, SLOTS) as b:
                stage(b)

        @block.tensor
        def _(pe):
            def turn_x(n, t, b):
                wait(pe, staged, b + 1)
                wait(pe, xq_kept, n)
                for k in range(KD):
                    mm = pe.transpose(x_ps[:, k * P:(k + 1) * P], xs[:, t, k, :], ident[:, :])
                mm.then_inc(x_turned, 1)

            def turn_xq(n):
                wait(pe, x_quant, n + 1)
                for k in range(KD):
                    mm = pe.transpose(x_ps[:, D + k * P:D + (k + 1) * P], xq[:, k * P:(k + 1) * P], ident[:, :])
                mm.then_inc(xq_turned, 1)

            def gate_up(n):
                wait(pe, xq_kept, n + 1)
                wait(pe, h_ready, n)
                for i, w in enumerate((gate_t, up_t)):
                    for half in range(2):
                        for k in range(KD):
                            mm = pe.matmul(gu_ps[:, 2 * i + half, 0:HF], xq_t[:, k, :], w[:, k, half * HF:(half + 1) * HF],
                                           start=(k == 0), stop=(k == KD - 1))
                mm.then_inc(gu_ready, 1)

            def down(n):
                wait(pe, h_quant, n + 1)
                wait(pe, hq_kept, n)
                for t in range(QFT):
                    w = widths[t]
                    mm = pe.transpose(h_ps[0:w, t // 4, (t % 4) * P:(t % 4 + 1) * P], hq[:, t * P:t * P + w], ident[:, :])
                mm.then_inc(hq_turned, 1)
                wait(pe, hq_kept, n + 1)
                wait(pe, added, n)
                for m in range(KD):
                    for t in range(QFT):
                        w = widths[t]
                        mm = pe.matmul(y_ps[:, m, :], down_t[0:w, t, m * P:(m + 1) * P], hq_t[0:w, t, :],
                                       start=(t == 0), stop=(t == QFT - 1))
                mm.then_inc(y_ready, 1)

            def tile(n, t, b, first=False):
                turn_xq(n)
                turn_x(n + 1, 1 - t, b + t)
                gate_up(n)
                if not first:
                    down(n - 1)

            turn_x(0, 0, 0)
            tile(0, 0, 0, first=True)
            tile(1, 1, 0)
            with pe.Fori(1, B) as b:
                tile(2 * b, 0, b)
                tile(2 * b + 1, 1, b)
            down(2 * B - 1)

        @block.scalar
        def _(act):
            def split_x(n):
                wait(act, x_turned, n + 1)
                wait(act, x_quant, n)
                act.activation(mag_x[:, :], x_ps[:, 0:D], ACT.Abs).then_inc(x_abs, 1)
                act.activation(sign_x[:, :], x_ps[:, 0:D], ACT.Sign).then_inc(x_sign, 1)

            def keep_xq(n):
                wait(act, xq_turned, n + 1)
                wait(act, gu_ready, n)
                act.activation(xq_t[:, :, :].rearrange("p k t -> p (k t)"), x_ps[:, D:2 * D], ACT.Copy).then_inc(xq_kept, 1)

            def gate(n):
                wait(act, gu_ready, n + 1)
                wait(act, h_ready, n)
                act.activation(silu[:, :, :], gu_ps[:, 0:2, 0:HF], ACT.Silu).then_inc(silu_ready, 1)

            def keep_hq(n):
                wait(act, hq_turned, n + 1)
                wait(act, y_ready, n)
                act.activation(hq_t[:, 0:4, :].rearrange("p t n -> p (t n)"), h_ps[:, 0, :], ACT.Copy)
                act.activation(hq_t[:, 4, :], h_ps[:, 1, 0:P], ACT.Copy)
                act.activation(hq_t[0:widths[5], 5, :], h_ps[0:widths[5], 1, P:2 * P], ACT.Copy).then_inc(hq_kept, 1)

            def split_h(n):
                wait(act, h_ready, n + 1)
                wait(act, h_quant, n)
                act.activation(qx.mag[:, 0, :], hid[:, :], ACT.Abs).then_inc(h_abs, 1)
                act.activation(qx.sign[:, 0, :], hid[:, :], ACT.Sign).then_inc(h_sign, 1)

            def tile(n, first=False):
                keep_xq(n)
                split_x(n + 1)
                gate(n)
                if not first:
                    keep_hq(n - 1)
                split_h(n)

            split_x(0)
            tile(0, first=True)
            with act.Fori(1, 2 * B) as n:
                tile(n)
            keep_hq(2 * B - 1)

        @block.vector
        def _(dve):
            def quantise_x(n):
                wait(dve, x_abs, n + 1)
                wait(dve, x_sign, n + 1)
                wait(dve, xq_turned, n)
                dve.sem_inc(x_hold, 1)
                qx(dve, xq[:, :], mag_x[:, :], sign_x[:, :], level_x[:, :], PER * n)
                dve.sem_inc(x_quant, 1)

            def multiply(n):
                wait(dve, silu_ready, n + 1)
                wait(dve, h_abs, n)
                wait(dve, h_sign, n)
                dve.tensor_tensor(hid[:, :].rearrange("p (a f) -> p a f", a=2), silu[:, :, :], gu_ps[:, 2:4, 0:HF], ALU.mult)\
                    .then_inc(h_ready, 1)

            def quantise_h(n):
                wait(dve, h_abs, n + 1)
                wait(dve, h_sign, n + 1)
                wait(dve, hq_turned, n)
                dve.sem_inc(x_hold, 1)
                qx(dve, hq[:, :], qx.mag[:, 0, :], qx.sign[:, 0, :], qx.level[:, 0, :], PER * n + Quantiser.STEPS)
                dve.sem_inc(h_quant, 1)

            def add(n, t, b):
                wait(dve, y_ready, n + 1)
                for m in range(KD):
                    r = tokens(res, m, b)[:, :, t * P:(t + 1) * P].rearrange("p a t -> p (a t)")
                    op = dve.tensor_tensor(r, r, y_ps[:, m, :], ALU.add)
                op.then_inc(added, 1)

            def tile(n, t, b, first=False):
                multiply(n)
                quantise_h(n)
                if not first:
                    add(n - 1, 1 - t, b - (1 - t))
                quantise_x(n + 1)

            quantise_x(0)
            tile(0, 0, 0, first=True)
            tile(1, 1, 0)
            with dve.Fori(1, B) as b:
                tile(2 * b, 0, b)
                tile(2 * b + 1, 1, b)
            add(2 * B - 1, 1, B - 1)
    ph.close()


def program(nc, dram, out):
    whole = ExitStack()

    def sb(name, shape, dt=F32):
        return whole.enter_context(nc.sbuf_tensor(name, shape, dt))

    h = sb("h", [P, KD, SLOTS * PAD])
    xr = sb("xr", [P, KD, SLOTS * PAD])
    xn = sb("xn", [P, KD, SLOTS * PAD])
    w_in = sb("w_in", [P, KD, 3 * INNER])
    w_out = sb("w_out", [P, INNER // P, D])
    ident, ones = sb("ident", [P, P]), sb("ones", [P, P])
    iota, eps = sb("iota", [P, 1]), sb("eps", [P, 1])
    expo, no_bias = sb("expo", [P, 2 * HG]), sb("no_bias", [P, KD])
    tok_g, tok_b = sb("tok_g", [P, KD]), sb("tok_b", [P, KD])
    mask = sb("mask", [P, QT, S])
    rows = lambda w: w.rearrange("(k p) n -> p k n", p=P)

    start = Phase(nc, "start")
    s = start.stack
    emb, pca = start.sb("emb", [V, D]), start.sb("pca", [V, P])
    proj, fus = start.sb("proj", [PCA, D]), start.sb("fus", [P, 2 * KD, D])
    proj_b, fus_b = start.sb("proj_b", [P, KD]), start.sb("fus_b", [P, KD])
    a_in, b_in = start.sb("a_in", [16, 3, D]), start.sb("b_in", [16, 3 * INNER])
    a_out, b_out = start.sb("a_out", [16, INNER]), start.sb("b_out", [16, D])
    loaded, pca_zeroed = start.sem("loaded"), start.sem("pca_zeroed")
    first = [(ident[:, :], dram["ident"]), (ones[:, :], dram["ones"]), (iota[:, :], dram["iota"]),
             (emb[:, :], dram["emb"]), (pca[:, 0:PCA], dram["pca"]), (proj[:, :], dram["proj_w"]),
             (fus[:, :, :], rows(dram["fus_w"])), (proj_b[:, :], dram["proj_b"]),
             (fus_b[:, :], dram["fus_b"]), (tok_g[:, :], dram["tok_g"]),
             (tok_b[:, :], dram["tok_b"])]
    with nc.Block() as block:
        @block.sync
        def _(sp):
            sp.wait_ge(pca_zeroed, 1)
            for dst, source in first:
                sp.dma_start(dst, source).then_inc(loaded, 16)
            sp.wait_ge(loaded, 16 * len(first))

        @block.vector
        def _(dve):
            dve.memset(pca[:, :], 0.0).then_inc(pca_zeroed, 1)
            dve.memset(eps[:, :], EPS)
            dve.memset(expo[:, :], -0.5)
            dve.memset(no_bias[:, :], 0.0)
            for x in (h, xr, xn):
                dve.memset(x[:, :, :], 0.0)
    token_features(nc, {"iota": iota}, dram, emb, pca, proj, proj_b, fus, fus_b, xn,
                   [(w_in[:, :, :], rows(dram["l0_w_in"])), (w_out[:, :, :], rows(dram["l0_w_out"])),
                    (a_in[:, :, :], dram["l0_a_in"]), (b_in[:, :], dram["l0_b_in"]),
                    (a_out[:, :], dram["l0_a_out"]), (b_out[:, :], dram["l0_b_out"]),
                    (mask[:, :, :], dram["causal"])])
    layer_norm(nc, "tok_norm", xn, h, ones, eps, gamma=tok_g, beta=tok_b)

    merge_lora(nc, w_in, w_out, a_in, b_in, a_out, b_out)
    start.close()
    layer_norm(nc, "norm0", h, xn, ones, eps)
    bias = Phase(nc, "bias")
    bias_in, bias_out = bias.sb("in", [P, 3 * INNER]), bias.sb("out", [P, KD])
    with nc.Block() as block:
        @block.vector
        def _(dve):
            dve.memset(bias_in[:, :], 0.0)
    attention(nc, "attn0", "plain", xn, h, w_in, w_out, ident, mask, L0_HD ** -0.5, [(0, P), (0, S)],
              bias_in, no_bias, None, None, None, [])

    layer_norm(nc, "norm1", h, xn, ones, eps)
    quant = Phase(nc, "quant")
    gate_t, up_t = quant.sb("gate_t", [P, KD, QF]), quant.sb("up_t", [P, KD, QF])
    down_t = quant.sb("down_t", [P, QFT, D])
    quantise_weights(nc, gate_t, up_t, down_t, dram, ident,
                     [(w_in[:, :, :], rows(dram["l1_w_in"])), (w_out[:, :, :], rows(dram["l1_w_out"]))])
    quantised_feed_forward(nc, xn, h, gate_t, up_t, down_t, ident,
                           [(bias_in[:, :], dram["l1_b_in"].unsqueeze(0).broadcast_to([P, 3 * INNER])),
                            (bias_out[:, :], dram["l1_b_out"]), (mask[:, :, :], dram["open"]),
                            (tok_g[:, :], dram["l1_g"]), (tok_b[:, :], dram["l1_b"])])
    quant.close()

    layer_norm(nc, "norm2", h, xr, ones, eps)
    layer_norm(nc, "norm3", xr, xn, ones, eps, gamma=tok_g, beta=tok_b)
    attention(nc, "attn1", "plain", xn, h, w_in, w_out, ident, mask, HD ** -0.5, [(0, S), (0, S)],
              bias_in, bias_out, None, None, None, [])
    bias.close()
    layer_norm(nc, "norm4", h, xr, ones, eps)

    w1, w2 = sb("w1", [P, KD, 2 * FF]), sb("w2", [P, FT, D])
    b1, b2 = sb("b1", [P, 2 * FT]), sb("b2", [P, KD])
    ln_g, ln_b = sb("ln_g", [P, KD]), sb("ln_b", [P, KD])
    cos_base, sin_base = sb("cos_base", [P, QT, 2, HD]), sb("sin_base", [P, QT, 2, HD])
    cos, sin = sb("cos", [P, QT, 2, HD]), sb("sin", [P, QT, 2, HD])
    head_scale, head_scale_swapped = sb("head_scale", [P, 2, HD]), sb("head_scale_swapped", [P, 2, HD])

    def layer_of(name, l):
        v = dram[name][bass.ds(l, 1)]
        return v.rearrange("a b -> (a b)") if len(v.shape) == 2 else v.rearrange("a b c -> (a b) c")

    def attention_loads(l):
        half = HD // 2
        loads = [(w_in[:, :, :], rows(layer_of("Wqkv", l))), (w_out[:, :, :], rows(layer_of("Wo", l)))]
        for i, name in enumerate(("q_scale", "k_scale")):
            v = layer_of(name, l)
            loads.append((head_scale[:, i, :], v.unsqueeze(0).broadcast_to([P, HD])))
            for lo in (0, half):
                loads.append((head_scale_swapped[:, i, lo:lo + half],
                              v[half - lo:HD - lo].unsqueeze(0).broadcast_to([P, half])))
        return loads

    def feed_forward_loads(l):
        w1_l, w2_l = layer_of("W1", l), layer_of("W2", l)
        whole_rows = (FT - 1) * P
        rest = FF - whole_rows
        loads = [(w1[:, :, :], rows(w1_l)), (w2[:, 0:FT - 1, :], rows(w2_l[0:whole_rows, :])),
                 (w2[0:rest, FT - 1, :], w2_l[whole_rows:FF, :])]
        for dst, name in ((b1, "b1"), (b2, "b2"), (ln_g, "ln_g"), (ln_b, "ln_b")):
            loads.append((dst[:, :], layer_of(name, l)))
        return loads

    pre = Phase(nc, "pre")
    pre_loaded = pre.sem("loaded")
    pre_loads = [(cos_base[:, :, :, :], dram["cos"]), (sin_base[:, :, :, :], dram["sin"]), (mask[:, :, :], dram["local"])]
    pre_loads += attention_loads(0)
    with nc.Block() as block:
        @block.sync
        def _(sp):
            for dst, source in pre_loads:
                sp.dma_start(dst, source).then_inc(pre_loaded, 16)
            sp.wait_ge(pre_loaded, 16 * len(pre_loads))
    pre.close()

    with nc.Fori(0, DEPTH) as l:
        with nc.Block() as block:
            @block.vector
            def _(dve):
                for t in range(QT):
                    dve.tensor_tensor(cos[:, t, :, :], cos_base[:, t, :, :], head_scale[:, :, :], ALU.mult)
                    dve.tensor_tensor(sin[:, t, :, :], sin_base[:, t, :, :], head_scale_swapped[:, :, :], ALU.mult)
        attention(nc, "local", "rope", xr, xr, w_in, w_out, ident, mask, 8.0, [(0, P), (WINDOW, S)],
                  None, no_bias, cos, sin, expo, feed_forward_loads(l))
        layer_norm(nc, "ff_norm", xr, xn, ones, eps, shift=True, gamma=ln_g, beta=ln_b)
        feed_forward(nc, "ff", xn, xr, w1, b1, w2, b2, attention_loads((l + 1) % DEPTH))

    end = Phase(nc, "end")
    summed, stored = end.sem("summed"), end.sem("stored")
    with nc.Block() as block:
        @block.vector
        def _(dve):
            for k in range(KD):
                dve.tensor_tensor(tokens(xn, k, 0, B), tokens(h, k, 0, B), tokens(xr, k, 0, B), ALU.add).then_inc(summed, 1)

        @block.sync
        def _(sp):
            for k in range(KD):
                sp.wait_ge(summed, k + 1)
                sp.dma_start(out[k * P:(k + 1) * P, :].rearrange("p (b t) -> p b t", t=S), tokens(xn, k, 0, B)).then_inc(stored, 16)
            sp.wait_ge(stored, 16 * KD)
    end.close()
    whole.close()


def constants():
    i, j = np.arange(S)[:, None], np.arange(S)[None, :]
    tiled = lambda x: np.ascontiguousarray(x.reshape(QT, P, *x.shape[1:]).swapaxes(0, 1), dtype=np.float32)
    additive = lambda allowed: tiled(np.where(allowed, 0.0, LOW))
    half = np.arange(0, HD, 2, dtype=np.float32)
    inv_freq = (1.0 / 10000.0 ** (half / HD)).astype(np.float32)
    t = np.arange(S, dtype=np.float32)
    freqs = (t[:, None] * inv_freq[None, :]).astype(np.float32)
    freqs = np.concatenate([freqs, freqs], -1)
    base = ((half + 0.4 * HD) / (1.4 * HD)).astype(np.float32)
    power = (t - S // 2) / (WINDOW // 2)
    scale = (base[None, :] ** power[:, None]).astype(np.float32)
    scale = np.concatenate([scale, scale], -1)
    sign = np.where(np.arange(HD) < HD // 2, -1.0, 1.0)
    cos = np.stack([np.cos(freqs) * scale, np.cos(freqs) / scale], 1)
    sin = np.stack([np.sin(freqs) * scale * sign, np.sin(freqs) / scale * sign], 1)
    return {
        "ident": np.eye(P, dtype=np.float32), "ones": np.full((P, P), 1.0 / D, np.float32),
        "iota": np.arange(P, dtype=np.float32)[:, None],
        "causal": additive(j <= i), "open": additive(i + j >= 0), "local": additive((j <= i) & (j >= i - WINDOW)),
        "cos": tiled(cos), "sin": tiled(sin),
    }


def laid_out(x):
    def spread(w):
        o = np.zeros((*w.shape[:-1], H, HD), w.dtype)
        o[..., :L0_HD] = w.reshape(*w.shape[:-1], H, L0_HD)
        return o.reshape(*w.shape[:-1], INNER)

    def by_partition(v):
        n = -(-v.shape[-1] // P)
        o = np.zeros((*v.shape[:-1], n * P), v.dtype)
        o[..., :v.shape[-1]] = v
        return o.reshape(*v.shape[:-1], n, P).swapaxes(-1, -2)

    a = {
        "x": x["x"].reshape(-1), "mask": x["mask_BS_i1_0"].reshape(-1),
        "emb": x["L0_tok_emb"], "pca": x["L0_tok_pca_lookup"], "proj_w": x["L0_tok_proj_w"], "fus_w": x["L0_tok_fus_w"],
        "proj_b": by_partition(x["L0_tok_proj_b"]), "fus_b": by_partition(x["L0_tok_fus_b"]), "tok_g": by_partition(x["L0_tok_ln_g"]), "tok_b": by_partition(x["L0_tok_ln_b"]),
        "l0_w_in": np.concatenate([spread(x[f"L0_attn_w{c}"].T) for c in "qkv"], 1),
        "l0_w_out": spread(x["L0_attn_wo"]).T,
        "l0_a_in": np.stack([x[f"L0_attn_a{c}"] for c in "qkv"], 1),
        "l0_b_in": np.concatenate([spread(x[f"L0_attn_b{c}"].T) for c in "qkv"], 1),
        "l0_a_out": spread(x["L0_attn_ao"]), "l0_b_out": x["L0_attn_bo"].T,
        "w_gate": x["L0_ffn_w_gate"], "w_up": x["L0_ffn_w_up"], "w_down": x["L0_ffn_w_down"],
        "l1_w_in": x["L1_attn_w_qkv"], "l1_w_out": x["L1_attn_w_out"], "l1_b_in": x["L1_attn_b_qkv"],
        "l1_b_out": by_partition(x["L1_attn_b_out"]), "l1_g": by_partition(x["L1_attn_ln_gamma"]), "l1_b": by_partition(x["L1_attn_ln_beta"]),
    }
    for n in ("Wqkv", "q_scale", "k_scale", "Wo", "W1", "W2"):
        a[n] = x[f"L1_ffn_{n}"]
    for n in ("ln_g", "ln_b", "b2"):
        a[n] = by_partition(x[f"L1_ffn_{n}"])
    b1 = x["L1_ffn_b1"]
    a["b1"] = np.concatenate([by_partition(b1[:, :FF]), by_partition(b1[:, FF:])], -1)
    return a


def build(nc, arrays):
    dram = {n: nc.dram_tensor(f"in_{n}", a.shape, mybir.dt.from_np(a.dtype), kind="ExternalInput").ap()
            for n, a in arrays.items()}
    out = nc.dram_tensor("out_0", (D, B * S), F32, kind="ExternalOutput").ap()
    program(nc, dram, out)


def kernel(**inputs):
    import concourse.bacc as bacc
    from concourse.bass_utils import run_bass_kernel_spmd

    arrays = {n: np.ascontiguousarray(a) for n, a in {**laid_out({k: np.asarray(v) for k, v in inputs.items()}), **constants()}.items()}
    nc = bacc.Bacc("TRN2", target_bir_lowering=False, num_devices=1)
    build(nc, arrays)
    r = run_bass_kernel_spmd(nc, [{f"in_{n}": a for n, a in arrays.items()}], core_ids=[0])
    return np.ascontiguousarray(r.results[0]["out_0"].reshape(D, B, S).transpose(1, 2, 0))
```

```python
from contextlib import ExitStack

import numpy as np
import concourse.bass as bass
from concourse import mybir

F32 = mybir.dt.float32
I32 = mybir.dt.int32
ALU = mybir.AluOpType
ACT = mybir.ActivationFunctionType
AX = mybir.AxisListType

P = 128
B, S, D = 8, 256, 256
KD = D // P
PAD = S + 1
SLOTS = B + 1
H, HD = 16, 64
INNER = H * HD
HG = 4
NG = H // HG
GW = HG * HD
QT = S // P
DEPTH = 6
WINDOW = 64
V, PCA = 28, 20
FF = 682
FT = -(-FF // P)
QF = 704
QFT = -(-QF // P)
BLK = 16
LOW = -1e30
EPS = 1e-5
L0_HD = 16


def wait(eng, sem, value):
    if isinstance(value, int) and value <= 0:
        return
    eng.wait_ge(sem, value)


class Phase:

    def __init__(self, nc, name):
        self.nc, self.name, self.stack, self.sems = nc, name, ExitStack(), []

    def sb(self, name, shape, dt=F32):
        return self.stack.enter_context(self.nc.sbuf_tensor(f"{self.name}_{name}", shape, dt))

    def psum(self, name, shape, dt=F32):
        return self.stack.enter_context(self.nc.psum_tensor(f"{self.name}_{name}", shape, dt))

    def sem(self, name):
        s = self.stack.enter_context(self.nc.semaphore(f"{self.name}_{name}"))
        self.sems.append(s)
        return s

    def close(self):
        for s in self.sems:
            self.nc.sync.sem_clear(s)
        self.nc.all_engine_barrier()
        self.stack.close()


def tokens(x, k, b, n=1, shift=False):
    v = x[:, k, :].rearrange("p (b t) -> p b t", t=PAD)
    at = 0 if shift and k == 1 else 1
    return v[:, bass.ds(b, n), at:at + S]


CH = 2 * S
NCH = B * S // CH
TC = CH // P


class Norm:

    def __init__(self, ph, consts, src, dst, shift, gamma, beta, ring):
        self.ring = ring
        self.c, self.src, self.dst, self.shift, self.gamma, self.beta = consts, src, dst, shift, gamma, beta
        self.sq = ph.sb("norm_sq", [P, ring, KD, CH])
        self.var = ph.sb("norm_var", [P, ring, TC])
        self.rstd = ph.sb("norm_rstd", [P, ring, TC])
        self.diag = ph.sb("norm_diag", [P, ring, CH])
        self.mean_ps = ph.psum("norm_mean_ps", [P, ring, CH])
        self.spread_ps = ph.psum("norm_spread_ps", [P, ring, CH])
        (self.mean_ready, self.centred, self.squared, self.var_ready, self.var_kept, self.rstd_ready,
         self.diag_ready, self.spread_ready, self.scaled, self.normed) = (
            ph.sem("norm_" + n) for n in ("mean_ready", "centred", "squared", "var_ready", "var_kept",
                                          "rstd_ready", "diag_ready", "spread_ready", "scaled", "normed"))
        self.done = self.scaled if gamma is None else self.normed

    def mean(self, pe, c):
        wait(pe, self.centred, c + 1 - self.ring)
        for k in range(KD):
            mm = pe.matmul(self.mean_ps[:, c % self.ring, :].rearrange("p (b t) -> p b t", t=S), self.c["ones"][:, :],
                           tokens(self.src, k, 2 * c, 2, self.shift), start=(k == 0), stop=(k == KD - 1))
        mm.then_inc(self.mean_ready, 1)

    def centre(self, dve, c):
        wait(dve, self.mean_ready, c + 1)
        for k in range(KD):
            op = dve.tensor_tensor(self.dst(c, k), tokens(self.src, k, 2 * c, 2, self.shift),
                                   self.mean_ps[:, c % self.ring, :].rearrange("p (b t) -> p b t", t=S), ALU.subtract)
        op.then_inc(self.centred, 1)

    def square(self, act, c):
        wait(act, self.centred, c + 1)
        wait(act, self.var_ready, c + 1 - self.ring)
        for k in range(KD):
            op = act.activation(self.sq[:, c % self.ring, k, :].rearrange("p (b t) -> p b t", t=S), self.dst(c, k), ACT.Square)
        op.then_inc(self.squared, 1)

    def variance(self, pe, c):
        wait(pe, self.squared, c + 1)
        wait(pe, self.scaled, c + 1 - self.ring)
        for t in range(TC):
            for k in range(KD):
                mm = pe.matmul(self.spread_ps[:, c % self.ring, t:t + 1], self.sq[:, c % self.ring, k, t * P:(t + 1) * P], self.c["ones"][:, 0:1],
                               start=(k == 0), stop=(k == KD - 1))
        mm.then_inc(self.var_ready, 1)

    def keep_variance(self, dve, c):
        wait(dve, self.var_ready, c + 1)
        wait(dve, self.rstd_ready, c + 1 - self.ring)
        dve.tensor_scalar(self.var[:, c % self.ring, :], self.spread_ps[:, c % self.ring, 0:TC], EPS, None, ALU.add).then_inc(self.var_kept, 1)

    def power(self, pool, c):
        wait(pool, self.var_kept, c + 1)
        wait(pool, self.diag_ready, c + 1 - self.ring)
        pool.tensor_tensor(self.rstd[:, c % self.ring, :], self.var[:, c % self.ring, :], self.c["expo"][:, 0:TC], ALU.pow).then_inc(self.rstd_ready, 1)

    def diagonal(self, dve, c):
        wait(dve, self.rstd_ready, c + 1)
        wait(dve, self.spread_ready, c + 1 - self.ring)
        for t in range(TC):
            op = dve.tensor_scalar(self.diag[:, c % self.ring, t * P:(t + 1) * P], self.c["ident"][:, :], self.rstd[:, c % self.ring, t:t + 1], None, ALU.mult)
        op.then_inc(self.diag_ready, 1)

    def spread(self, pe, c):
        wait(pe, self.diag_ready, c + 1)
        pe.matmul(self.spread_ps[:, c % self.ring, :], self.c["full"][:, :], self.diag[:, c % self.ring, :], start=True, stop=True).then_inc(self.spread_ready, 1)

    def scale(self, dve, c):
        wait(dve, self.spread_ready, c + 1)
        for k in range(KD):
            op = dve.tensor_tensor(self.dst(c, k), self.dst(c, k), self.spread_ps[:, c % self.ring, :].rearrange("p (b t) -> p b t", t=S), ALU.mult)
        op.then_inc(self.scaled, 1)

    def affine(self, act, c):
        if self.gamma is None:
            return
        wait(act, self.scaled, c + 1)
        for k in range(KD):
            op = act.activation(self.dst(c, k), self.dst(c, k), ACT.Identity, bias=self.beta[:, k:k + 1], scale=self.gamma[:, k:k + 1])
        op.then_inc(self.normed, 1)


def layer_norm(nc, name, src, dst, consts, gamma=None, beta=None):
    ph = Phase(nc, name)
    norm = Norm(ph, consts, src, lambda c, k: tokens(dst, k, 2 * c, 2), False, gamma, beta, NCH)

    with nc.Block() as block:
        @block.tensor
        def _(pe):
            for c in range(NCH):
                norm.mean(pe, c)
            for c in range(NCH + 1):
                if c < NCH:
                    norm.variance(pe, c)
                if c:
                    norm.spread(pe, c - 1)

        @block.scalar
        def _(act):
            for c in range(NCH):
                norm.square(act, c)
            for c in range(NCH):
                norm.affine(act, c)

        @block.vector
        def _(dve):
            for c in range(NCH):
                norm.centre(dve, c)
            for c in range(NCH + 1):
                if c < NCH:
                    norm.keep_variance(dve, c)
                    norm.diagonal(dve, c)
                if c:
                    norm.scale(dve, c - 1)

        @block.gpsimd
        def _(pool):
            for c in range(NCH):
                norm.power(pool, c)
    ph.close()


def attention(nc, name, kind, src, res, w_in, w_out, ident, mask, scale, keys, bias_in, bias_out,
              cos, sin, expo, loads):
    ph = Phase(nc, name)
    rope = kind == "rope"
    xs = ph.sb("xs", [P, KD, S])
    qk = ph.sb("qk", [P, 2, QT, 2 * GW])
    qk_rot = ph.sb("qk_rot", [P, QT, 2 * GW]) if rope else None
    sq = ph.sb("sq", [P, QT, 2 * GW]) if rope else None
    ssq = ph.sb("ssq", [P, QT, 2 * HG]) if rope else None
    q_t = ph.sb("q_t", [P, 2, 2, S])
    k_t = ph.sb("k_t", [P, 2, 2, S])
    v_sb = ph.sb("v_sb", [P, 2, QT, GW])
    probs = ph.sb("probs", [P, 4, QT, S])
    probs_t = ph.sb("probs_t", [P, 2, QT, S])
    row_max = ph.sb("row_max", [P, 4, QT])
    neg_max = ph.sb("neg_max", [P, 4, QT])
    row_sum = ph.sb("row_sum", [P, 2, 2, QT * 2])
    inv_sum = ph.sb("inv_sum", [P, 2, QT * 2])
    out = ph.sb("out", [P, QT, GW])
    out_t = ph.sb("out_t", [P, 2, S])

    proj_ps = ph.psum("proj_ps", [P, 2, 512])
    score_ps = ph.psum("score_ps", [P, 2, QT, S])
    probs_t_ps = ph.psum("probs_t_ps", [P, QT, S])
    turn_ps = ph.psum("turn_ps", [P, 2, S])
    val_ps = ph.psum("val_ps", [P, 2, 512])

    xs_ready, proj_full, proj_free = ph.sem("xs_ready"), ph.sem("proj_full"), ph.sem("proj_free")
    sq_done, ssq_done, qk_ready, pool_step = ph.sem("sq_done"), ph.sem("ssq_done"), ph.sem("qk_ready"), ph.sem("pool_step")
    turn_full, turn_free = ph.sem("turn_full"), ph.sem("turn_free")
    score_full, score_free, max_ready = ph.sem("score_full"), ph.sem("score_free"), ph.sem("max_ready")
    exp_done, pt_full, pt_ready = ph.sem("exp_done"), ph.sem("pt_full"), ph.sem("pt_ready")
    val_done, inv_ready, out_ready = ph.sem("val_done"), ph.sem("inv_ready"), ph.sem("out_ready")
    dve_hold, pool_hold = ph.sem("dve_hold"), ph.sem("pool_hold")
    loaded, cleared = ph.sem("loaded"), ph.sem("cleared")

    def q_fill(G):
        return 0 if isinstance(G, int) and G == 0 else 3 * G - 1

    def k_fill(G):
        return 1 if isinstance(G, int) and G == 0 else 3 * G

    def out_fill(G):
        return 3 * G + 4

    def v_fill(G):
        return 3 * G + 2 if isinstance(G, int) and G < 3 else 4 * G - 1

    def qk_fill(G, t):
        return 3 * G + t if isinstance(G, int) and G < 4 else 4 * G - 3 + t

    def w_fill(G):
        if isinstance(G, int) and G >= NG * B - 2:
            return 4 * NG * B + 3 + G - (NG * B - 2)
        return 4 * G + 12

    def proj_bank(fill, steady):
        return proj_ps[:, fill % 2 if isinstance(fill, int) else steady, :]

    def pair_of(ps, pair):
        return ps[:, pair, 0:QT * 2 * HD].rearrange("p (t h d) -> p t h d", t=QT, d=HD)

    def back(N, forward):
        return not isinstance(N, int) or (N >= 0 and (forward or N < HG * NG * B))

    def blocks():
        return [(kt, qt) for qt in range(QT) for kt in range(QT)
                if keys[qt][0] < (kt + 1) * P and keys[qt][1] > kt * P]

    with nc.Block() as block:
        @block.tensor
        def _(pe):
            def project(G, g, part, batch):
                f = v_fill(G) if part == 2 else qk_fill(G, part)
                bank = proj_bank(f, (1, 0, 1)[part])
                wait(pe, proj_free, f - 1)
                if g == 0 and part == 0:
                    wait(pe, xs_ready, batch + 1)
                if part < 2:
                    for k in range(KD):
                        w = w_in[:, k, 0:2 * INNER].rearrange("p (s n) -> p s n", s=2)[:, :, g * GW:(g + 1) * GW]
                        mm = pe.matmul(bank, xs[:, k, part * P:(part + 1) * P], w, start=(k == 0), stop=(k == KD - 1))
                else:
                    for t in range(QT):
                        for k in range(KD):
                            mm = pe.matmul(bank[:, t * GW:(t + 1) * GW], xs[:, k, t * P:(t + 1) * P],
                                           w_in[:, k, 2 * INNER + g * GW:2 * INNER + (g + 1) * GW],
                                           start=(k == 0), stop=(k == KD - 1))
                mm.then_inc(proj_full, 1)

            def turn(src_tiles, fill):
                wait(pe, turn_free, fill)
                for i, j, tile in src_tiles:
                    mm = pe.transpose(turn_ps[:, i, j * P:(j + 1) * P], tile, ident[:, :])
                mm.then_inc(turn_full, 1)

            def turn_qk(G, g, which):
                if rope:
                    wait(pe, qk_ready, 2 * G + 2)
                else:
                    wait(pe, proj_free, qk_fill(G, 1) + 1)
                turn([(i, t, qk[:, g % 2, t, which * GW + i * P:which * GW + (i + 1) * P]) for i in range(2) for t in range(QT)],
                     (q_fill, k_fill)[which](G))

            def scores(N, G, g, j):
                if j == 0:
                    wait(pe, turn_free, k_fill(G) + 1)
                wait(pe, score_free, N - 1)
                r = slice((j % 2) * HD, (j % 2 + 1) * HD)
                for qt in range(QT):
                    a, z = keys[qt]
                    mm = pe.matmul(score_ps[:, j % 2, qt, a:z], q_t[r, g % 2, j // 2, qt * P:(qt + 1) * P],
                                   k_t[r, g % 2, j // 2, a:z], start=True, stop=True)
                mm.then_inc(score_full, 1)

            def turn_probs(N, j):
                wait(pe, exp_done, N + 1)
                wait(pe, pt_ready, N)
                for kt, qt in blocks():
                    mm = pe.transpose(probs_t_ps[:, kt, qt * P:(qt + 1) * P], probs[:, j, qt, kt * P:(kt + 1) * P], ident[:, :])
                mm.then_inc(pt_full, 1)

            def values(N, G, g, j):
                wait(pe, pt_ready, N + 1)
                if j == 0:
                    wait(pe, proj_free, v_fill(G) + 1)
                if j % 2 == 0:
                    wait(pe, out_ready, 2 * G + j // 2 - 1)
                for qt in range(QT):
                    kts = [kt for kt, q in blocks() if q == qt]
                    for kt in kts:
                        mm = pe.matmul(pair_of(val_ps, j // 2)[:, qt, j % 2, :], probs_t[:, j % 2, kt, qt * P:(qt + 1) * P],
                                       v_sb[:, g % 2, kt, j * HD:(j + 1) * HD], start=(kt == kts[0]), stop=(kt == kts[-1]))
                mm.then_inc(val_done, 1)

            def turn_out(G):
                wait(pe, out_ready, 2 * G + 2)
                turn([(i, t, out[:, t, i * P:(i + 1) * P]) for i in range(2) for t in range(QT)], out_fill(G))

            def project_out(G, g):
                f = w_fill(G)
                wait(pe, turn_free, out_fill(G) + 1)
                wait(pe, proj_free, f - 1)
                for m in range(KD):
                    for k in range(2):
                        mm = pe.matmul(proj_bank(f, 0)[:, m * S:(m + 1) * S], w_out[:, 2 * g + k, m * P:(m + 1) * P],
                                       out_t[:, k, :], start=(k == 0), stop=(k == 1))
                mm.then_inc(proj_full, 1)

            def body(b, forward=True):
                for g in range(NG):
                    G = NG * b + g
                    gn, gp, gq = (g + 1) % NG, (g - 1) % NG, (g + 2) % NG
                    for j in range(HG):
                        N = HG * G + j
                        if forward and j < 3:
                            scores(N + 1, G, g, j + 1)
                        if back(N - 1, forward):
                            turn_probs(N - 1, (j - 1) % HG)
                        if j == 0 and forward:
                            project(G + 1, gn, 2, b + (g + 1) // NG)
                        if j == 1 and back(HG * (G - 2), forward):
                            project_out(G - 2, gq)
                        if j == 2:
                            if back(HG * (G - 1), forward):
                                turn_out(G - 1)
                            if forward:
                                project(G + 2, gq, 0, b + (g + 2) // NG)
                        if j == 3 and forward:
                            turn_qk(G + 1, gn, 0)
                            project(G + 2, gq, 1, b + (g + 2) // NG)
                            turn_qk(G + 1, gn, 1)
                        if back(N - 2, forward):
                            values(N - 2, G if j >= 2 else G - 1, g if j >= 2 else gp, (j - 2) % HG)
                        if j == 3 and forward:
                            scores(N + 1, G + 1, gn, 0)
                    if not forward:
                        project_out(G - 1, gp)
                        break

            for part in range(3):
                project(0, 0, part, 0)
            project(1, 1, 0, 0)
            project(1, 1, 1, 0)
            turn_qk(0, 0, 0)
            turn_qk(0, 0, 1)
            scores(0, 0, 0, 0)
            body(0)
            with pe.Fori(1, B) as b:
                body(b)
            body(B, forward=False)

        @block.scalar
        def _(act):
            def stage(b):
                wait(act, proj_full, 4 * NG * b - 4)
                for k in range(KD):
                    op = act.activation(xs[:, k, :], tokens(src, k, b, 1, rope).rearrange("p a t -> p (a t)"), ACT.Copy)
                op.then_inc(xs_ready, 1)

            def square(G, g, t):
                f = qk_fill(G, t)
                wait(act, proj_full, f + 1)
                wait(act, ssq_done, 2 * (G - 1) + t + 1)
                act.activation(sq[:, t, :], proj_bank(f, 1 - t), ACT.Square).then_inc(sq_done, 1)

            def keep_qk(G, g, which):
                wait(act, turn_full, (q_fill, k_fill)[which](G) + 1)
                wait(act, score_full, HG * (G - 1))
                dst = (q_t, k_t)[which][:, g % 2, :, :]
                act.activation(dst, turn_ps[:, :, :], ACT.Copy).then_inc(turn_free, 1)

            def exps(N, G, g, j):
                wait(act, max_ready, N + 1)
                if j == 0:
                    wait(act, out_ready, 2 * G - 2)
                for qt in range(QT):
                    a, z = keys[qt]
                    op = act.activation(probs[:, j, qt, a:z], probs[:, j, qt, a:z], ACT.Exp, bias=neg_max[:, j, qt:qt + 1],
                                        scale=scale, accum_out=row_sum[:, g % 2, j // 2, 2 * qt + j % 2:2 * qt + j % 2 + 1])
                op.then_inc(exp_done, 1)

            def keep_probs_t(N, j):
                wait(act, pt_full, N + 1)
                wait(act, val_done, N - 1)
                if len(blocks()) == QT * QT:
                    op = act.activation(probs_t[:, j % 2, :, :], probs_t_ps[:, :, :], ACT.Copy)
                else:
                    act.activation(probs_t[:, j % 2, 0, :], probs_t_ps[:, 0, :], ACT.Copy)
                    op = act.activation(probs_t[:, j % 2, 1, P:S], probs_t_ps[:, 1, P:S], ACT.Copy)
                op.then_inc(pt_ready, 1)

            def keep_out_t(G):
                wait(act, turn_full, out_fill(G) + 1)
                if not (isinstance(G, int) and G == 0):
                    wait(act, proj_full, w_fill(G - 1) + 1)
                act.activation(out_t[:, :, :], turn_ps[:, :, :], ACT.Copy).then_inc(turn_free, 1)

            def body(b, forward=True):
                for g in range(NG):
                    G = NG * b + g
                    gn, gq = (g + 1) % NG, (g + 2) % NG
                    for j in range(HG):
                        N = HG * G + j
                        if forward and j == 1 and g == NG - 2:
                            stage(b + 1)
                        if back(N - 1, forward):
                            keep_probs_t(N - 1, (j - 1) % HG)
                        if j == 2 and back(HG * (G - 1), forward):
                            keep_out_t(G - 1)
                        if forward:
                            if j < 3:
                                exps(N + 1, G, g, j + 1)
                            if rope and j == 2:
                                square(G + 2, gq, 0)
                            if j == 3:
                                keep_qk(G + 1, gn, 0)
                                if rope:
                                    square(G + 2, gq, 1)
                                keep_qk(G + 1, gn, 1)
                                exps(N + 1, G + 1, gn, 0)
                    if not forward:
                        break

            stage(0)
            if rope:
                for G in (0, 1):
                    square(G, G, 0)
                    square(G, G, 1)
            keep_qk(0, 0, 0)
            keep_qk(0, 0, 1)
            exps(0, 0, 0, 0)
            body(0)
            with act.Fori(1, B) as b:
                body(b)
            body(B, forward=False)

        @block.vector
        def _(dve):
            def maxima(N, j):
                wait(dve, score_full, N + 1)
                wait(dve, pt_full, N - 3)
                dve.sem_inc(dve_hold, 1)
                for qt in range(QT):
                    a, z = keys[qt]
                    op = dve.tensor_tensor_reduce(probs[:, j, qt, a:z], score_ps[:, j % 2, qt, a:z], mask[:, qt, a:z],
                                                  1.0, -3e38, ALU.add, ALU.max, row_max[:, j, qt:qt + 1])
                op.then_inc(score_free, 1)
                wait(dve, score_free, N + 1)
                dve.tensor_scalar(neg_max[:, j, :], row_max[:, j, :], -scale, None, ALU.mult).then_inc(max_ready, 1)

            def turn_heads(G, g, t):
                f = qk_fill(G, t)
                bank = proj_bank(f, 1 - t)
                if not rope:
                    wait(dve, proj_full, f + 1)
                    if not (isinstance(G, int) and G < 2):
                        wait(dve, turn_full, k_fill(G - 2) + 1)
                    w = bias_in[:, 0:2 * INNER].rearrange("p (s n) -> p s n", s=2)[:, :, g * GW:(g + 1) * GW]
                    dve.tensor_tensor(qk[:, g % 2, t, :].rearrange("p (s n) -> p s n", s=2), bank.rearrange("p (s n) -> p s n", s=2),
                                      w, ALU.add).then_inc(proj_free, 1)
                    return
                wait(dve, sq_done, 2 * G + t + 1)
                wait(dve, qk_ready, 2 * (G - 1) + t + 1)
                dve.tensor_reduce(ssq[:, t, :], sq[:, t, :].rearrange("p (h d) -> p h d", d=HD), AX.X, ALU.add).then_inc(ssq_done, 1)
                if not (isinstance(G, int) and G < 2):
                    wait(dve, turn_full, k_fill(G - 2) + 1)
                view = lambda x: x.rearrange("p (s h d) -> p s h d", s=2, h=HG)
                table = lambda x, lo, hi: x[:, t, :, lo:hi].unsqueeze(2).broadcast_to([P, 2, HG, hi - lo])
                dve.tensor_tensor(view(qk[:, g % 2, t, :]), view(bank), table(cos, 0, HD), ALU.mult)
                half = HD // 2
                for lo in (0, half):
                    other = half - lo
                    op = dve.tensor_tensor(view(qk_rot[:, t, :])[:, :, :, lo:lo + half], view(bank)[:, :, :, other:other + half],
                                           table(sin, lo, lo + half), ALU.mult)
                op.then_inc(proj_free, 1)

            def keep_v(G, g):
                wait(dve, proj_full, v_fill(G) + 1)
                wait(dve, val_done, HG * (G - 1))
                dst = v_sb[:, g % 2, :, :]
                bank = proj_bank(v_fill(G), 1).rearrange("p (t n) -> p t n", t=QT)
                if rope:
                    op = dve.tensor_copy(dst, bank)
                else:
                    w = bias_in[:, 2 * INNER + g * GW:2 * INNER + (g + 1) * GW].unsqueeze(1).broadcast_to([P, QT, GW])
                    op = dve.tensor_tensor(dst, bank, w, ALU.add)
                op.then_inc(proj_free, 1)

            def norm(G, g, pair):
                wait(dve, val_done, HG * G + 2 * pair + 2)
                dve.reciprocal(inv_sum[:, pair, :], row_sum[:, g % 2, pair, :]).then_inc(inv_ready, 1)
                if not (isinstance(G, int) and G == 0):
                    wait(dve, turn_full, out_fill(G - 1) + 1)
                dve.wait_ge(inv_ready, 2 * G + pair + 1)
                dst = out[:, :, pair * P:(pair + 1) * P].rearrange("p t (h d) -> p t h d", d=HD)
                inv = inv_sum[:, pair, :].rearrange("p (t h) -> p t h", h=2).unsqueeze(3).broadcast_to([P, QT, 2, HD])
                dve.tensor_tensor(dst, pair_of(val_ps, pair), inv, ALU.mult).then_inc(out_ready, 1)

            def residual(G, g, b):
                f = w_fill(G)
                wait(dve, proj_full, f + 1)
                if g:
                    wait(dve, proj_free, w_fill(G - 1) + 1)
                for m in range(KD):
                    r, y = tokens(res, m, b).rearrange("p a t -> p (a t)"), proj_bank(f, 0)[:, m * S:(m + 1) * S]
                    if g == 0:
                        op = dve.scalar_tensor_tensor(r, y, bias_out[:, m:m + 1], r, ALU.add, ALU.add)
                    else:
                        op = dve.tensor_tensor(r, y, r, ALU.add)
                op.then_inc(proj_free, 1)

            def body(b, forward=True):
                for g in range(NG):
                    G = NG * b + g
                    gn, gp, gq = (g + 1) % NG, (g - 1) % NG, (g + 2) % NG
                    for j in range(HG):
                        N = HG * G + j
                        if j == 3 and forward:
                            turn_heads(G + 2, gq, 1)
                            norm(G, g, 0)
                        if forward:
                            maxima(N + 1, (j + 1) % HG)
                        if j == 1:
                            if back(HG * (G - 1), forward):
                                norm(G - 1, gp, 1)
                            if forward:
                                keep_v(G + 1, gn)
                            if back(HG * (G - 2), forward):
                                residual(G - 2, gq, b + (g - 2) // NG)
                        if j == 2 and forward:
                            turn_heads(G + 2, gq, 0)
                    if not forward:
                        residual(G - 1, gp, b - 1)
                        break

            op = dve.memset(probs[:, :, :, :], 0.0)
            op.then_inc(cleared, 1)
            turn_heads(0, 0, 0)
            turn_heads(0, 0, 1)
            keep_v(0, 0)
            turn_heads(1, 1, 0)
            turn_heads(1, 1, 1)
            wait(dve, cleared, 1)
            maxima(0, 0)
            body(0)
            with dve.Fori(1, B) as b:
                body(b)
            body(B, forward=False)

        @block.gpsimd
        def _(pool):
            def scale_heads(G, g, t):
                step = 3 * (2 * G + t)
                wait(pool, ssq_done, 2 * G + t + 1)
                pool.sem_inc(pool_hold, 1)
                pool.tensor_scalar(ssq[:, t, :], ssq[:, t, :], 1e-24, None, ALU.max).then_inc(pool_step, 1)
                pool.wait_ge(pool_step, step + 1)
                pool.tensor_tensor(ssq[:, t, :], ssq[:, t, :], expo[:, :], ALU.pow).then_inc(pool_step, 1)
                wait(pool, proj_free, qk_fill(G, t) + 1)
                pool.tensor_tensor(qk[:, g % 2, t, :], qk[:, g % 2, t, :], qk_rot[:, t, :], ALU.add).then_inc(pool_step, 1)
                pool.wait_ge(pool_step, step + 3)
                view = qk[:, g % 2, t, :].rearrange("p (h d) -> p h d", d=HD)
                pool.tensor_tensor(view, view, ssq[:, t, :].unsqueeze(2).broadcast_to([P, 2 * HG, HD]), ALU.mult)\
                    .then_inc(qk_ready, 1)

            def body(b):
                for g in range(NG):
                    scale_heads(NG * b + g + 2, (g + 2) % NG, 0)
                    scale_heads(NG * b + g + 2, (g + 2) % NG, 1)

            if rope:
                for G in (0, 1):
                    scale_heads(G, G, 0)
                    scale_heads(G, G, 1)
                body(0)
                with pool.Fori(1, B) as b:
                    body(b)

        @block.sync
        def _(sp):
            for n, (dst, source) in enumerate(loads):
                sp.dma_start(dst, source).then_inc(loaded, 16)
            wait(sp, loaded, 16 * len(loads))
    ph.close()


def feed_forward(nc, name, res, w1, b1, w2, b2, gamma, beta, consts, loads):
    ph = Phase(nc, name)
    xn = ph.sb("xn", [P, 2, KD, CH])
    gate = ph.sb("gate", [P, 2, CH])
    hid = ph.sb("hid", [P, FT, CH])
    up_ps = ph.psum("up_ps", [P, 2, 2, CH])
    down_ps = ph.psum("down_ps", [P, KD, CH])
    norm = Norm(ph, consts, res, lambda c, k: xn[:, c % 2, k, :].rearrange("p (b t) -> p b t", t=S), True, gamma, beta, 1)
    up_full, gate_ready, hid_ready = ph.sem("up_full"), ph.sem("gate_ready"), ph.sem("hid_ready")
    down_full, res_done, loaded = ph.sem("down_full"), ph.sem("res_done"), ph.sem("loaded")
    width = [min(P, FF - m * P) for m in range(FT)]

    with nc.Block() as block:
        @block.tensor
        def _(pe):
            def up(c, m):
                wait(pe, norm.done, c + 1)
                wait(pe, hid_ready, FT * c + m - 1)
                for part in (0, 1):
                    for k in range(KD):
                        mm = pe.matmul(up_ps[0:width[m], m % 2, part, :],
                                       w1[:, k, part * FF + m * P:part * FF + m * P + width[m]],
                                       xn[:, c % 2, k, :], start=(k == 0), stop=(k == KD - 1))
                mm.then_inc(up_full, 1)

            def down(c, m):
                wait(pe, hid_ready, FT * c + m + 1)
                if m == 0:
                    wait(pe, res_done, c)
                for n in range(KD):
                    mm = pe.matmul(down_ps[:, n, :], w2[0:width[m], m, n * P:(n + 1) * P], hid[0:width[m], m, :],
                                   start=(m == 0), stop=(m == FT - 1))
                if m == FT - 1:
                    mm.then_inc(down_full, 1)

            norm.mean(pe, 0)
            norm.variance(pe, 0)
            norm.spread(pe, 0)
            for c in range(NCH):
                for m in range(FT + 2):
                    if m < FT:
                        up(c, m)
                    if c + 1 < NCH:
                        if m == 0:
                            norm.mean(pe, c + 1)
                        if m == 2:
                            norm.variance(pe, c + 1)
                        if m == 4:
                            norm.spread(pe, c + 1)
                    if m >= 2:
                        down(c, m - 2)

        @block.scalar
        def _(act):
            norm.square(act, 0)
            norm.affine(act, 0)
            for c in range(NCH):
                for m in range(FT):
                    wait(act, up_full, FT * c + m + 1)
                    wait(act, hid_ready, FT * c + m - 1)
                    act.activation(gate[0:width[m], m % 2, :], up_ps[0:width[m], m % 2, 1, :], ACT.Gelu,
                                   bias=b1[0:width[m], FT + m:FT + m + 1]).then_inc(gate_ready, 1)
                    if c + 1 < NCH and m == 0:
                        norm.square(act, c + 1)
                    if c + 1 < NCH and m == FT - 1:
                        norm.affine(act, c + 1)

        @block.gpsimd
        def _(pool):
            for c in range(NCH):
                norm.power(pool, c)

        @block.vector
        def _(dve):
            norm.centre(dve, 0)
            norm.keep_variance(dve, 0)
            norm.diagonal(dve, 0)
            norm.scale(dve, 0)
            for c in range(NCH):
                for m in range(FT):
                    wait(dve, gate_ready, FT * c + m + 1)
                    if m == 0:
                        wait(dve, down_full, c)
                    w = width[m]
                    dve.scalar_tensor_tensor(hid[0:w, m, :], up_ps[0:w, m % 2, 0, :], b1[0:w, m:m + 1],
                                             gate[0:w, m % 2, :], ALU.add, ALU.mult).then_inc(hid_ready, 1)
                    if c + 1 < NCH:
                        if m == 0:
                            norm.centre(dve, c + 1)
                        if m == 2:
                            norm.keep_variance(dve, c + 1)
                            norm.diagonal(dve, c + 1)
                        if m == 4:
                            norm.scale(dve, c + 1)
                wait(dve, down_full, c + 1)
                for n in range(KD):
                    r = tokens(res, n, 2 * c, 2)
                    op = dve.scalar_tensor_tensor(r, down_ps[:, n, :].rearrange("p (b t) -> p b t", t=S),
                                                  b2[:, n:n + 1], r, ALU.add, ALU.add)
                op.then_inc(res_done, 1)

        @block.sync
        def _(sp):
            for dst, source in loads:
                sp.dma_start(dst, source).then_inc(loaded, 16)
            wait(sp, loaded, 16 * len(loads))
    ph.close()


def token_features(nc, consts, dram, emb, pca, proj, proj_b, fus, fus_b, dst, loads):
    ph = Phase(nc, "tok")
    ids = ph.sb("ids", [V, B * S], I32)
    one_hot = ph.sb("one_hot", [V, B * S])
    mask_i = ph.sb("mask_i", [PCA, B * S], I32)
    mask = ph.sb("mask", [PCA, B, S + 2])
    length = ph.sb("length", [PCA, B, S])
    masked = ph.sb("masked", [PCA, B, S + 2])
    window = ph.sb("window", [PCA, B, S])
    comb = ph.sb("comb", [P, 2 * KD, CH])
    look_ps = ph.psum("look_ps", [P, KD + 1, CH])
    proj_ps = ph.psum("proj_ps", [P, KD, CH])
    fus_ps = ph.psum("fus_ps", [P, KD, CH])
    got_ids, loaded, zeroed, step = ph.sem("got_ids"), ph.sem("loaded"), ph.sem("zeroed"), ph.sem("step")
    looked, kept, windowed, projected = ph.sem("looked"), ph.sem("kept"), ph.sem("windowed"), ph.sem("projected")
    biased, fused, stored, added = ph.sem("biased"), ph.sem("fused"), ph.sem("stored"), ph.sem("added")
    chunk = lambda x, c: x[:, bass.ds(c * CH, CH)]

    with nc.Block() as block:
        @block.sync
        def _(sp):
            sp.dma_start(ids[:, :], dram["x"].unsqueeze(0).broadcast_to([V, B * S])).then_inc(got_ids, 16)
            sp.dma_start(mask_i[:, :], dram["mask"].unsqueeze(0).broadcast_to([PCA, B * S])).then_inc(got_ids, 16)
            for d, source in loads:
                sp.dma_start(d, source).then_inc(loaded, 16)
            wait(sp, loaded, 16 * len(loads))

        @block.vector
        def _(dve):
            dve.memset(mask[:, :, :], 0.0).then_inc(zeroed, 1)
            dve.memset(masked[:, :, :], 0.0).then_inc(zeroed, 1)
            dve.wait_ge(got_ids, 32)
            dve.wait_ge(zeroed, 2)
            dve.tensor_scalar(one_hot[:, :], ids[:, :], consts["iota"][0:V, :], None, ALU.is_equal).then_inc(step, 1)
            dve.tensor_copy(mask[:, :, 1:S + 1], mask_i[:, :].rearrange("p (b t) -> p b t", t=S)).then_inc(step, 1)
            dve.wait_ge(step, 2)
            dve.tensor_tensor(length[:, :, :], mask[:, :, 0:S], mask[:, :, 1:S + 1], ALU.add).then_inc(step, 1)
            dve.wait_ge(step, 3)
            dve.tensor_tensor(length[:, :, :], length[:, :, :], mask[:, :, 2:S + 2], ALU.add).then_inc(step, 1)
            dve.wait_ge(step, 4)
            dve.tensor_scalar(length[:, :, :], length[:, :, :], 1.0, None, ALU.max).then_inc(step, 1)
            dve.wait_ge(step, 5)
            dve.reciprocal(length[:, :, :], length[:, :, :]).then_inc(step, 1)
            dve.wait_ge(step, 6)
            with dve.Fori(0, B // 2) as c:
                two = lambda x, lo=0: x[:, bass.ds(c * 2, 2), lo:lo + S]
                dve.wait_ge(looked, c + 1)
                dve.tensor_tensor(two(masked, 1), look_ps[0:PCA, KD, :].rearrange("p (b t) -> p b t", t=S), two(mask, 1),
                                  ALU.mult).then_inc(added, 1)
                dve.wait_ge(added, 4 * c + 1)
                dve.tensor_tensor(two(window), two(masked, 0), two(masked, 1), ALU.add).then_inc(added, 1)
                dve.wait_ge(added, 4 * c + 2)
                dve.tensor_tensor(two(window), two(window), two(masked, 2), ALU.add).then_inc(added, 1)
                dve.wait_ge(added, 4 * c + 3)
                dve.tensor_tensor(two(window), two(window), two(length), ALU.mult).then_inc(added, 1)
                dve.wait_ge(added, 4 * c + 4)
                dve.sem_inc(windowed, 1)
                dve.wait_ge(fused, c + 1)
                for m in range(KD):
                    op = dve.tensor_scalar(tokens(dst, m, c * 2, 2), fus_ps[:, m, :].rearrange("p (b t) -> p b t", t=S),
                                           fus_b[:, m:m + 1], None, ALU.add)
                op.then_inc(stored, 1)

        @block.scalar
        def _(act):
            with act.Fori(0, B // 2) as c:
                act.wait_ge(looked, c + 1)
                act.activation(comb[:, 0:KD, :], look_ps[:, 0:KD, :], ACT.Copy).then_inc(kept, 1)
                act.wait_ge(projected, c + 1)
                for m in range(KD):
                    op = act.activation(comb[:, KD + m, :], proj_ps[:, m, :], ACT.Identity, bias=proj_b[:, m:m + 1])
                op.then_inc(biased, 1)

        @block.tensor
        def _(pe):
            def chunk_of(c):
                wait(pe, windowed, c)
                for m in range(KD):
                    pe.matmul(look_ps[:, m, :], emb[:, m * P:(m + 1) * P], chunk(one_hot, c), start=True, stop=True)
                pe.matmul(look_ps[:, KD, :], pca[:, :], chunk(one_hot, c), start=True, stop=True).then_inc(looked, 1)
                pe.wait_ge(windowed, c + 1)
                for m in range(KD):
                    mm = pe.matmul(proj_ps[:, m, :], proj[:, m * P:(m + 1) * P],
                                   window[:, bass.ds(c * 2, 2), :].rearrange("p b t -> p (b t)"), start=True, stop=True)
                mm.then_inc(projected, 1)
                pe.wait_ge(biased, c + 1)
                wait(pe, stored, c)
                for m in range(KD):
                    for k in range(2 * KD):
                        mm = pe.matmul(fus_ps[:, m, :], fus[:, k, m * P:(m + 1) * P], comb[:, k, :],
                                       start=(k == 0), stop=(k == 2 * KD - 1))
                mm.then_inc(fused, 1)

            pe.wait_ge(step, 1)
            chunk_of(0)
            with pe.Fori(1, B // 2) as c:
                chunk_of(c)
    ph.close()


def merge_lora(nc, w_in, w_out, a_in, b_in, a_out, b_out):
    ph = Phase(nc, "lora")
    RANK = 16
    ps = ph.psum("ps", [P, 8, 512])
    full, done = ph.sem("full"), ph.sem("done")
    NC = 3 * INNER // 512
    pieces = [(w_in[:, k, n * 512:(n + 1) * 512], a_in[:, n // 2, k * P:(k + 1) * P], b_in[:, n * 512:(n + 1) * 512])
              for k in range(KD) for n in range(NC)]
    pieces += [(w_out[:, k, :], a_out[:, k * P:(k + 1) * P], b_out[:, :]) for k in range(INNER // P)]

    with nc.Block() as block:
        @block.tensor
        def _(pe):
            for n, (w, a, b) in enumerate(pieces):
                wait(pe, done, n - 7)
                pe.matmul(ps[:, n % 8, 0:w.shape[1]], a, b, start=True, stop=True).then_inc(full, 1)

        @block.vector
        def _(dve):
            for n, (w, a, b) in enumerate(pieces):
                dve.wait_ge(full, n + 1)
                dve.scalar_tensor_tensor(w, ps[:, n % 8, 0:w.shape[1]], 1.0 / RANK, w, ALU.mult, ALU.add).then_inc(done, 1)
    ph.close()


class Quantiser:

    STEPS = 14

    def __init__(self, ph, rows, n):
        self.step = ph.sem("quant_step")
        self.mag = ph.sb("mag", [P, rows, n])
        self.sign = ph.sb("sign", [P, rows, n])
        self.level = ph.sb("level", [P, rows, n])
        self.scale = ph.sb("scale", [P, rows * n // BLK])
        self.inverse = ph.sb("inverse", [P, rows * n // BLK])

    def __call__(self, dve, out, mag, sign, level, before):
        n = mag.shape[1]
        sc, inv = self.scale[:, 0:n // BLK], self.inverse[:, 0:n // BLK]
        blocks = lambda x: x.rearrange("p (b e) -> p b e", e=BLK)
        spread = lambda x: x.unsqueeze(2).broadcast_to([P, n // BLK, BLK])
        made = 0

        def then(op):
            nonlocal made
            made += 1
            op.then_inc(self.step, 1)
            dve.wait_ge(self.step, before + made)

        then(dve.tensor_reduce(sc, blocks(mag), AX.X, ALU.max))
        then(dve.tensor_scalar(sc, sc, 1.0 / 6.0, 1e-12, ALU.mult, ALU.max))
        then(dve.reciprocal(inv, sc))
        then(dve.tensor_tensor(blocks(mag), blocks(mag), spread(inv), ALU.mult))
        then(dve.tensor_scalar(level, mag, 5.0, 2.0, ALU.is_gt, ALU.mult))
        then(dve.scalar_tensor_tensor(level, mag, 3.5, level, ALU.is_gt, ALU.add))
        then(dve.scalar_tensor_tensor(level, mag, 2.5, level, ALU.is_gt, ALU.add))
        then(dve.tensor_scalar(level, level, 2.0, None, ALU.mult))
        for threshold in (1.75, 1.25, 0.75, 0.25):
            then(dve.scalar_tensor_tensor(level, mag, threshold, level, ALU.is_gt, ALU.add))
        then(dve.scalar_tensor_tensor(level, level, 0.5, sign, ALU.mult, ALU.mult))
        then(dve.tensor_tensor(blocks(out), blocks(level), spread(sc), ALU.mult))
        assert made == self.STEPS


def quantise_weights(nc, gate_t, up_t, down_t, dram, ident, loads):
    ph = Phase(nc, "qw")
    raw = ph.sb("raw", [P, 3, 6 * D])
    q = Quantiser(ph, 1, 6 * D)
    turn_ps = ph.psum("turn_ps", [P, 2, 512])
    got, abs_ready, sign_ready, ready = ph.sem("got"), ph.sem("abs_ready"), ph.sem("sign_ready"), ph.sem("ready")
    turned, kept, loaded, zeroed = ph.sem("turned"), ph.sem("kept"), ph.sem("loaded"), ph.sem("zeroed")
    full = QF // P
    rest = QF - full * P
    n_of = (6 * D, 6 * D, KD * QF)

    def turns(i):
        if i < 2:
            dst = (gate_t, up_t)[i]
            for t in range(QFT):
                w = P if t < full else rest
                for k in range(KD):
                    yield dst[:, k, t * P:t * P + w], raw[0:w, i, t * D + k * P:t * D + (k + 1) * P], w
        else:
            for m in range(KD):
                for t in range(QFT):
                    w = P if t < full else rest
                    yield down_t[0:w, t, m * P:(m + 1) * P], raw[:, 2, m * QF + t * P:m * QF + t * P + w], w

    with nc.Block() as block:
        @block.sync
        def _(sp):
            sp.wait_ge(zeroed, 1)
            for i, name in enumerate(("w_gate", "w_up")):
                sp.dma_start(raw[:, i, 0:full * D].rearrange("p (t d) -> p t d", d=D),
                             dram[name][0:full * P, :].rearrange("(t p) d -> p t d", p=P)).then_inc(got, 16)
                sp.dma_start(raw[0:rest, i, full * D:QFT * D], dram[name][full * P:QF, :]).then_inc(got, 16)
            sp.dma_start(raw[:, 2, 0:KD * QF].rearrange("p (m n) -> p m n", n=QF),
                         dram["w_down"].rearrange("(m p) n -> p m n", p=P)).then_inc(got, 16)
            for d, source in loads:
                sp.dma_start(d, source).then_inc(loaded, 16)
            wait(sp, loaded, 16 * len(loads))

        @block.scalar
        def _(act):
            act.wait_ge(got, 5 * 16)
            for i in range(3):
                n = n_of[i]
                wait(act, ready, i)
                act.activation(q.mag[:, 0, 0:n], raw[:, i, 0:n], ACT.Abs).then_inc(abs_ready, 1)
                act.activation(q.sign[:, 0, 0:n], raw[:, i, 0:n], ACT.Sign).then_inc(sign_ready, 1)

        @block.vector
        def _(dve):
            dve.memset(raw[:, 0:2, full * D:QFT * D], 0.0).then_inc(zeroed, 1)
            for i in range(3):
                n = n_of[i]
                dve.wait_ge(abs_ready, i + 1)
                dve.wait_ge(sign_ready, i + 1)
                q(dve, raw[:, i, 0:n], q.mag[:, 0, 0:n], q.sign[:, 0, 0:n], q.level[:, 0, 0:n], q.STEPS * i)
                dve.sem_inc(ready, 1)
                f = sum(len(list(turns(a))) for a in range(i))
                for n_, (dst, tile, w) in enumerate(turns(i)):
                    dve.wait_ge(turned, f + n_ + 1)
                    dve.tensor_copy(dst, turn_ps[0:dst.shape[0], (f + n_) % 2, 0:dst.shape[1]]).then_inc(kept, 1)

        @block.tensor
        def _(pe):
            f = 0
            for i in range(3):
                pe.wait_ge(ready, i + 1)
                for dst, tile, w in turns(i):
                    wait(pe, kept, f - 1)
                    rows = tile.shape[0]
                    pe.transpose(turn_ps[0:tile.shape[1], f % 2, 0:rows], tile, ident[0:rows, 0:rows]).then_inc(turned, 1)
                    f += 1
    ph.close()


def quantised_feed_forward(nc, src, res, gate_t, up_t, down_t, ident, loads):
    ph = Phase(nc, "qff")
    HF = QF // 2
    xs = ph.sb("xs", [P, 2, KD, P])
    qx = Quantiser(ph, 1, QF)
    xq = ph.sb("xq", [P, D])
    xq_t = ph.sb("xq_t", [P, KD, P])
    silu = ph.sb("silu", [P, 2, HF])
    hid = ph.sb("hid", [P, QF])
    hq = ph.sb("hq", [P, QF])
    hq_t = ph.sb("hq_t", [P, QFT, P])
    mag_x, sign_x, level_x = ph.sb("mag_x", [P, D]), ph.sb("sign_x", [P, D]), ph.sb("level_x", [P, D])
    gu_ps = ph.psum("gu_ps", [P, 4, 512])
    x_ps = ph.psum("x_ps", [P, 512])
    h_ps = ph.psum("h_ps", [P, 2, 512])
    y_ps = ph.psum("y_ps", [P, KD, P])
    staged, x_turned, x_abs, x_sign, x_quant = (ph.sem(n) for n in ("staged", "x_turned", "x_abs", "x_sign", "x_quant"))
    xq_turned, xq_kept, gu_ready, silu_ready = (ph.sem(n) for n in ("xq_turned", "xq_kept", "gu_ready", "silu_ready"))
    h_ready, h_abs, h_sign, h_quant, hq_turned = (ph.sem(n) for n in ("h_ready", "h_abs", "h_sign", "h_quant", "hq_turned"))
    x_hold = ph.sem("x_hold")
    hq_kept, y_ready, added, loaded = (ph.sem(n) for n in ("hq_kept", "y_ready", "added", "loaded"))
    widths = [min(P, QF - t * P) for t in range(QFT)]
    PER = 2 * Quantiser.STEPS

    with nc.Block() as block:
        @block.sync
        def _(sp):
            for d, source in loads:
                sp.dma_start(d, source).then_inc(loaded, 16)
            wait(sp, loaded, 16 * len(loads))

        @block.gpsimd
        def _(pool):
            def stage(b):
                wait(pool, x_turned, 2 * b)
                for t in range(2):
                    for k in range(KD):
                        op = pool.tensor_copy(xs[:, t, k, :], tokens(src, k, b)[:, :, t * P:(t + 1) * P].rearrange("p a t -> p (a t)"))
                op.then_inc(staged, 1)
            stage(0)
            with pool.Fori(1, SLOTS) as b:
                stage(b)

        @block.tensor
        def _(pe):
            def turn_x(n, t, b):
                wait(pe, staged, b + 1)
                wait(pe, xq_kept, n - 1)
                for k in range(KD):
                    mm = pe.transpose(x_ps[:, k * P:(k + 1) * P], xs[:, t, k, :], ident[:, :])
                mm.then_inc(x_turned, 1)

            def turn_xq(n):
                wait(pe, x_quant, n + 1)
                for k in range(KD):
                    mm = pe.transpose(x_ps[:, D + k * P:D + (k + 1) * P], xq[:, k * P:(k + 1) * P], ident[:, :])
                mm.then_inc(xq_turned, 1)

            def gate_up(n):
                wait(pe, xq_kept, n + 1)
                wait(pe, h_ready, n)
                for i, w in enumerate((gate_t, up_t)):
                    for half in range(2):
                        for k in range(KD):
                            mm = pe.matmul(gu_ps[:, 2 * i + half, 0:HF], xq_t[:, k, :], w[:, k, half * HF:(half + 1) * HF],
                                           start=(k == 0), stop=(k == KD - 1))
                mm.then_inc(gu_ready, 1)

            def down(n):
                wait(pe, h_quant, n + 1)
                wait(pe, hq_kept, n)
                for t in range(QFT):
                    w = widths[t]
                    mm = pe.transpose(h_ps[0:w, t // 4, (t % 4) * P:(t % 4 + 1) * P], hq[:, t * P:t * P + w], ident[:, :])
                mm.then_inc(hq_turned, 1)
                wait(pe, hq_kept, n + 1)
                wait(pe, added, n)
                for m in range(KD):
                    for t in range(QFT):
                        w = widths[t]
                        mm = pe.matmul(y_ps[:, m, :], down_t[0:w, t, m * P:(m + 1) * P], hq_t[0:w, t, :],
                                       start=(t == 0), stop=(t == QFT - 1))
                mm.then_inc(y_ready, 1)

            def tile(n, t, b):
                turn_xq(n + 1)
                gate_up(n + 1)
                turn_x(n + 2, t, b + 1)
                down(n)

            turn_x(0, 0, 0)
            turn_xq(0)
            gate_up(0)
            turn_x(1, 1, 0)
            tile(0, 0, 0)
            tile(1, 1, 0)
            with pe.Fori(1, B) as b:
                tile(2 * b, 0, b)
                tile(2 * b + 1, 1, b)

        @block.scalar
        def _(act):
            def split_x(n):
                wait(act, x_turned, n + 1)
                wait(act, x_quant, n)
                act.activation(mag_x[:, :], x_ps[:, 0:D], ACT.Abs).then_inc(x_abs, 1)
                act.activation(sign_x[:, :], x_ps[:, 0:D], ACT.Sign).then_inc(x_sign, 1)

            def keep_xq(n):
                wait(act, xq_turned, n + 1)
                wait(act, gu_ready, n)
                act.activation(xq_t[:, :, :].rearrange("p k t -> p (k t)"), x_ps[:, D:2 * D], ACT.Copy).then_inc(xq_kept, 1)

            def gate(n):
                wait(act, gu_ready, n + 1)
                wait(act, h_ready, n)
                act.activation(silu[:, :, :], gu_ps[:, 0:2, 0:HF], ACT.Silu).then_inc(silu_ready, 1)

            def keep_hq(n):
                wait(act, hq_turned, n + 1)
                wait(act, y_ready, n)
                act.activation(hq_t[:, 0:4, :].rearrange("p t n -> p (t n)"), h_ps[:, 0, :], ACT.Copy)
                act.activation(hq_t[:, 4, :], h_ps[:, 1, 0:P], ACT.Copy)
                act.activation(hq_t[0:widths[5], 5, :], h_ps[0:widths[5], 1, P:2 * P], ACT.Copy).then_inc(hq_kept, 1)

            def split_h(n):
                wait(act, h_ready, n + 1)
                wait(act, h_quant, n)
                act.activation(qx.mag[:, 0, :], hid[:, :], ACT.Abs).then_inc(h_abs, 1)
                act.activation(qx.sign[:, 0, :], hid[:, :], ACT.Sign).then_inc(h_sign, 1)

            def tile(n):
                split_h(n)
                keep_xq(n + 1)
                gate(n + 1)
                split_x(n + 2)
                keep_hq(n)

            split_x(0)
            keep_xq(0)
            gate(0)
            split_x(1)
            tile(0)
            with act.Fori(1, 2 * B) as n:
                tile(n)

        @block.vector
        def _(dve):
            def x_steps(n):
                return 0 if isinstance(n, int) and n == 0 else PER * n - Quantiser.STEPS

            def quantise_x(n):
                wait(dve, x_abs, n + 1)
                wait(dve, x_sign, n + 1)
                wait(dve, xq_turned, n)
                dve.sem_inc(x_hold, 1)
                qx(dve, xq[:, :], mag_x[:, :], sign_x[:, :], level_x[:, :], x_steps(n))
                dve.sem_inc(x_quant, 1)

            def multiply(n):
                wait(dve, silu_ready, n + 1)
                wait(dve, h_abs, n)
                wait(dve, h_sign, n)
                dve.tensor_tensor(hid[:, :].rearrange("p (a f) -> p a f", a=2), silu[:, :, :], gu_ps[:, 2:4, 0:HF], ALU.mult)\
                    .then_inc(h_ready, 1)

            def quantise_h(n):
                wait(dve, h_abs, n + 1)
                wait(dve, h_sign, n + 1)
                wait(dve, hq_turned, n)
                dve.sem_inc(x_hold, 1)
                qx(dve, hq[:, :], qx.mag[:, 0, :], qx.sign[:, 0, :], qx.level[:, 0, :], PER * n + PER)
                dve.sem_inc(h_quant, 1)

            def add(n, t, b):
                wait(dve, y_ready, n + 1)
                for m in range(KD):
                    r = tokens(res, m, b)[:, :, t * P:(t + 1) * P].rearrange("p a t -> p (a t)")
                    op = dve.tensor_tensor(r, r, y_ps[:, m, :], ALU.add)
                op.then_inc(added, 1)

            def tile(n, t, b, first=False):
                multiply(n)
                quantise_x(n + 1)
                quantise_h(n)
                if not first:
                    add(n - 1, 1 - t, b - (1 - t))

            quantise_x(0)
            tile(0, 0, 0, first=True)
            tile(1, 1, 0)
            with dve.Fori(1, B) as b:
                tile(2 * b, 0, b)
                tile(2 * b + 1, 1, b)
            add(2 * B - 1, 1, B - 1)
    ph.close()


def program(nc, dram, out):
    whole = ExitStack()

    def sb(name, shape, dt=F32):
        return whole.enter_context(nc.sbuf_tensor(name, shape, dt))

    h = sb("h", [P, KD, SLOTS * PAD])
    xr = sb("xr", [P, KD, SLOTS * PAD])
    xn = sb("xn", [P, KD, SLOTS * PAD])
    w_in = sb("w_in", [P, KD, 3 * INNER])
    w_out = sb("w_out", [P, INNER // P, D])
    ident, ones = sb("ident", [P, P]), sb("ones", [P, P])
    full, iota = sb("full", [P, P]), sb("iota", [P, 1])
    expo, no_bias = sb("expo", [P, 2 * HG]), sb("no_bias", [P, KD])
    consts = {"ident": ident, "ones": ones, "full": full, "expo": expo, "iota": iota}
    tok_g, tok_b = sb("tok_g", [P, KD]), sb("tok_b", [P, KD])
    mask = sb("mask", [P, QT, S])
    rows = lambda w: w.rearrange("(k p) n -> p k n", p=P)

    start = Phase(nc, "start")
    s = start.stack
    emb, pca = start.sb("emb", [V, D]), start.sb("pca", [V, P])
    proj, fus = start.sb("proj", [PCA, D]), start.sb("fus", [P, 2 * KD, D])
    proj_b, fus_b = start.sb("proj_b", [P, KD]), start.sb("fus_b", [P, KD])
    a_in, b_in = start.sb("a_in", [16, 3, D]), start.sb("b_in", [16, 3 * INNER])
    a_out, b_out = start.sb("a_out", [16, INNER]), start.sb("b_out", [16, D])
    loaded, pca_zeroed = start.sem("loaded"), start.sem("pca_zeroed")
    first = [(ident[:, :], dram["ident"]), (ones[:, :], dram["ones"]), (iota[:, :], dram["iota"]),
             (emb[:, :], dram["emb"]), (pca[:, 0:PCA], dram["pca"]), (proj[:, :], dram["proj_w"]),
             (fus[:, :, :], rows(dram["fus_w"])), (proj_b[:, :], dram["proj_b"]),
             (fus_b[:, :], dram["fus_b"]), (tok_g[:, :], dram["tok_g"]),
             (tok_b[:, :], dram["tok_b"])]
    with nc.Block() as block:
        @block.sync
        def _(sp):
            sp.wait_ge(pca_zeroed, 1)
            for dst, source in first:
                sp.dma_start(dst, source).then_inc(loaded, 16)
            sp.wait_ge(loaded, 16 * len(first))

        @block.vector
        def _(dve):
            dve.memset(pca[:, :], 0.0).then_inc(pca_zeroed, 1)
            dve.memset(full[:, :], 1.0)
            dve.memset(expo[:, :], -0.5)
            dve.memset(no_bias[:, :], 0.0)
            for x in (h, xr, xn):
                dve.memset(x[:, :, :], 0.0)
    token_features(nc, consts, dram, emb, pca, proj, proj_b, fus, fus_b, xn,
                   [(w_in[:, :, :], rows(dram["l0_w_in"])), (w_out[:, :, :], rows(dram["l0_w_out"])),
                    (a_in[:, :, :], dram["l0_a_in"]), (b_in[:, :], dram["l0_b_in"]),
                    (a_out[:, :], dram["l0_a_out"]), (b_out[:, :], dram["l0_b_out"]),
                    (mask[:, :, :], dram["causal"])])
    layer_norm(nc, "tok_norm", xn, h, consts, gamma=tok_g, beta=tok_b)

    merge_lora(nc, w_in, w_out, a_in, b_in, a_out, b_out)
    start.close()
    layer_norm(nc, "norm0", h, xn, consts)
    bias = Phase(nc, "bias")
    bias_in, bias_out = bias.sb("in", [P, 3 * INNER]), bias.sb("out", [P, KD])
    with nc.Block() as block:
        @block.vector
        def _(dve):
            dve.memset(bias_in[:, :], 0.0)
    attention(nc, "attn0", "plain", xn, h, w_in, w_out, ident, mask, L0_HD ** -0.5, [(0, P), (0, S)],
              bias_in, no_bias, None, None, None, [])

    layer_norm(nc, "norm1", h, xn, consts)
    quant = Phase(nc, "quant")
    gate_t, up_t = quant.sb("gate_t", [P, KD, QF]), quant.sb("up_t", [P, KD, QF])
    down_t = quant.sb("down_t", [P, QFT, D])
    quantise_weights(nc, gate_t, up_t, down_t, dram, ident,
                     [(w_in[:, :, :], rows(dram["l1_w_in"])), (w_out[:, :, :], rows(dram["l1_w_out"]))])
    quantised_feed_forward(nc, xn, h, gate_t, up_t, down_t, ident,
                           [(bias_in[:, :], dram["l1_b_in"].unsqueeze(0).broadcast_to([P, 3 * INNER])),
                            (bias_out[:, :], dram["l1_b_out"]), (mask[:, :, :], dram["open"]),
                            (tok_g[:, :], dram["l1_g"]), (tok_b[:, :], dram["l1_b"])])
    quant.close()

    layer_norm(nc, "norm2", h, xr, consts)
    layer_norm(nc, "norm3", xr, xn, consts, gamma=tok_g, beta=tok_b)
    attention(nc, "attn1", "plain", xn, h, w_in, w_out, ident, mask, HD ** -0.5, [(0, S), (0, S)],
              bias_in, bias_out, None, None, None, [])
    bias.close()
    layer_norm(nc, "norm4", h, xr, consts)

    w1, w2 = sb("w1", [P, KD, 2 * FF]), sb("w2", [P, FT, D])
    b1, b2 = sb("b1", [P, 2 * FT]), sb("b2", [P, KD])
    ln_g, ln_b = sb("ln_g", [P, KD]), sb("ln_b", [P, KD])
    cos_base, sin_base = sb("cos_base", [P, QT, 2, HD]), sb("sin_base", [P, QT, 2, HD])
    cos, sin = sb("cos", [P, QT, 2, HD]), sb("sin", [P, QT, 2, HD])
    head_scale, head_scale_swapped = sb("head_scale", [P, 2, HD]), sb("head_scale_swapped", [P, 2, HD])

    def layer_of(name, l):
        v = dram[name][bass.ds(l, 1)]
        return v.rearrange("a b -> (a b)") if len(v.shape) == 2 else v.rearrange("a b c -> (a b) c")

    def attention_loads(l):
        half = HD // 2
        loads = [(w_in[:, :, :], rows(layer_of("Wqkv", l))), (w_out[:, :, :], rows(layer_of("Wo", l)))]
        for i, name in enumerate(("q_scale", "k_scale")):
            v = layer_of(name, l)
            loads.append((head_scale[:, i, :], v.unsqueeze(0).broadcast_to([P, HD])))
            for lo in (0, half):
                loads.append((head_scale_swapped[:, i, lo:lo + half],
                              v[half - lo:HD - lo].unsqueeze(0).broadcast_to([P, half])))
        return loads

    def feed_forward_loads(l):
        w1_l, w2_l = layer_of("W1", l), layer_of("W2", l)
        whole_rows = (FT - 1) * P
        rest = FF - whole_rows
        loads = [(w1[:, :, :], rows(w1_l)), (w2[:, 0:FT - 1, :], rows(w2_l[0:whole_rows, :])),
                 (w2[0:rest, FT - 1, :], w2_l[whole_rows:FF, :])]
        for dst, name in ((b1, "b1"), (b2, "b2"), (ln_g, "ln_g"), (ln_b, "ln_b")):
            loads.append((dst[:, :], layer_of(name, l)))
        return loads

    pre = Phase(nc, "pre")
    pre_loaded = pre.sem("loaded")
    pre_loads = [(cos_base[:, :, :, :], dram["cos"]), (sin_base[:, :, :, :], dram["sin"]), (mask[:, :, :], dram["local"])]
    pre_loads += attention_loads(0)
    with nc.Block() as block:
        @block.sync
        def _(sp):
            for dst, source in pre_loads:
                sp.dma_start(dst, source).then_inc(pre_loaded, 16)
            sp.wait_ge(pre_loaded, 16 * len(pre_loads))
    pre.close()

    with nc.Fori(0, DEPTH) as l:
        with nc.Block() as block:
            @block.vector
            def _(dve):
                for t in range(QT):
                    dve.tensor_tensor(cos[:, t, :, :], cos_base[:, t, :, :], head_scale[:, :, :], ALU.mult)
                    dve.tensor_tensor(sin[:, t, :, :], sin_base[:, t, :, :], head_scale_swapped[:, :, :], ALU.mult)
        attention(nc, "local", "rope", xr, xr, w_in, w_out, ident, mask, 8.0, [(0, P), (WINDOW, S)],
                  None, no_bias, cos, sin, expo, feed_forward_loads(l))
        feed_forward(nc, "ff", xr, w1, b1, w2, b2, ln_g, ln_b, consts, attention_loads((l + 1) % DEPTH))

    end = Phase(nc, "end")
    summed, stored = end.sem("summed"), end.sem("stored")
    with nc.Block() as block:
        @block.vector
        def _(dve):
            for k in range(KD):
                dve.tensor_tensor(tokens(xn, k, 0, B), tokens(h, k, 0, B), tokens(xr, k, 0, B), ALU.add).then_inc(summed, 1)

        @block.sync
        def _(sp):
            for k in range(KD):
                sp.wait_ge(summed, k + 1)
                sp.dma_start(out[k * P:(k + 1) * P, :].rearrange("p (b t) -> p b t", t=S), tokens(xn, k, 0, B)).then_inc(stored, 16)
            sp.wait_ge(stored, 16 * KD)
    end.close()
    whole.close()


def constants():
    i, j = np.arange(S)[:, None], np.arange(S)[None, :]
    tiled = lambda x: np.ascontiguousarray(x.reshape(QT, P, *x.shape[1:]).swapaxes(0, 1), dtype=np.float32)
    additive = lambda allowed: tiled(np.where(allowed, 0.0, LOW))
    half = np.arange(0, HD, 2, dtype=np.float32)
    inv_freq = (1.0 / 10000.0 ** (half / HD)).astype(np.float32)
    t = np.arange(S, dtype=np.float32)
    freqs = (t[:, None] * inv_freq[None, :]).astype(np.float32)
    freqs = np.concatenate([freqs, freqs], -1)
    base = ((half + 0.4 * HD) / (1.4 * HD)).astype(np.float32)
    power = (t - S // 2) / (WINDOW // 2)
    scale = (base[None, :] ** power[:, None]).astype(np.float32)
    scale = np.concatenate([scale, scale], -1)
    sign = np.where(np.arange(HD) < HD // 2, -1.0, 1.0)
    cos = np.stack([np.cos(freqs) * scale, np.cos(freqs) / scale], 1)
    sin = np.stack([np.sin(freqs) * scale * sign, np.sin(freqs) / scale * sign], 1)
    return {
        "ident": np.eye(P, dtype=np.float32), "ones": np.full((P, P), 1.0 / D, np.float32),
        "iota": np.arange(P, dtype=np.float32)[:, None],
        "causal": additive(j <= i), "open": additive(i + j >= 0), "local": additive((j <= i) & (j >= i - WINDOW)),
        "cos": tiled(cos), "sin": tiled(sin),
    }


def laid_out(x):
    def spread(w):
        o = np.zeros((*w.shape[:-1], H, HD), w.dtype)
        o[..., :L0_HD] = w.reshape(*w.shape[:-1], H, L0_HD)
        return o.reshape(*w.shape[:-1], INNER)

    def by_partition(v):
        n = -(-v.shape[-1] // P)
        o = np.zeros((*v.shape[:-1], n * P), v.dtype)
        o[..., :v.shape[-1]] = v
        return o.reshape(*v.shape[:-1], n, P).swapaxes(-1, -2)

    a = {
        "x": x["x"].reshape(-1), "mask": x["mask_BS_i1_0"].reshape(-1),
        "emb": x["L0_tok_emb"], "pca": x["L0_tok_pca_lookup"], "proj_w": x["L0_tok_proj_w"], "fus_w": x["L0_tok_fus_w"],
        "proj_b": by_partition(x["L0_tok_proj_b"]), "fus_b": by_partition(x["L0_tok_fus_b"]), "tok_g": by_partition(x["L0_tok_ln_g"]), "tok_b": by_partition(x["L0_tok_ln_b"]),
        "l0_w_in": np.concatenate([spread(x[f"L0_attn_w{c}"].T) for c in "qkv"], 1),
        "l0_w_out": spread(x["L0_attn_wo"]).T,
        "l0_a_in": np.stack([x[f"L0_attn_a{c}"] for c in "qkv"], 1),
        "l0_b_in": np.concatenate([spread(x[f"L0_attn_b{c}"].T) for c in "qkv"], 1),
        "l0_a_out": spread(x["L0_attn_ao"]), "l0_b_out": x["L0_attn_bo"].T,
        "w_gate": x["L0_ffn_w_gate"], "w_up": x["L0_ffn_w_up"], "w_down": x["L0_ffn_w_down"],
        "l1_w_in": x["L1_attn_w_qkv"], "l1_w_out": x["L1_attn_w_out"], "l1_b_in": x["L1_attn_b_qkv"],
        "l1_b_out": by_partition(x["L1_attn_b_out"]), "l1_g": by_partition(x["L1_attn_ln_gamma"]), "l1_b": by_partition(x["L1_attn_ln_beta"]),
    }
    for n in ("Wqkv", "q_scale", "k_scale", "Wo", "W1", "W2"):
        a[n] = x[f"L1_ffn_{n}"]
    for n in ("ln_g", "ln_b", "b2"):
        a[n] = by_partition(x[f"L1_ffn_{n}"])
    b1 = x["L1_ffn_b1"]
    a["b1"] = np.concatenate([by_partition(b1[:, :FF]), by_partition(b1[:, FF:])], -1)
    return a


def build(nc, arrays):
    dram = {n: nc.dram_tensor(f"in_{n}", a.shape, mybir.dt.from_np(a.dtype), kind="ExternalInput").ap()
            for n, a in arrays.items()}
    out = nc.dram_tensor("out_0", (D, B * S), F32, kind="ExternalOutput").ap()
    program(nc, dram, out)


def kernel(**inputs):
    import concourse.bacc as bacc
    from concourse.bass_utils import run_bass_kernel_spmd

    arrays = {n: np.ascontiguousarray(a) for n, a in {**laid_out({k: np.asarray(v) for k, v in inputs.items()}), **constants()}.items()}
    nc = bacc.Bacc("TRN2", target_bir_lowering=False, num_devices=1)
    build(nc, arrays)
    r = run_bass_kernel_spmd(nc, [{f"in_{n}": a for n, a in arrays.items()}], core_ids=[0])
    return np.ascontiguousarray(r.results[0]["out_0"].reshape(D, B, S).transpose(1, 2, 0))
```

```python
from contextlib import ExitStack

import numpy as np
import concourse.bass as bass
from concourse import mybir

F32 = mybir.dt.float32
I32 = mybir.dt.int32
F32R = mybir.dt.float32r
ALU = mybir.AluOpType
ACT = mybir.ActivationFunctionType
AX = mybir.AxisListType

P = 128
B, S, D = 8, 256, 256
KD = D // P
PAD = S + 1
SLOTS = B + 1
H, HD = 16, 64
INNER = H * HD
HG = 4
NG = H // HG
GW = HG * HD
QT = S // P
DEPTH = 6
WINDOW = 64
V, PCA = 28, 20
FF = 682
FT = -(-FF // P)
QF = 704
QFT = -(-QF // P)
BLK = 16
LOW = -1e30
EPS = 1e-5
L0_HD = 16
IN_COLS = KD * 3 * INNER
ATT_COLS = IN_COLS + INNER // P * D
UP_COLS = KD * 2 * FT * P
FF_COLS = UP_COLS + FT * D


def wait(eng, sem, value):
    if isinstance(value, int) and value <= 0:
        return
    eng.wait_ge(sem, value)


class WeightStream:

    def __init__(self, ph, source, hi, lo, pieces, ring):
        self.source, self.hi, self.lo, self.ring = source, hi, lo, ring
        self.pieces, self.width = pieces, source.shape[-1] // pieces
        self.stage = ph.sb("stage", [P, ring, self.width])
        self.loaded = [ph.sem(f"piece_loaded{i}") for i in range(ring)]
        self.rounded, self.split = ph.sem("piece_rounded"), ph.sem("piece_split")

    def _at(self, n):
        return slice(n * self.width, (n + 1) * self.width) if isinstance(n, int) else bass.ds(n * self.width, self.width)

    def _slot(self, n):
        return 0 if self.ring == 1 else n % self.ring

    def load(self, sp, n):
        wait(sp, self.split, n + 1 - self.ring)
        sp.dma_start(self.stage[:, self._slot(n), :], self.source[:, self._at(n)]).then_inc(self.loaded[self._slot(n)], 16)

    def await_piece(self, eng, n):
        turns = n if self.ring == 1 else n // self.ring
        eng.wait_ge(self.loaded[self._slot(n)], 16 * turns + 16)

    def round(self, act, n, ready=None):
        if ready is None:
            self.await_piece(act, n)
        else:
            act.wait_ge(ready, n + 1)
        act.activation(self.hi[:, self._at(n)], self.stage[:, self._slot(n), :], ACT.Copy).then_inc(self.rounded, 1)

    def rest(self, eng, n):
        eng.wait_ge(self.rounded, n + 1)
        eng.tensor_tensor(self.lo[:, self._at(n)], self.stage[:, self._slot(n), :], self.hi[:, self._at(n)].bitcast(F32),
                          ALU.subtract).then_inc(self.split, 1)


def products(pe, out, lhs, rhs, first=True, last=True):
    for k, ((lhs_hi, lhs_lo), (rhs_hi, rhs_lo)) in enumerate(zip(lhs, rhs)):
        pe.matmul(out, lhs_hi, rhs_hi, start=(first and k == 0), stop=False)
        pe.matmul(out, lhs_hi, rhs_lo, start=False, stop=False)
        mm = pe.matmul(out, lhs_lo, rhs_hi, start=False, stop=(last and k == len(lhs) - 1))
    return mm


class Phase:

    def __init__(self, nc, name):
        self.nc, self.name, self.stack, self.sems = nc, name, ExitStack(), []

    def sb(self, name, shape, dt=F32):
        return self.stack.enter_context(self.nc.sbuf_tensor(f"{self.name}_{name}", shape, dt))

    def psum(self, name, shape, dt=F32):
        return self.stack.enter_context(self.nc.psum_tensor(f"{self.name}_{name}", shape, dt))

    def sem(self, name):
        s = self.stack.enter_context(self.nc.semaphore(f"{self.name}_{name}"))
        self.sems.append(s)
        return s

    def close(self):
        for s in self.sems:
            self.nc.sync.sem_clear(s)
        self.nc.all_engine_barrier()
        self.stack.close()


def tokens(x, k, b, n=1, shift=False):
    v = x[:, k, :].rearrange("p (b t) -> p b t", t=PAD)
    at = 0 if shift and k == 1 else 1
    return v[:, bass.ds(b, n), at:at + S]


CH = 2 * S
NCH = B * S // CH
TC = CH // P


class Norm:

    def __init__(self, ph, consts, src, dst, shift, gamma, beta, ring, skip=0, sq=None, diag=None, means=None, spreads=None):
        self.ring = ring
        self.skip = skip
        self.c, self.src, self.dst, self.shift, self.gamma, self.beta = consts, src, dst, shift, gamma, beta
        self.sq = ph.sb("norm_sq", [P, ring, KD, CH]) if sq is None else sq
        self.var = ph.sb("norm_var", [P, ring, TC])
        self.rstd = ph.sb("norm_rstd", [P, ring, TC])
        self.diag = ph.sb("norm_diag", [P, ring, CH]) if diag is None else diag
        self.mean_ps = ph.psum("norm_mean_ps", [P, ring, CH]) if means is None else means
        self.spread_ps = ph.psum("norm_spread_ps", [P, ring, CH]) if spreads is None else spreads
        (self.mean_ready, self.centred, self.squared, self.var_ready, self.var_kept, self.rstd_ready,
         self.diag_ready, self.spread_ready, self.scaled, self.normed) = (
            ph.sem("norm_" + n) for n in ("mean_ready", "centred", "squared", "var_ready", "var_kept",
                                          "rstd_ready", "diag_ready", "spread_ready", "scaled", "normed"))
        self.done = self.scaled if gamma is None else self.normed

    def mean(self, pe, c):
        wait(pe, self.centred, c + 1 - self.ring - self.skip)
        for k in range(KD):
            mm = pe.matmul(self.mean_ps[:, c % self.ring, :].rearrange("p (b t) -> p b t", t=S), self.c["ones"][:, :],
                           tokens(self.src, k, 2 * c, 2, self.shift), start=(k == 0), stop=(k == KD - 1))
        mm.then_inc(self.mean_ready, 1)

    def centre(self, dve, c):
        wait(dve, self.mean_ready, c + 1 - self.skip)
        for k in range(KD):
            op = dve.tensor_tensor(self.dst(c, k), tokens(self.src, k, 2 * c, 2, self.shift),
                                   self.mean_ps[:, c % self.ring, :].rearrange("p (b t) -> p b t", t=S), ALU.subtract)
        op.then_inc(self.centred, 1)

    def square(self, act, c):
        wait(act, self.centred, c + 1 - self.skip)
        wait(act, self.var_ready, c + 1 - self.ring - self.skip)
        for k in range(KD):
            op = act.activation(self.sq[:, c % self.ring, k, :].rearrange("p (b t) -> p b t", t=S), self.dst(c, k), ACT.Square)
        op.then_inc(self.squared, 1)

    def variance(self, pe, c):
        wait(pe, self.squared, c + 1 - self.skip)
        wait(pe, self.scaled, c + 1 - self.ring - self.skip)
        for t in range(TC):
            for k in range(KD):
                mm = pe.matmul(self.spread_ps[:, c % self.ring, t:t + 1], self.sq[:, c % self.ring, k, t * P:(t + 1) * P], self.c["ones"][:, 0:1],
                               start=(k == 0), stop=(k == KD - 1))
        mm.then_inc(self.var_ready, 1)

    def keep_variance(self, dve, c):
        wait(dve, self.var_ready, c + 1 - self.skip)
        wait(dve, self.rstd_ready, c + 1 - self.ring - self.skip)
        dve.tensor_scalar(self.var[:, c % self.ring, :], self.spread_ps[:, c % self.ring, 0:TC], EPS, None, ALU.add).then_inc(self.var_kept, 1)

    def power(self, pool, c):
        wait(pool, self.var_kept, c + 1 - self.skip)
        wait(pool, self.diag_ready, c + 1 - self.ring - self.skip)
        pool.tensor_tensor(self.rstd[:, c % self.ring, :], self.var[:, c % self.ring, :], self.c["expo"][:, 0:TC], ALU.pow).then_inc(self.rstd_ready, 1)

    def diagonal(self, dve, c):
        wait(dve, self.rstd_ready, c + 1 - self.skip)
        wait(dve, self.spread_ready, c + 1 - self.ring - self.skip)
        for t in range(TC):
            op = dve.tensor_scalar(self.diag[:, c % self.ring, t * P:(t + 1) * P], self.c["ident"][:, :], self.rstd[:, c % self.ring, t:t + 1], None, ALU.mult)
        op.then_inc(self.diag_ready, 1)

    def spread(self, pe, c):
        wait(pe, self.diag_ready, c + 1 - self.skip)
        pe.matmul(self.spread_ps[:, c % self.ring, :], self.c["full"][:, :], self.diag[:, c % self.ring, :], start=True, stop=True).then_inc(self.spread_ready, 1)

    def scale(self, dve, c):
        wait(dve, self.spread_ready, c + 1 - self.skip)
        for k in range(KD):
            op = dve.tensor_tensor(self.dst(c, k), self.dst(c, k), self.spread_ps[:, c % self.ring, :].rearrange("p (b t) -> p b t", t=S), ALU.mult)
        op.then_inc(self.scaled, 1)

    def affine(self, act, c):
        if self.gamma is None:
            return
        wait(act, self.scaled, c + 1 - self.skip)
        for k in range(KD):
            op = act.activation(self.dst(c, k), self.dst(c, k), ACT.Identity, bias=self.beta[:, k:k + 1], scale=self.gamma[:, k:k + 1])
        op.then_inc(self.normed, 1)


def layer_norm(nc, name, src, dst, consts, gamma=None, beta=None, weights=None):
    ph = Phase(nc, name)
    stream = None if weights is None else WeightStream(ph, *weights, 16, 4)
    per_stage = 0 if weights is None else stream.pieces // NCH
    norm = Norm(ph, consts, src, lambda c, k: tokens(dst, k, 2 * c, 2), False, gamma, beta, NCH)

    with nc.Block() as block:
        @block.tensor
        def _(pe):
            for c in range(NCH):
                norm.mean(pe, c)
            for c in range(NCH + 1):
                if c < NCH:
                    norm.variance(pe, c)
                if c:
                    norm.spread(pe, c - 1)

        @block.scalar
        def _(act):
            for c in range(NCH):
                norm.square(act, c)
                for n in range(c * per_stage, (c + 1) * per_stage):
                    stream.round(act, n)
            for c in range(NCH):
                norm.affine(act, c)

        @block.vector
        def _(dve):
            for c in range(NCH):
                norm.centre(dve, c)
            for c in range(NCH + 1):
                if c < NCH:
                    norm.keep_variance(dve, c)
                    norm.diagonal(dve, c)
                if c:
                    norm.scale(dve, c - 1)

        @block.gpsimd
        def _(pool):
            for c in range(NCH):
                norm.power(pool, c)
                for n in range(c * per_stage, (c + 1) * per_stage):
                    stream.rest(pool, n)

        @block.sync
        def _(sp):
            for n in range(NCH * per_stage):
                stream.load(sp, n)
    ph.close()


def attention(nc, name, kind, src, res, w_hi, w_lo, ident, mask, scale, keys, bias_qk, bias_v, bias_out,
              cos, sin, expo, loads, weights=None, next_norm=None):
    ph = Phase(nc, name)
    rope = kind == "rope"
    stream = None if weights is None else WeightStream(ph, *weights, B, 1)
    xs_hi = ph.sb("xs_hi", [P, KD, S], F32R)
    xs_lo = ph.sb("xs_lo", [P, KD, S], F32R)
    w_in = [x[:, 0:IN_COLS].rearrange("p (k n) -> p k n", k=KD) for x in (w_hi, w_lo)]
    w_out = [x[:, IN_COLS:ATT_COLS].rearrange("p (k n) -> p k n", n=D) for x in (w_hi, w_lo)]
    qk = ph.sb("qk", [P, 2, QT, 2 * GW]) if rope else None
    qk_rot = ph.sb("qk_rot", [P, QT, 2 * GW]) if rope else None
    sq = ph.sb("sq", [P, QT, 2 * GW]) if rope else None
    ssq = ph.sb("ssq", [P, QT, 2 * HG]) if rope else None
    q_t, k_t = [[ph.sb(n + part, [P, 2, 2, S], F32 if rope else F32R) for part in (("",) if rope else ("_hi", "_lo"))]
                for n in ("q_t", "k_t")]
    v_sb = ph.sb("v_sb", [P, 2, QT, GW])
    probs = ph.sb("probs", [P, 4, QT, S])
    probs_t = ph.sb("probs_t", [P, 2, QT, S])
    row_max = ph.sb("row_max", [P, 4, QT])
    neg_max = ph.sb("neg_max", [P, 4, QT])
    row_sum = ph.sb("row_sum", [P, 2, 2, QT * 2])
    inv_sum = ph.sb("inv_sum", [P, 2, QT * 2])
    out = ph.sb("out", [P, QT, GW])
    out_t_hi = ph.sb("out_t_hi", [P, 2, S], F32R)
    out_t_lo = ph.sb("out_t_lo", [P, 2, S], F32R)

    proj_ps = ph.psum("proj_ps", [P, 2, 512])
    score_ps = ph.psum("score_ps", [P, 2, QT, S])
    probs_t_ps = ph.psum("probs_t_ps", [P, QT, S])
    turn_ps = ph.psum("turn_ps", [P, 2, S])
    val_ps = ph.psum("val_ps", [P, 2, 512])

    xs_rounded, out_rounded, qk_rounded = ph.sem("xs_rounded"), ph.sem("out_rounded"), ph.sem("qk_rounded")
    xs_ready, proj_full, proj_free = ph.sem("xs_ready"), ph.sem("proj_full"), ph.sem("proj_free")
    sq_done, ssq_done, qk_ready, pool_step = ph.sem("sq_done"), ph.sem("ssq_done"), ph.sem("qk_ready"), ph.sem("pool_step")
    turn_full, turn_free = ph.sem("turn_full"), ph.sem("turn_free")
    score_full, score_free, max_ready = ph.sem("score_full"), ph.sem("score_free"), ph.sem("max_ready")
    exp_done, pt_full, pt_ready = ph.sem("exp_done"), ph.sem("pt_full"), ph.sem("pt_ready")
    val_done, inv_ready, out_ready = ph.sem("val_done"), ph.sem("inv_ready"), ph.sem("out_ready")
    dve_hold, pool_hold = ph.sem("dve_hold"), ph.sem("pool_hold")
    loaded, cleared = ph.sem("loaded"), ph.sem("cleared")

    def q_fill(G):
        return 0 if isinstance(G, int) and G == 0 else 3 * G - 1

    def k_fill(G):
        return 1 if isinstance(G, int) and G == 0 else 3 * G

    def out_fill(G):
        return 3 * G + 4 if rope else G

    def v_fill(G):
        return 3 * G + 2 if isinstance(G, int) and G < 3 else 4 * G - 1

    def qk_fill(G, t):
        return 3 * G + t if isinstance(G, int) and G < 4 else 4 * G - 3 + t

    def w_fill(G):
        if isinstance(G, int) and G >= NG * B - 2:
            return 4 * NG * B + 3 + G - (NG * B - 2)
        return 4 * G + 12

    def proj_bank(fill, steady):
        return proj_ps[:, fill % 2 if isinstance(fill, int) else steady, :]

    def pair_of(ps, pair):
        return ps[:, pair, 0:QT * 2 * HD].rearrange("p (t h d) -> p t h d", t=QT, d=HD)

    def back(N, forward):
        return not isinstance(N, int) or (N >= 0 and (forward or N < HG * NG * B))

    def blocks():
        return [(kt, qt) for qt in range(QT) for kt in range(QT)
                if keys[qt][0] < (kt + 1) * P and keys[qt][1] > kt * P]

    ahead = None
    if next_norm:
        flat = lambda x: x[:, :, :].rearrange("p a b -> p (a b)")
        score_bank = lambda i: score_ps[:, i:i + 1, :, :].rearrange("p i t n -> p i (t n)")
        ahead = Norm(ph, next_norm[0], res, lambda c, k: next_norm[1][:, k, :].rearrange("p (b t) -> p b t", t=S), True, None, None, 1,
                     sq=flat(sq)[:, 0:KD * CH].rearrange("p (r k n) -> p r k n", r=1, k=KD),
                     diag=flat(qk_rot)[:, 0:CH].unsqueeze(1), means=score_bank(1), spreads=score_bank(0))

    with nc.Block() as block:
        @block.tensor
        def _(pe):
            def project(G, g, part, batch):
                f = v_fill(G) if part == 2 else qk_fill(G, part)
                bank = proj_bank(f, (1, 0, 1)[part])
                wait(pe, proj_free, f - 1)
                if g == 0 and part == 0:
                    pe.wait_ge(xs_ready, batch + 1)
                if part < 2 and not rope:
                    for i in range(2):
                        at = part * INNER + g * GW + i * P
                        mm = products(pe, bank[:, i * S:(i + 1) * S], [[w[:, k, at:at + P] for w in w_in] for k in range(KD)],
                                      [(xs_hi[:, k, :], xs_lo[:, k, :]) for k in range(KD)])
                elif part < 2:
                    mm = products(pe, bank, [(xs_hi[:, k, part * P:(part + 1) * P], xs_lo[:, k, part * P:(part + 1) * P]) for k in range(KD)],
                                  [[w[:, k, 0:2 * INNER].rearrange("p (s n) -> p s n", s=2)[:, :, g * GW:(g + 1) * GW] for w in w_in]
                                   for k in range(KD)])
                else:
                    for t in range(QT):
                        mm = products(pe, bank[:, t * GW:(t + 1) * GW], [(xs_hi[:, k, t * P:(t + 1) * P], xs_lo[:, k, t * P:(t + 1) * P]) for k in range(KD)],
                                      [[w[:, k, 2 * INNER + g * GW:2 * INNER + (g + 1) * GW] for w in w_in] for k in range(KD)])
                mm.then_inc(proj_full, 1)

            def turn(src_tiles, fill):
                wait(pe, turn_free, fill)
                for i, j, tile in src_tiles:
                    mm = pe.transpose(turn_ps[:, i, j * P:(j + 1) * P], tile, ident[:, :])
                mm.then_inc(turn_full, 1)

            def turn_qk(G, g, which):
                if not rope:
                    return
                pe.wait_ge(qk_ready, 2 * G + 2)
                turn([(i, t, qk[:, g % 2, t, which * GW + i * P:which * GW + (i + 1) * P]) for i in range(2) for t in range(QT)],
                     (q_fill, k_fill)[which](G))

            def scores(N, G, g, j):
                if j == 0 and rope:
                    pe.wait_ge(turn_free, k_fill(G) + 1)
                if j == 0 and not rope:
                    pe.wait_ge(proj_free, qk_fill(G, 1) + 1)
                wait(pe, score_free, N - 1)
                r = slice((j % 2) * HD, (j % 2 + 1) * HD)
                for qt in range(QT):
                    a, z = keys[qt]
                    q, k = [x[r, g % 2, j // 2, qt * P:(qt + 1) * P] for x in q_t], [x[r, g % 2, j // 2, a:z] for x in k_t]
                    if rope:
                        mm = pe.matmul(score_ps[:, j % 2, qt, a:z], q[0], k[0], start=True, stop=True)
                    else:
                        mm = products(pe, score_ps[:, j % 2, qt, a:z], [q], [k])
                mm.then_inc(score_full, 1)

            def turn_probs(N, j):
                pe.wait_ge(exp_done, N + 1)
                wait(pe, pt_ready, N)
                for kt, qt in blocks():
                    mm = pe.transpose(probs_t_ps[:, kt, qt * P:(qt + 1) * P], probs[:, j, qt, kt * P:(kt + 1) * P], ident[:, :])
                mm.then_inc(pt_full, 1)

            def values(N, G, g, j):
                pe.wait_ge(pt_ready, N + 1)
                if j == 0:
                    pe.wait_ge(proj_free, v_fill(G) + 1)
                if j % 2 == 0:
                    wait(pe, out_ready, 2 * G + j // 2 - 1)
                for qt in range(QT):
                    kts = [kt for kt, q in blocks() if q == qt]
                    for kt in kts:
                        mm = pe.matmul(pair_of(val_ps, j // 2)[:, qt, j % 2, :], probs_t[:, j % 2, kt, qt * P:(qt + 1) * P],
                                       v_sb[:, g % 2, kt, j * HD:(j + 1) * HD], start=(kt == kts[0]), stop=(kt == kts[-1]))
                mm.then_inc(val_done, 1)

            def turn_out(G):
                pe.wait_ge(out_ready, 2 * G + 2)
                turn([(i, t, out[:, t, i * P:(i + 1) * P]) for i in range(2) for t in range(QT)], out_fill(G))

            def project_out(G, g):
                f = w_fill(G)
                pe.wait_ge(turn_free, out_fill(G) + 1)
                wait(pe, proj_free, f - 1)
                for m in range(KD):
                    mm = products(pe, proj_bank(f, 0)[:, m * S:(m + 1) * S],
                                  [[w[:, 2 * g + k, m * P:(m + 1) * P] for w in w_out] for k in range(2)],
                                  [(out_t_hi[:, k, :], out_t_lo[:, k, :]) for k in range(2)])
                mm.then_inc(proj_full, 1)

            def body(b, forward=True):
                for g in range(NG):
                    G = NG * b + g
                    gn, gp, gq = (g + 1) % NG, (g - 1) % NG, (g + 2) % NG
                    for j in range(HG):
                        N = HG * G + j
                        if ahead and not forward and j == 0:
                            pe.wait_ge(score_free, HG * NG * B + 1)
                            ahead.mean(pe, 0)
                        if ahead and not forward and j == 2:
                            ahead.variance(pe, 0)
                        if forward and j < 3:
                            scores(N + 1, G, g, j + 1)
                        if back(N - 1, forward):
                            turn_probs(N - 1, (j - 1) % HG)
                        if j == 0 and forward:
                            project(G + 1, gn, 2, b + (g + 1) // NG)
                        if j == 1 and back(HG * (G - 2), forward):
                            project_out(G - 2, gq)
                        if j == 2:
                            if back(HG * (G - 1), forward):
                                turn_out(G - 1)
                            if forward:
                                project(G + 2, gq, 0, b + (g + 2) // NG)
                        if j == 3 and forward:
                            turn_qk(G + 1, gn, 0)
                        if back(N - 2, forward):
                            values(N - 2, G if j >= 2 else G - 1, g if j >= 2 else gp, (j - 2) % HG)
                        if j == 3 and forward:
                            turn_qk(G + 1, gn, 1)
                            project(G + 2, gq, 1, b + (g + 2) // NG)
                            scores(N + 1, G + 1, gn, 0)
                    if not forward:
                        if ahead:
                            ahead.spread(pe, 0)
                        project_out(G - 1, gp)
                        break

            for part in range(3):
                project(0, 0, part, 0)
            project(1, 1, 0, 0)
            project(1, 1, 1, 0)
            turn_qk(0, 0, 0)
            turn_qk(0, 0, 1)
            scores(0, 0, 0, 0)
            body(0)
            with pe.Fori(1, B) as b:
                body(b)
            body(B, forward=False)

        @block.scalar
        def _(act):
            def stage(b):
                wait(act, proj_full, 4 * NG * b - 4)
                for k in range(KD):
                    op = act.activation(xs_hi[:, k, :], tokens(src, k, b, 1, rope).rearrange("p a t -> p (a t)"), ACT.Copy)
                op.then_inc(xs_rounded, 1)

            def square(G, g, t):
                f = qk_fill(G, t)
                act.wait_ge(proj_full, f + 1)
                wait(act, ssq_done, 2 * (G - 1) + t + 1)
                act.activation(sq[:, t, :], proj_bank(f, 1 - t), ACT.Square).then_inc(sq_done, 1)

            def keep_qk(G, g, which):
                if not rope:
                    return
                act.wait_ge(turn_full, (q_fill, k_fill)[which](G) + 1)
                wait(act, score_full, HG * (G - 1))
                dst = (q_t, k_t)[which][0][:, g % 2, :, :]
                act.activation(dst, turn_ps[:, :, :], ACT.Copy).then_inc(turn_free, 1)

            def exps(N, G, g, j):
                act.wait_ge(max_ready, N + 1)
                if j == 0:
                    wait(act, out_ready, 2 * G - 2)
                for qt in range(QT):
                    a, z = keys[qt]
                    op = act.activation(probs[:, j, qt, a:z], probs[:, j, qt, a:z], ACT.Exp, bias=neg_max[:, j, qt:qt + 1],
                                        scale=scale, accum_out=row_sum[:, g % 2, j // 2, 2 * qt + j % 2:2 * qt + j % 2 + 1])
                op.then_inc(exp_done, 1)

            def keep_probs_t(N, j):
                act.wait_ge(pt_full, N + 1)
                wait(act, val_done, N - 1)
                if len(blocks()) == QT * QT:
                    op = act.activation(probs_t[:, j % 2, :, :], probs_t_ps[:, :, :], ACT.Copy)
                else:
                    act.activation(probs_t[:, j % 2, 0, :], probs_t_ps[:, 0, :], ACT.Copy)
                    op = act.activation(probs_t[:, j % 2, 1, P:S], probs_t_ps[:, 1, P:S], ACT.Copy)
                op.then_inc(pt_ready, 1)

            def keep_out_t(G):
                act.wait_ge(turn_full, out_fill(G) + 1)
                if not (isinstance(G, int) and G == 0):
                    wait(act, proj_full, w_fill(G - 1) + 1)
                act.activation(out_t_hi[:, :, :], turn_ps[:, :, :], ACT.Copy).then_inc(out_rounded, 1)

            def body(b, forward=True):
                for g in range(NG):
                    G = NG * b + g
                    gn, gq = (g + 1) % NG, (g + 2) % NG
                    for j in range(HG):
                        N = HG * G + j
                        if forward and j == 1 and g == NG - 2:
                            stage(b + 1)
                        if back(N - 1, forward):
                            keep_probs_t(N - 1, (j - 1) % HG)
                        if ahead and not forward and j == 1:
                            wait(act, ssq_done, 2 * (NG * B + 2))
                            ahead.square(act, 0)
                        if j == 2 and back(HG * (G - 1), forward):
                            keep_out_t(G - 1)
                        if forward:
                            if j < 3:
                                exps(N + 1, G, g, j + 1)
                            if rope and j == 2:
                                square(G + 2, gq, 0)
                            if j == 3:
                                keep_qk(G + 1, gn, 0)
                                keep_qk(G + 1, gn, 1)
                                if rope:
                                    square(G + 2, gq, 1)
                                exps(N + 1, G + 1, gn, 0)
                    if not forward:
                        break
                if forward and stream:
                    stream.round(act, b)

            stage(0)
            if rope:
                for G in (0, 1):
                    square(G, G, 0)
                    square(G, G, 1)
            keep_qk(0, 0, 0)
            keep_qk(0, 0, 1)
            exps(0, 0, 0, 0)
            body(0)
            with act.Fori(1, B) as b:
                body(b)
            body(B, forward=False)

        @block.vector
        def _(dve):
            def maxima(N, j):
                dve.wait_ge(score_full, N + 1)
                wait(dve, pt_full, N - 3)
                dve.sem_inc(dve_hold, 1)
                for qt in range(QT):
                    a, z = keys[qt]
                    op = dve.tensor_tensor_reduce(probs[:, j, qt, a:z], score_ps[:, j % 2, qt, a:z], mask[:, qt, a:z],
                                                  1.0, -3e38, ALU.add, ALU.max, row_max[:, j, qt:qt + 1])
                op.then_inc(score_free, 1)
                dve.wait_ge(score_free, N + 1)
                dve.tensor_scalar(neg_max[:, j, :], row_max[:, j, :], -scale, None, ALU.mult).then_inc(max_ready, 1)

            def turn_heads(G, g, t):
                f = qk_fill(G, t)
                bank = proj_bank(f, 1 - t)
                if not rope:
                    dve.wait_ge(proj_full, f + 1)
                    wait(dve, score_full, HG * (G - 1))
                    hi, lo = (q_t, k_t)[t]
                    for i in range(2):
                        at = t * (INNER // P) + g * (GW // P) + i
                        dve.tensor_scalar(hi[:, g % 2, i, :], bank[:, i * S:(i + 1) * S], bias_qk[:, at:at + 1], None, ALU.add)\
                            .then_inc(qk_rounded, 1)
                    for i in range(2):
                        at = t * (INNER // P) + g * (GW // P) + i
                        dve.wait_ge(qk_rounded, 2 * (2 * G + t) + i + 1)
                        op = dve.scalar_tensor_tensor(lo[:, g % 2, i, :], bank[:, i * S:(i + 1) * S], bias_qk[:, at:at + 1],
                                                      hi[:, g % 2, i, :].bitcast(F32), ALU.add, ALU.subtract)
                    op.then_inc(proj_free, 1)
                    return
                dve.wait_ge(sq_done, 2 * G + t + 1)
                wait(dve, qk_ready, 2 * (G - 1) + t + 1)
                dve.tensor_reduce(ssq[:, t, :], sq[:, t, :].rearrange("p (h d) -> p h d", d=HD), AX.X, ALU.add).then_inc(ssq_done, 1)
                if not (isinstance(G, int) and G < 2):
                    wait(dve, turn_full, k_fill(G - 2) + 1)
                view = lambda x: x.rearrange("p (s h d) -> p s h d", s=2, h=HG)
                table = lambda x, lo, hi: x[:, t, :, lo:hi].unsqueeze(2).broadcast_to([P, 2, HG, hi - lo])
                dve.tensor_tensor(view(qk[:, g % 2, t, :]), view(bank), table(cos, 0, HD), ALU.mult)
                half = HD // 2
                for lo in (0, half):
                    other = half - lo
                    op = dve.tensor_tensor(view(qk_rot[:, t, :])[:, :, :, lo:lo + half], view(bank)[:, :, :, other:other + half],
                                           table(sin, lo, lo + half), ALU.mult)
                op.then_inc(proj_free, 1)

            def keep_v(G, g):
                dve.wait_ge(proj_full, v_fill(G) + 1)
                wait(dve, val_done, HG * (G - 1))
                dst = v_sb[:, g % 2, :, :]
                bank = proj_bank(v_fill(G), 1).rearrange("p (t n) -> p t n", t=QT)
                if rope:
                    op = dve.tensor_copy(dst, bank)
                else:
                    w = bias_v[:, g * GW:(g + 1) * GW].unsqueeze(1).broadcast_to([P, QT, GW])
                    op = dve.tensor_tensor(dst, bank, w, ALU.add)
                op.then_inc(proj_free, 1)

            def norm(G, g, pair):
                dve.wait_ge(val_done, HG * G + 2 * pair + 2)
                dve.reciprocal(inv_sum[:, pair, :], row_sum[:, g % 2, pair, :]).then_inc(inv_ready, 1)
                if not (isinstance(G, int) and G == 0):
                    wait(dve, turn_full, out_fill(G - 1) + 1)
                dve.wait_ge(inv_ready, 2 * G + pair + 1)
                dst = out[:, :, pair * P:(pair + 1) * P].rearrange("p t (h d) -> p t h d", d=HD)
                inv = inv_sum[:, pair, :].rearrange("p (t h) -> p t h", h=2).unsqueeze(3).broadcast_to([P, QT, 2, HD])
                dve.tensor_tensor(dst, pair_of(val_ps, pair), inv, ALU.mult).then_inc(out_ready, 1)

            def out_rest(G):
                dve.wait_ge(out_rounded, G + 1)
                dve.tensor_tensor(out_t_lo[:, :, :], turn_ps[:, :, :], out_t_hi[:, :, :].bitcast(F32), ALU.subtract).then_inc(turn_free, 1)

            def residual(G, g, b):
                f = w_fill(G)
                dve.wait_ge(proj_full, f + 1)
                if g:
                    wait(dve, proj_free, w_fill(G - 1) + 1)
                for m in range(KD):
                    r, y = tokens(res, m, b).rearrange("p a t -> p (a t)"), proj_bank(f, 0)[:, m * S:(m + 1) * S]
                    if g == 0:
                        op = dve.scalar_tensor_tensor(r, y, bias_out[:, m:m + 1], r, ALU.add, ALU.add)
                    else:
                        op = dve.tensor_tensor(r, y, r, ALU.add)
                op.then_inc(proj_free, 1)

            def body(b, forward=True):
                for g in range(NG):
                    G = NG * b + g
                    gn, gp, gq = (g + 1) % NG, (g - 1) % NG, (g + 2) % NG
                    for j in range(HG):
                        N = HG * G + j
                        if ahead and not forward and j == 0:
                            ahead.centre(dve, 0)
                        if ahead and not forward and j == 2:
                            ahead.keep_variance(dve, 0)
                        if j == 3 and forward:
                            norm(G, g, 0)
                        if forward:
                            maxima(N + 1, (j + 1) % HG)
                        if j == 3 and forward:
                            turn_heads(G + 2, gq, 1)
                        if j == 1:
                            if back(HG * (G - 1), forward):
                                norm(G - 1, gp, 1)
                            if forward:
                                keep_v(G + 1, gn)
                            if back(HG * (G - 2), forward):
                                residual(G - 2, gq, b + (g - 2) // NG)
                        if j == 2 and back(HG * (G - 1), forward):
                            out_rest(G - 1)
                        if j == 2 and forward:
                            turn_heads(G + 2, gq, 0)
                    if not forward:
                        if ahead:
                            wait(dve, qk_ready, 2 * (NG * B + 2))
                            ahead.diagonal(dve, 0)
                            ahead.scale(dve, 0)
                        residual(G - 1, gp, b - 1)
                        break

            op = dve.memset(probs[:, :, :, :], 0.0)
            op.then_inc(cleared, 1)
            turn_heads(0, 0, 0)
            turn_heads(0, 0, 1)
            keep_v(0, 0)
            turn_heads(1, 1, 0)
            turn_heads(1, 1, 1)
            wait(dve, cleared, 1)
            maxima(0, 0)
            body(0)
            with dve.Fori(1, B) as b:
                body(b)
            body(B, forward=False)

        @block.gpsimd
        def _(pool):
            def scale_heads(G, g, t):
                step = 3 * (2 * G + t)
                pool.wait_ge(ssq_done, 2 * G + t + 1)
                pool.sem_inc(pool_hold, 1)
                pool.tensor_scalar(ssq[:, t, :], ssq[:, t, :], 1e-24, None, ALU.max).then_inc(pool_step, 1)
                pool.wait_ge(pool_step, step + 1)
                pool.tensor_tensor(ssq[:, t, :], ssq[:, t, :], expo[:, :], ALU.pow).then_inc(pool_step, 1)
                pool.wait_ge(proj_free, qk_fill(G, t) + 1)
                pool.tensor_tensor(qk[:, g % 2, t, :], qk[:, g % 2, t, :], qk_rot[:, t, :], ALU.add).then_inc(pool_step, 1)
                pool.wait_ge(pool_step, step + 3)
                view = qk[:, g % 2, t, :].rearrange("p (h d) -> p h d", d=HD)
                pool.tensor_tensor(view, view, ssq[:, t, :].unsqueeze(2).broadcast_to([P, 2 * HG, HD]), ALU.mult)\
                    .then_inc(qk_ready, 1)

            def stage_rest(b):
                pool.wait_ge(xs_rounded, b + 1)
                for k in range(KD):
                    op = pool.tensor_tensor(xs_lo[:, k, :], tokens(src, k, b, 1, rope).rearrange("p a t -> p (a t)"),
                                            xs_hi[:, k, :].bitcast(F32), ALU.subtract)
                op.then_inc(xs_ready, 1)

            def body(b):
                for g in range(NG):
                    if g == NG - 2:
                        stage_rest(b + 1)
                    if rope:
                        scale_heads(NG * b + g + 2, (g + 2) % NG, 0)
                        scale_heads(NG * b + g + 2, (g + 2) % NG, 1)
                if stream:
                    stream.rest(pool, b)

            stage_rest(0)
            if rope:
                for G in (0, 1):
                    scale_heads(G, G, 0)
                    scale_heads(G, G, 1)
            body(0)
            with pool.Fori(1, B) as b:
                body(b)
            if ahead:
                ahead.power(pool, 0)

        @block.sync
        def _(sp):
            for n, (dst, source) in enumerate(loads):
                sp.dma_start(dst, source).then_inc(loaded, 16)
            if stream:
                stream.load(sp, 0)
                with sp.Fori(1, B) as b:
                    stream.load(sp, b)
            wait(sp, loaded, 16 * len(loads))
    ph.close()


def feed_forward(nc, name, res, w_hi, w_lo, b1, b2, gamma, beta, consts, loads, weights, tables, xn):
    ph = Phase(nc, name)
    RING = 4
    w1 = [x[:, 0:UP_COLS].rearrange("p (k a n) -> p k a n", k=KD, a=2) for x in (w_hi, w_lo)]
    w2 = [x[:, UP_COLS:FF_COLS].rearrange("p (m n) -> p m n", n=D) for x in (w_hi, w_lo)]
    xn_hi, xn_lo = ph.sb("xn_hi", [P, 2, KD, CH], F32R), ph.sb("xn_lo", [P, 2, KD, CH], F32R)
    gate = ph.sb("gate", [P, 2, CH])
    hid = ph.sb("hid", [P, 2, CH])
    hid_hi, hid_lo = ph.sb("hid_hi", [P, RING, CH], F32R), ph.sb("hid_lo", [P, RING, CH], F32R)
    stream = WeightStream(ph, *weights, 16, 2)
    up_ps = ph.psum("up_ps", [P, 2, 2, CH])
    down_ps = ph.psum("down_ps", [P, KD, CH])
    norm = Norm(ph, consts, res, lambda c, k: xn[:, k, :].rearrange("p (b t) -> p b t", t=S), True, gamma, beta, 1, skip=1)
    xn_rounded, xn_split = ph.sem("xn_rounded"), ph.sem("xn_split")
    up_full, gate_ready, hid_ready = ph.sem("up_full"), ph.sem("gate_ready"), ph.sem("hid_ready")
    hid_rounded, hid_split = ph.sem("hid_rounded"), ph.sem("hid_split")
    down_done, res_done, loaded = ph.sem("down_done"), ph.sem("res_done"), ph.sem("loaded")

    with nc.Block() as block:
        @block.tensor
        def _(pe):
            def up(c, m):
                pe.wait_ge(xn_split, c + 1)
                wait(pe, hid_ready, FT * c + m - 1)
                for part in (0, 1):
                    mm = products(pe, up_ps[:, m % 2, part, :], [[w[:, k, part, m * P:(m + 1) * P] for w in w1] for k in range(KD)],
                                  [(xn_hi[:, c % 2, k, :], xn_lo[:, c % 2, k, :]) for k in range(KD)])
                mm.then_inc(up_full, 1)

            def down(c, m):
                pe.wait_ge(hid_split, FT * c + m + 1)
                if m == 0:
                    wait(pe, res_done, c)
                for n in range(KD):
                    mm = products(pe, down_ps[:, n, :], [[w[:, m, n * P:(n + 1) * P] for w in w2]], [(hid_hi[:, (FT * c + m) % RING, :], hid_lo[:, (FT * c + m) % RING, :])],
                                  m == 0, m == FT - 1)
                mm.then_inc(down_done, 1)

            for t in range(FT * NCH + 2):
                c, m = t // FT, t % FT
                if c + 1 < NCH and m == 4:
                    norm.spread(pe, c + 1)
                if c < NCH:
                    up(c, m)
                if c + 1 < NCH and m == 0:
                    norm.mean(pe, c + 1)
                if c + 1 < NCH and m == 2:
                    norm.variance(pe, c + 1)
                if t >= 2:
                    down((t - 2) // FT, (t - 2) % FT)

        @block.scalar
        def _(act):
            def round_xn(c):
                act.wait_ge(norm.done, c + 1)
                wait(act, down_done, FT * (c - 1))
                act.activation(xn_hi[:, c % 2, :, :], xn[:, :, :], ACT.Copy).then_inc(xn_rounded, 1)

            def round_hid(c, m):
                act.wait_ge(hid_ready, FT * c + m + 1)
                wait(act, down_done, FT * c + m + 1 - RING)
                act.activation(hid_hi[:, (FT * c + m) % RING, :], hid[:, (FT * c + m) % 2, :], ACT.Copy).then_inc(hid_rounded, 1)

            norm.affine(act, 0)
            round_xn(0)
            for c in range(NCH):
                for m in range(FT):
                    act.wait_ge(up_full, FT * c + m + 1)
                    wait(act, hid_ready, FT * c + m - 1)
                    act.activation(gate[:, m % 2, :], up_ps[:, m % 2, 1, :], ACT.Gelu,
                                   bias=b1[:, FT + m:FT + m + 1]).then_inc(gate_ready, 1)
                    if c + 1 < NCH and m == 0:
                        norm.square(act, c + 1)
                    round_hid(c, m)
                    if c + 1 < NCH and m == 4:
                        norm.affine(act, c + 1)
                        round_xn(c + 1)
                    if FT * c + m < stream.pieces:
                        stream.round(act, FT * c + m)

        @block.gpsimd
        def _(pool):
            for c in range(NCH):
                for m in range(FT):
                    if FT * c + m < stream.pieces:
                        stream.rest(pool, FT * c + m)
                    if m == 1 and c + 1 < NCH:
                        norm.power(pool, c + 1)
            tables(pool, loaded, 16 * len(loads))

        @block.vector
        def _(dve):
            def rest_xn(c):
                dve.wait_ge(xn_rounded, c + 1)
                dve.tensor_tensor(xn_lo[:, c % 2, :, :], xn[:, :, :], xn_hi[:, c % 2, :, :].bitcast(F32), ALU.subtract).then_inc(xn_split, 1)

            def rest_hid(c, m):
                dve.wait_ge(hid_rounded, FT * c + m + 1)
                r = (FT * c + m) % RING
                dve.tensor_tensor(hid_lo[:, r, :], hid[:, (FT * c + m) % 2, :], hid_hi[:, r, :].bitcast(F32), ALU.subtract).then_inc(hid_split, 1)

            def add(c):
                dve.wait_ge(down_done, FT * (c + 1))
                for n in range(KD):
                    r = tokens(res, n, 2 * c, 2)
                    op = dve.scalar_tensor_tensor(r, down_ps[:, n, :].rearrange("p (b t) -> p b t", t=S),
                                                  b2[:, n:n + 1], r, ALU.add, ALU.add)
                op.then_inc(res_done, 1)

            rest_xn(0)
            for c in range(NCH):
                for m in range(FT):
                    if c + 1 < NCH and m == 3:
                        norm.diagonal(dve, c + 1)
                    if c + 1 < NCH and m == 4:
                        norm.scale(dve, c + 1)
                    if c + 1 < NCH and m == FT - 1:
                        rest_xn(c + 1)
                    dve.wait_ge(gate_ready, FT * c + m + 1)
                    wait(dve, hid_split, FT * c + m - 1)
                    dve.scalar_tensor_tensor(hid[:, (FT * c + m) % 2, :], up_ps[:, m % 2, 0, :], b1[:, m:m + 1],
                                             gate[:, m % 2, :], ALU.add, ALU.mult).then_inc(hid_ready, 1)
                    if c or m:
                        rest_hid((FT * c + m - 1) // FT, (m - 1) % FT)
                    if c and m == 1:
                        add(c - 1)
                    if c + 1 < NCH:
                        if m == 0:
                            dve.wait_ge(xn_split, c + 1)
                            norm.centre(dve, c + 1)
                        if m == 2:
                            norm.keep_variance(dve, c + 1)
            rest_hid(NCH - 1, FT - 1)
            add(NCH - 1)

        @block.sync
        def _(sp):
            for dst, source in loads:
                sp.dma_start(dst, source).then_inc(loaded, 16)
            for n in range(stream.pieces):
                stream.load(sp, n)
            wait(sp, loaded, 16 * len(loads))
    ph.close()


def token_features(nc, dram, dst, loads):
    ph = Phase(nc, "tok")
    LOW_ROWS, ROWS = 32, 32 + V
    ids, iota = ph.sb("ids", [ROWS, B * S], I32), ph.sb("iota", [ROWS, 1])
    features = ph.sb("features", [ROWS, B, S])
    mask_i = ph.sb("mask_i", [ROWS, B * S], I32)
    mask = ph.sb("mask", [ROWS, B, S + 2])
    length = ph.sb("length", [ROWS, B, S])
    masked = ph.sb("masked", [ROWS, B, S + 2])
    emb_t, pca_t = ph.sb("emb_t", [P, KD, ROWS]), ph.sb("pca_t", [PCA, ROWS])
    proj_t, fus = ph.sb("proj_t", [P, KD, PCA]), ph.sb("fus", [P, 2 * KD, D])
    proj_b, fus_b = ph.sb("proj_b", [P, KD]), ph.sb("fus_b", [P, KD])
    projected, table, bias = ph.sb("projected", [PCA, D]), ph.sb("table", [ROWS, D]), ph.sb("bias", [P, KD])
    small_ps, bias_ps = ph.psum("small_ps", [P, 2, 512]), ph.psum("bias_ps", [P, 512])
    out_ps = ph.psum("out_ps", [P, 2, KD, CH])
    got, zeroed, padded, loaded = ph.sem("got"), ph.sem("zeroed"), ph.sem("padded"), ph.sem("loaded")
    proj_full, proj_kept, table_full, table_kept = (ph.sem(n) for n in ("proj_full", "proj_kept", "table_full", "table_kept"))
    masks, lengths, inverted, one_hot = (ph.sem(n) for n in ("masks", "lengths", "inverted", "one_hot"))
    step, windowed, fused, stored = (ph.sem(n) for n in ("step", "windowed", "fused", "stored"))
    low = slice(LOW_ROWS, ROWS)
    two = lambda x, c, lo=0: x[:, 2 * c:2 * c + 2, lo:lo + S]
    two_low = lambda x, c, lo=0: x[low, 2 * c:2 * c + 2, lo:lo + S]
    firsts = [(ids[:, :], dram["x"].unsqueeze(0).broadcast_to([ROWS, B * S])), (iota[:, :], dram["iota"]),
              (mask_i[:, :], dram["mask"].unsqueeze(0).broadcast_to([ROWS, B * S]))]
    tables = [(proj_t[:, :, :], dram["proj_t"]), (fus[:, :, :], dram["fus_w"].rearrange("(k p) n -> p k n", p=P)),
              (emb_t[:, :, :], dram["emb_t"]), (pca_t[:, :], dram["pca_t"]),
              (proj_b[:, :], dram["proj_b"]), (fus_b[:, :], dram["fus_b"])]

    with nc.Block() as block:
        @block.sync
        def _(sp):
            for d, source in firsts:
                sp.dma_start(d, source).then_inc(got, 16)
            for d, source in tables:
                sp.dma_start(d, source).then_inc(loaded, 16)
            for d, source in loads:
                sp.dma_start(d, source).then_inc(padded, 16)
            wait(sp, padded, 16 * len(loads))

        @block.gpsimd
        def _(pool):
            pool.memset(mask[:, :, :], 0.0).then_inc(zeroed, 1)
            pool.memset(masked[:, :, :], 0.0).then_inc(zeroed, 1)
            pool.wait_ge(got, 16 * len(firsts))
            pool.wait_ge(zeroed, 2)
            for c in range(NCH):
                pool.tensor_copy(two(mask, c, 1), mask_i[:, c * CH:(c + 1) * CH].rearrange("p (b t) -> p b t", t=S)).then_inc(masks, 1)
                pool.wait_ge(masks, c + 1)
                pool.tensor_tensor(two(length, c), two(mask, c, 0), two(mask, c, 1), ALU.add).then_inc(lengths, 1)
                pool.wait_ge(lengths, 2 * c + 1)
                pool.tensor_tensor(two(length, c), two(length, c), two(mask, c, 2), ALU.add).then_inc(lengths, 1)

        @block.vector
        def _(dve):
            dve.wait_ge(got, 16 * len(firsts))
            for c in range(NCH):
                dve.tensor_scalar(two(features, c), ids[:, c * CH:(c + 1) * CH].rearrange("p (b t) -> p b t", t=S),
                                  iota[:, :], None, ALU.is_equal).then_inc(one_hot, 1)
            for c in range(NCH):
                at = 5 * c
                dve.wait_ge(lengths, 2 * c + 2)
                dve.tensor_scalar(two_low(length, c), two_low(length, c), 1.0, None, ALU.max).then_inc(step, 1)
                dve.wait_ge(one_hot, c + 1)
                dve.tensor_tensor(two_low(masked, c, 1), two_low(features, c), two_low(mask, c, 1), ALU.mult).then_inc(step, 1)
                dve.wait_ge(step, at + 2)
                dve.tensor_tensor(two_low(features, c), two_low(masked, c, 0), two_low(masked, c, 1), ALU.add).then_inc(step, 1)
                dve.reciprocal(two_low(length, c), two_low(length, c)).then_inc(step, 1)
                dve.wait_ge(step, at + 4)
                dve.tensor_tensor(two_low(features, c), two_low(features, c), two_low(masked, c, 2), ALU.add).then_inc(step, 1)
                dve.wait_ge(step, at + 5)
                dve.tensor_tensor(two_low(features, c), two_low(features, c), two_low(length, c), ALU.mult).then_inc(windowed, 1)

        @block.tensor
        def _(pe):
            pe.wait_ge(loaded, 16 * len(tables))
            for k in range(KD):
                mm = pe.matmul(small_ps[0:PCA, 0, 0:D], proj_t[:, k, :], fus[:, KD + k, :], start=(k == 0), stop=(k == KD - 1))
            for m in range(KD):
                for k in range(KD):
                    mm = pe.matmul(bias_ps[:, m:m + 1], fus[:, KD + k, m * P:(m + 1) * P], proj_b[:, k:k + 1], start=(k == 0), stop=(k == KD - 1))
            mm.then_inc(proj_full, 1)
            pe.wait_ge(proj_kept, 1)
            for k in range(KD):
                pe.matmul(small_ps[0:ROWS, 1, 0:D], emb_t[:, k, :], fus[:, k, :], start=(k == 0), stop=False)
            pe.matmul(small_ps[0:ROWS, 1, 0:D], pca_t[:, :], projected[:, :], start=False, stop=True).then_inc(table_full, 1)
            pe.wait_ge(table_kept, 1)
            for c in range(NCH):
                pe.wait_ge(windowed, c + 1)
                wait(pe, stored, c - 1)
                for m in range(KD):
                    mm = pe.matmul(out_ps[:, c % 2, m, :], table[:, m * P:(m + 1) * P],
                                   two(features, c).rearrange("p b t -> p (b t)"), start=True, stop=True)
                mm.then_inc(fused, 1)

        @block.scalar
        def _(act):
            act.wait_ge(proj_full, 1)
            act.activation(projected[:, :], small_ps[0:PCA, 0, 0:D], ACT.Copy).then_inc(proj_kept, 1)
            for m in range(KD):
                act.activation(bias[:, m:m + 1], bias_ps[:, m:m + 1], ACT.Identity, bias=fus_b[:, m:m + 1])
            act.wait_ge(table_full, 1)
            act.activation(table[:, :], small_ps[0:ROWS, 1, 0:D], ACT.Copy).then_inc(table_kept, 1)
            act.wait_ge(table_kept, 1)
            for c in range(NCH):
                act.wait_ge(fused, c + 1)
                for m in range(KD):
                    op = act.activation(tokens(dst, m, 2 * c, 2), out_ps[:, c % 2, m, :].rearrange("p (b t) -> p b t", t=S),
                                        ACT.Identity, bias=bias[:, m:m + 1])
                op.then_inc(stored, 1)
    ph.close()


def merge_lora(nc, weights, smalls):
    ph = Phase(nc, "lora")
    RANK = 16
    ps = ph.psum("ps", [P, 8, 512])
    a_in, b_in = ph.sb("a_in", [RANK, 3, D]), ph.sb("b_in", [RANK, 3 * INNER])
    a_out, b_out = ph.sb("a_out", [RANK, INNER]), ph.sb("b_out", [RANK, D])
    small, full, merged = ph.sem("small"), ph.sem("full"), ph.sem("merged")
    stream = WeightStream(ph, *weights, 16, 4)
    NC = 3 * INNER // 512
    pieces = [[(0, a_in[:, n // 2, k * P:(k + 1) * P], b_in[:, n * 512:(n + 1) * 512])] for k in range(KD) for n in range(NC)]
    pieces += [[(i * D, a_out[:, (2 * k + i) * P:(2 * k + i + 1) * P], b_out[:, :]) for i in range(2)] for k in range(INNER // P // 2)]

    with nc.Block() as block:
        @block.sync
        def _(sp):
            for dst, source in zip((a_in[:, :, :], b_in[:, :], a_out[:, :], b_out[:, :]), smalls):
                sp.dma_start(dst, source).then_inc(small, 16)
            for n in range(stream.pieces):
                stream.load(sp, n)

        @block.tensor
        def _(pe):
            pe.wait_ge(small, 16 * len(smalls))
            for n, parts in enumerate(pieces):
                wait(pe, merged, n - 7)
                for at, a, b in parts:
                    mm = pe.matmul(ps[:, n % 8, at:at + b.shape[1]], a, b, start=True, stop=True)
                mm.then_inc(full, 1)

        @block.vector
        def _(dve):
            for n in range(len(pieces) + 1):
                if n < len(pieces):
                    stream.await_piece(dve, n)
                    dve.wait_ge(full, n + 1)
                    w = stream.stage[:, n % stream.ring, :]
                    dve.scalar_tensor_tensor(w, ps[:, n % 8, :], 1.0 / RANK, w, ALU.mult, ALU.add).then_inc(merged, 1)
                if n:
                    stream.rest(dve, n - 1)

        @block.scalar
        def _(act):
            for n in range(stream.pieces):
                stream.round(act, n, ready=merged)
    ph.close()


class Quantiser:

    STEPS = 14

    def __init__(self, ph, rows, n):
        self.step = ph.sem("quant_step")
        self.mag = ph.sb("mag", [P, rows, n])
        self.sign = ph.sb("sign", [P, rows, n])
        self.level = ph.sb("level", [P, rows, n])
        self.scale = ph.sb("scale", [P, rows * n // BLK])
        self.inverse = ph.sb("inverse", [P, rows * n // BLK])

    def __call__(self, dve, out, mag, sign, level, before):
        n = mag.shape[1]
        sc, inv = self.scale[:, 0:n // BLK], self.inverse[:, 0:n // BLK]
        blocks = lambda x: x.rearrange("p (b e) -> p b e", e=BLK)
        spread = lambda x: x.unsqueeze(2).broadcast_to([P, n // BLK, BLK])
        made = 0

        def then(op):
            nonlocal made
            made += 1
            op.then_inc(self.step, 1)
            dve.wait_ge(self.step, before + made)

        then(dve.tensor_reduce(sc, blocks(mag), AX.X, ALU.max))
        then(dve.tensor_scalar(sc, sc, 1.0 / 6.0, 1e-12, ALU.mult, ALU.max))
        then(dve.reciprocal(inv, sc))
        then(dve.tensor_tensor(blocks(mag), blocks(mag), spread(inv), ALU.mult))
        then(dve.tensor_scalar(level, mag, 5.0, 2.0, ALU.is_gt, ALU.mult))
        then(dve.scalar_tensor_tensor(level, mag, 3.5, level, ALU.is_gt, ALU.add))
        then(dve.scalar_tensor_tensor(level, mag, 2.5, level, ALU.is_gt, ALU.add))
        then(dve.tensor_scalar(level, level, 2.0, None, ALU.mult))
        for threshold in (1.75, 1.25, 0.75, 0.25):
            then(dve.scalar_tensor_tensor(level, mag, threshold, level, ALU.is_gt, ALU.add))
        then(dve.scalar_tensor_tensor(level, level, 0.5, sign, ALU.mult, ALU.mult))
        then(dve.tensor_tensor(blocks(out), blocks(level), spread(sc), ALU.mult))
        assert made == self.STEPS


def quantise_weights(nc, gate_t, up_t, down_t, dram, ident):
    ph = Phase(nc, "qw")
    raw = ph.sb("raw", [P, 3, 6 * D])
    q = Quantiser(ph, 2, 6 * D)
    BANKS = 4
    turn_ps = ph.psum("turn_ps", [P, BANKS, 4, P])
    got = [ph.sem(f"got{i}") for i in range(3)]
    split, ready, turned, kept, zeroed = (ph.sem(n) for n in ("split", "ready", "turned", "kept", "zeroed"))
    full = QF // P
    rest = QF - full * P
    n_of = (6 * D, 6 * D, KD * QF)

    fills = [[], [], []]
    for i in range(2):
        for k in range(KD):
            for t0, t1 in ((0, 4), (4, full)):
                fills[i].append(((gate_t, up_t)[i][:, k, t0 * P:t1 * P].rearrange("p (t n) -> p t n", n=P), P, P,
                                 [raw[:, i, t * D + k * P:t * D + (k + 1) * P] for t in range(t0, t1)]))
            fills[i].append(((gate_t, up_t)[i][:, k, full * P:QF].unsqueeze(1), P, rest,
                             [raw[0:rest, i, full * D + k * P:full * D + (k + 1) * P]]))
    for m in range(KD):
        for t0, t1 in ((0, 4), (4, full)):
            fills[2].append((down_t[:, t0:t1, m * P:(m + 1) * P], P, P,
                             [raw[:, 2, m * QF + t * P:m * QF + (t + 1) * P] for t in range(t0, t1)]))
        fills[2].append((down_t[0:rest, full:QFT, m * P:(m + 1) * P], rest, P,
                         [raw[:, 2, m * QF + full * P:(m + 1) * QF]]))
    before = [sum(len(f) for f in fills[:i]) for i in range(3)]

    with nc.Block() as block:
        @block.sync
        def _(sp):
            sp.wait_ge(zeroed, 1)
            for i, name in enumerate(("w_gate", "w_up")):
                sp.dma_start(raw[:, i, 0:full * D].rearrange("p (t d) -> p t d", d=D),
                             dram[name][0:full * P, :].rearrange("(t p) d -> p t d", p=P)).then_inc(got[i], 16)
                sp.dma_start(raw[0:rest, i, full * D:QFT * D], dram[name][full * P:QF, :]).then_inc(got[i], 16)
            sp.dma_start(raw[:, 2, 0:KD * QF].rearrange("p (m n) -> p m n", n=QF),
                         dram["w_down"].rearrange("(m p) n -> p m n", p=P)).then_inc(got[2], 16)

        @block.scalar
        def _(act):
            def split_matrix(i):
                n = n_of[i]
                act.wait_ge(got[i], 32 if i < 2 else 16)
                wait(act, ready, i - 1)
                act.activation(q.mag[:, i % 2, 0:n], raw[:, i, 0:n], ACT.Abs).then_inc(split, 1)
                act.activation(q.sign[:, i % 2, 0:n], raw[:, i, 0:n], ACT.Sign).then_inc(split, 1)

            split_matrix(0)
            split_matrix(1)
            for i in range(3):
                if i == 1:
                    split_matrix(2)
                for f, (dst, rows, width, tiles) in enumerate(fills[i], before[i]):
                    act.wait_ge(turned, f + 1)
                    act.activation(dst, turn_ps[0:rows, f % BANKS, 0:len(tiles), 0:width], ACT.Copy).then_inc(kept, 1)

        @block.vector
        def _(dve):
            dve.memset(raw[:, 0:2, full * D:QFT * D], 0.0).then_inc(zeroed, 1)
            for i in range(3):
                n = n_of[i]
                dve.wait_ge(split, 2 * i + 2)
                q(dve, raw[:, i, 0:n], q.mag[:, i % 2, 0:n], q.sign[:, i % 2, 0:n], q.level[:, 0, 0:n], q.STEPS * i)
                dve.sem_inc(ready, 1)

        @block.tensor
        def _(pe):
            for i in range(3):
                pe.wait_ge(ready, i + 1)
                for f, (dst, rows, width, tiles) in enumerate(fills[i], before[i]):
                    wait(pe, kept, f + 1 - BANKS)
                    for t, tile in enumerate(tiles):
                        w = tile.shape[0]
                        mm = pe.transpose(turn_ps[0:rows, f % BANKS, t, 0:w], tile, ident[0:w, 0:w])
                    mm.then_inc(turned, 1)
    ph.close()


def quantised_feed_forward(nc, src, res, gate_t, up_t, down_t, ident, loads):
    ph = Phase(nc, "qff")
    HF = QF // 2
    xs = ph.sb("xs", [P, 2, KD, P])
    qx = Quantiser(ph, 1, QF)
    xq = ph.sb("xq", [P, D])
    xq_t = ph.sb("xq_t", [P, KD, P])
    silu = ph.sb("silu", [P, 2, HF])
    hid = ph.sb("hid", [P, QF])
    hq = ph.sb("hq", [P, QF])
    hq_t = ph.sb("hq_t", [P, QFT, P])
    mag_x, sign_x, level_x = ph.sb("mag_x", [P, D]), ph.sb("sign_x", [P, D]), ph.sb("level_x", [P, D])
    gu_ps = ph.psum("gu_ps", [P, 4, 512])
    x_ps = ph.psum("x_ps", [P, 512])
    h_ps = ph.psum("h_ps", [P, 2, 512])
    y_ps = ph.psum("y_ps", [P, KD, P])
    staged, x_turned, x_abs, x_sign, x_quant = (ph.sem(n) for n in ("staged", "x_turned", "x_abs", "x_sign", "x_quant"))
    xq_turned, xq_kept, gu_ready, silu_ready = (ph.sem(n) for n in ("xq_turned", "xq_kept", "gu_ready", "silu_ready"))
    h_ready, h_abs, h_sign, h_quant, hq_turned = (ph.sem(n) for n in ("h_ready", "h_abs", "h_sign", "h_quant", "hq_turned"))
    x_hold = ph.sem("x_hold")
    hq_kept, y_ready, added, loaded = (ph.sem(n) for n in ("hq_kept", "y_ready", "added", "loaded"))
    widths = [min(P, QF - t * P) for t in range(QFT)]
    PER = 2 * Quantiser.STEPS

    with nc.Block() as block:
        @block.sync
        def _(sp):
            for d, source in loads:
                sp.dma_start(d, source).then_inc(loaded, 16)
            wait(sp, loaded, 16 * len(loads))

        @block.gpsimd
        def _(pool):
            def stage(b):
                wait(pool, x_turned, 2 * b)
                for t in range(2):
                    for k in range(KD):
                        op = pool.tensor_copy(xs[:, t, k, :], tokens(src, k, b)[:, :, t * P:(t + 1) * P].rearrange("p a t -> p (a t)"))
                op.then_inc(staged, 1)
            stage(0)
            with pool.Fori(1, SLOTS) as b:
                stage(b)

        @block.tensor
        def _(pe):
            def turn_x(n, t, b):
                pe.wait_ge(staged, b + 1)
                wait(pe, xq_kept, n - 1)
                for k in range(KD):
                    mm = pe.transpose(x_ps[:, k * P:(k + 1) * P], xs[:, t, k, :], ident[:, :])
                mm.then_inc(x_turned, 1)

            def turn_xq(n):
                pe.wait_ge(x_quant, n + 1)
                for k in range(KD):
                    mm = pe.transpose(x_ps[:, D + k * P:D + (k + 1) * P], xq[:, k * P:(k + 1) * P], ident[:, :])
                mm.then_inc(xq_turned, 1)

            def gate_up(n):
                pe.wait_ge(xq_kept, n + 1)
                wait(pe, h_ready, n)
                for i, w in enumerate((gate_t, up_t)):
                    for half in range(2):
                        for k in range(KD):
                            mm = pe.matmul(gu_ps[:, 2 * i + half, 0:HF], xq_t[:, k, :], w[:, k, half * HF:(half + 1) * HF],
                                           start=(k == 0), stop=(k == KD - 1))
                mm.then_inc(gu_ready, 1)

            def down(n):
                pe.wait_ge(h_quant, n + 1)
                wait(pe, hq_kept, n)
                for t in range(QFT):
                    w = widths[t]
                    mm = pe.transpose(h_ps[0:w, t // 4, (t % 4) * P:(t % 4 + 1) * P], hq[:, t * P:t * P + w], ident[:, :])
                mm.then_inc(hq_turned, 1)
                pe.wait_ge(hq_kept, n + 1)
                wait(pe, added, n)
                for m in range(KD):
                    for t in range(QFT):
                        w = widths[t]
                        mm = pe.matmul(y_ps[:, m, :], down_t[0:w, t, m * P:(m + 1) * P], hq_t[0:w, t, :],
                                       start=(t == 0), stop=(t == QFT - 1))
                mm.then_inc(y_ready, 1)

            def tile(n, t, b):
                turn_xq(n + 1)
                gate_up(n + 1)
                turn_x(n + 2, t, b + 1)
                down(n)

            turn_x(0, 0, 0)
            turn_xq(0)
            gate_up(0)
            turn_x(1, 1, 0)
            tile(0, 0, 0)
            tile(1, 1, 0)
            with pe.Fori(1, B) as b:
                tile(2 * b, 0, b)
                tile(2 * b + 1, 1, b)

        @block.scalar
        def _(act):
            def split_x(n):
                act.wait_ge(x_turned, n + 1)
                wait(act, x_quant, n)
                act.activation(mag_x[:, :], x_ps[:, 0:D], ACT.Abs).then_inc(x_abs, 1)
                act.activation(sign_x[:, :], x_ps[:, 0:D], ACT.Sign).then_inc(x_sign, 1)

            def keep_xq(n):
                act.wait_ge(xq_turned, n + 1)
                wait(act, gu_ready, n)
                act.activation(xq_t[:, :, :].rearrange("p k t -> p (k t)"), x_ps[:, D:2 * D], ACT.Copy).then_inc(xq_kept, 1)

            def gate(n):
                act.wait_ge(gu_ready, n + 1)
                wait(act, h_ready, n)
                act.activation(silu[:, :, :], gu_ps[:, 0:2, 0:HF], ACT.Silu).then_inc(silu_ready, 1)

            def keep_hq(n):
                act.wait_ge(hq_turned, n + 1)
                wait(act, y_ready, n)
                act.activation(hq_t[:, 0:4, :].rearrange("p t n -> p (t n)"), h_ps[:, 0, :], ACT.Copy)
                act.activation(hq_t[:, 4, :], h_ps[:, 1, 0:P], ACT.Copy)
                act.activation(hq_t[0:widths[5], 5, :], h_ps[0:widths[5], 1, P:2 * P], ACT.Copy).then_inc(hq_kept, 1)

            def split_h(n):
                act.wait_ge(h_ready, n + 1)
                wait(act, h_quant, n)
                act.activation(qx.mag[:, 0, :], hid[:, :], ACT.Abs).then_inc(h_abs, 1)
                act.activation(qx.sign[:, 0, :], hid[:, :], ACT.Sign).then_inc(h_sign, 1)

            def tile(n):
                split_h(n)
                keep_xq(n + 1)
                gate(n + 1)
                split_x(n + 2)
                keep_hq(n)

            split_x(0)
            keep_xq(0)
            gate(0)
            split_x(1)
            tile(0)
            with act.Fori(1, 2 * B) as n:
                tile(n)

        @block.vector
        def _(dve):
            def x_steps(n):
                return 0 if isinstance(n, int) and n == 0 else PER * n - Quantiser.STEPS

            def quantise_x(n):
                dve.wait_ge(x_abs, n + 1)
                dve.wait_ge(x_sign, n + 1)
                wait(dve, xq_turned, n)
                dve.sem_inc(x_hold, 1)
                qx(dve, xq[:, :], mag_x[:, :], sign_x[:, :], level_x[:, :], x_steps(n))
                dve.sem_inc(x_quant, 1)

            def multiply(n):
                dve.wait_ge(silu_ready, n + 1)
                wait(dve, h_abs, n)
                wait(dve, h_sign, n)
                dve.tensor_tensor(hid[:, :].rearrange("p (a f) -> p a f", a=2), silu[:, :, :], gu_ps[:, 2:4, 0:HF], ALU.mult)\
                    .then_inc(h_ready, 1)

            def quantise_h(n):
                dve.wait_ge(h_abs, n + 1)
                dve.wait_ge(h_sign, n + 1)
                wait(dve, hq_turned, n)
                dve.sem_inc(x_hold, 1)
                qx(dve, hq[:, :], qx.mag[:, 0, :], qx.sign[:, 0, :], qx.level[:, 0, :], PER * n + PER)
                dve.sem_inc(h_quant, 1)

            def add(n, t, b):
                dve.wait_ge(y_ready, n + 1)
                for m in range(KD):
                    r = tokens(res, m, b)[:, :, t * P:(t + 1) * P].rearrange("p a t -> p (a t)")
                    op = dve.tensor_tensor(r, r, y_ps[:, m, :], ALU.add)
                op.then_inc(added, 1)

            def tile(n, t, b, first=False):
                multiply(n)
                quantise_x(n + 1)
                quantise_h(n)
                if not first:
                    add(n - 1, 1 - t, b - (1 - t))

            quantise_x(0)
            tile(0, 0, 0, first=True)
            tile(1, 1, 0)
            with dve.Fori(1, B) as b:
                tile(2 * b, 0, b)
                tile(2 * b + 1, 1, b)
            add(2 * B - 1, 1, B - 1)
    ph.close()


def program(nc, dram, out):
    whole = ExitStack()

    def sb(name, shape, dt=F32):
        return whole.enter_context(nc.sbuf_tensor(name, shape, dt))

    h = sb("h", [P, KD, SLOTS * PAD])
    xr = sb("xr", [P, KD, SLOTS * PAD])
    att_hi, att_lo = sb("att_hi", [P, ATT_COLS], F32R), sb("att_lo", [P, ATT_COLS], F32R)
    ident, ones = sb("ident", [P, P]), sb("ones", [P, P])
    full = sb("full", [P, P])
    expo, no_bias = sb("expo", [P, 2 * HG]), sb("no_bias", [P, KD])
    consts = {"ident": ident, "ones": ones, "full": full, "expo": expo}
    tok_g, tok_b = sb("tok_g", [P, KD]), sb("tok_b", [P, KD])
    mask = sb("mask", [P, QT, S])
    tower = Phase(nc, "tower")
    xn = tower.sb("xn", [P, KD, SLOTS * PAD])
    rows = lambda w: w.rearrange("(k p) n -> p k n", p=P)

    def layer_of(name, l):
        v = dram[name][bass.ds(l, 1)]
        return v.rearrange("a b -> (a b)") if len(v.shape) == 2 else v.rearrange("a b c -> (a b) c")

    first = [(ident[:, :], dram["ident"]), (ones[:, :], dram["ones"]), (tok_g[:, :], dram["tok_g"]),
             (tok_b[:, :], dram["tok_b"]), (mask[:, :, :], dram["causal"])]
    with nc.Block() as block:
        @block.vector
        def _(dve):
            dve.memset(full[:, :], 1.0)
            dve.memset(expo[:, :], -0.5)
            dve.memset(no_bias[:, :], 0.0)
            for x in (h, xr, xn):
                dve.memset(x[:, :, :], 0.0)
    token_features(nc, dram, xn, first)
    layer_norm(nc, "tok_norm", xn, h, consts, gamma=tok_g, beta=tok_b)

    merge_lora(nc, (dram["l0_w"], att_hi, att_lo), [dram[n] for n in ("l0_a_in", "l0_b_in", "l0_a_out", "l0_b_out")])
    layer_norm(nc, "norm0", h, xn, consts)
    bias = Phase(nc, "bias")
    bias_qk, bias_v, bias_out = bias.sb("qk", [P, 2 * INNER // P]), bias.sb("v", [P, INNER]), bias.sb("out", [P, KD])
    with nc.Block() as block:
        @block.vector
        def _(dve):
            dve.memset(bias_qk[:, :], 0.0)
            dve.memset(bias_v[:, :], 0.0)
    attention(nc, "attn0", "plain", xn, h, att_hi, att_lo, ident, mask, L0_HD ** -0.5, [(0, P), (0, S)],
              bias_qk, bias_v, no_bias, None, None, None, [])

    layer_norm(nc, "norm1", h, xn, consts)
    quant = Phase(nc, "quant")
    gate_t, up_t = quant.sb("gate_t", [P, KD, QF]), quant.sb("up_t", [P, KD, QF])
    down_t = quant.sb("down_t", [P, QFT, D])
    quantise_weights(nc, gate_t, up_t, down_t, dram, ident)
    quantised_feed_forward(nc, xn, h, gate_t, up_t, down_t, ident,
                           [(bias_qk[:, :], dram["l1_b_qk"]), (bias_v[:, :], dram["l1_b_v"].unsqueeze(0).broadcast_to([P, INNER])),
                            (bias_out[:, :], dram["l1_b_out"]), (mask[:, :, :], dram["open"]),
                            (tok_g[:, :], dram["l1_g"]), (tok_b[:, :], dram["l1_b"])])
    quant.close()


    layer_norm(nc, "norm2", h, xr, consts, weights=(dram["l1_w"], att_hi, att_lo))
    layer_norm(nc, "norm3", xr, xn, consts, gamma=tok_g, beta=tok_b)
    attention(nc, "attn1", "plain", xn, h, att_hi, att_lo, ident, mask, HD ** -0.5, [(0, S), (0, S)],
              bias_qk, bias_v, bias_out, None, None, None, [])
    bias.close()
    layer_norm(nc, "norm4", h, xr, consts, weights=(layer_of("w", 0), att_hi, att_lo))
    tower.close()

    ff_hi, ff_lo = sb("ff_hi", [P, FF_COLS], F32R), sb("ff_lo", [P, FF_COLS], F32R)
    b1, b2 = sb("b1", [P, 2 * FT]), sb("b2", [P, KD])
    ln_g, ln_b = sb("ln_g", [P, KD]), sb("ln_b", [P, KD])
    ff_xn = sb("ff_xn", [P, KD, CH])
    cos_base, sin_base = sb("cos_base", [P, QT, 2, HD]), sb("sin_base", [P, QT, 2, HD])
    cos, sin = sb("cos", [P, QT, 2, HD]), sb("sin", [P, QT, 2, HD])
    head_scale, head_scale_swapped = sb("head_scale", [P, 2, HD]), sb("head_scale_swapped", [P, 2, HD])

    def attention_loads(l):
        half = HD // 2
        loads = []
        for i, name in enumerate(("q_scale", "k_scale")):
            v = layer_of(name, l)
            loads.append((head_scale[:, i, :], v.unsqueeze(0).broadcast_to([P, HD])))
            for lo in (0, half):
                loads.append((head_scale_swapped[:, i, lo:lo + half],
                              v[half - lo:HD - lo].unsqueeze(0).broadcast_to([P, half])))
        return loads

    def feed_forward_loads(l):
        return [(dst[:, :], layer_of(name, l)) for dst, name in ((b1, "b1"), (b2, "b2"), (ln_g, "ln_g"), (ln_b, "ln_b"))]

    def rotary_tables(pool, sem, value):
        pool.wait_ge(sem, value)
        for t in range(QT):
            pool.tensor_tensor(cos[:, t, :, :], cos_base[:, t, :, :], head_scale[:, :, :], ALU.mult)
            pool.tensor_tensor(sin[:, t, :, :], sin_base[:, t, :, :], head_scale_swapped[:, :, :], ALU.mult)

    pre = Phase(nc, "pre")
    pre_loaded = pre.sem("loaded")
    pre_loads = [(cos_base[:, :, :, :], dram["cos"]), (sin_base[:, :, :, :], dram["sin"]), (mask[:, :, :], dram["local"])]
    pre_loads += attention_loads(0)
    with nc.Block() as block:
        @block.sync
        def _(sp):
            for dst, source in pre_loads:
                sp.dma_start(dst, source).then_inc(pre_loaded, 16)
            sp.wait_ge(pre_loaded, 16 * len(pre_loads))

        @block.gpsimd
        def _(pool):
            rotary_tables(pool, pre_loaded, 16 * len(pre_loads))
    pre.close()

    with nc.Fori(0, DEPTH) as l:
        attention(nc, "local", "rope", xr, xr, att_hi, att_lo, ident, mask, 8.0, [(0, P), (WINDOW, S)],
                  None, None, no_bias, cos, sin, expo, feed_forward_loads(l), (layer_of("w_ff", l), ff_hi, ff_lo), (consts, ff_xn))
        feed_forward(nc, "ff", xr, ff_hi, ff_lo, b1, b2, ln_g, ln_b, consts, attention_loads((l + 1) % DEPTH), (layer_of("w", (l + 1) % DEPTH), att_hi, att_lo), rotary_tables, ff_xn)

    end = Phase(nc, "end")
    summed, stored = end.sem("summed"), end.sem("stored")
    with nc.Block() as block:
        @block.vector
        def _(dve):
            for k in range(KD):
                dve.tensor_tensor(tokens(h, k, 0, B), tokens(h, k, 0, B), tokens(xr, k, 0, B), ALU.add).then_inc(summed, 1)

        @block.sync
        def _(sp):
            for k in range(KD):
                sp.wait_ge(summed, k + 1)
                sp.dma_start(out[k * P:(k + 1) * P, :].rearrange("p (b t) -> p b t", t=S), tokens(h, k, 0, B)).then_inc(stored, 16)
            sp.wait_ge(stored, 16 * KD)
    end.close()
    whole.close()


def constants():
    i, j = np.arange(S)[:, None], np.arange(S)[None, :]
    tiled = lambda x: np.ascontiguousarray(x.reshape(QT, P, *x.shape[1:]).swapaxes(0, 1), dtype=np.float32)
    additive = lambda allowed: tiled(np.where(allowed, 0.0, LOW))
    half = np.arange(0, HD, 2, dtype=np.float32)
    inv_freq = (1.0 / 10000.0 ** (half / HD)).astype(np.float32)
    t = np.arange(S, dtype=np.float32)
    freqs = (t[:, None] * inv_freq[None, :]).astype(np.float32)
    freqs = np.concatenate([freqs, freqs], -1)
    base = ((half + 0.4 * HD) / (1.4 * HD)).astype(np.float32)
    power = (t - S // 2) / (WINDOW // 2)
    scale = (base[None, :] ** power[:, None]).astype(np.float32)
    scale = np.concatenate([scale, scale], -1)
    sign = np.where(np.arange(HD) < HD // 2, -1.0, 1.0)
    cos = np.stack([np.cos(freqs) * scale, np.cos(freqs) / scale], 1)
    sin = np.stack([np.sin(freqs) * scale * sign, np.sin(freqs) / scale * sign], 1)
    return {
        "ident": np.eye(P, dtype=np.float32), "ones": np.full((P, P), 1.0 / D, np.float32),
        "iota": np.concatenate([np.arange(32), np.arange(V)]).astype(np.float32)[:, None],
        "causal": additive(j <= i), "open": additive(i + j >= 0), "local": additive((j <= i) & (j >= i - WINDOW)),
        "cos": tiled(cos), "sin": tiled(sin),
    }


def laid_out(x):
    def spread(w):
        o = np.zeros((*w.shape[:-1], H, HD), w.dtype)
        o[..., :L0_HD] = w.reshape(*w.shape[:-1], H, L0_HD)
        return o.reshape(*w.shape[:-1], INNER)

    def by_partition(v):
        n = -(-v.shape[-1] // P)
        o = np.zeros((*v.shape[:-1], n * P), v.dtype)
        o[..., :v.shape[-1]] = v
        return o.reshape(*v.shape[:-1], n, P).swapaxes(-1, -2)

    def packed(*ws):
        out = []
        for w in ws:
            w = w.reshape(*w.shape[:-2], w.shape[-2] // P, P, w.shape[-1]).swapaxes(-3, -2)
            out.append(w.reshape(*w.shape[:-2], -1))
        return np.concatenate(out, -1)

    def padded(w, axis):
        width = [(0, 0)] * w.ndim
        width[axis] = (0, FT * P - FF)
        return np.pad(w, width)

    W1 = padded(x["L1_ffn_W1"].reshape(DEPTH, D, 2, FF), 3).reshape(DEPTH, D, 2 * FT * P)
    a = {
        "w": packed(x["L1_ffn_Wqkv"], x["L1_ffn_Wo"]), "w_ff": packed(W1, padded(x["L1_ffn_W2"], 1)),
        "x": x["x"].reshape(-1), "mask": x["mask_BS_i1_0"].reshape(-1),
        "emb_t": packed(np.concatenate([x["L0_tok_emb"].T, np.zeros((D, 32), np.float32)], 1)).reshape(P, KD, 32 + V),
        "pca_t": np.concatenate([np.zeros((PCA, 32), np.float32), x["L0_tok_pca_lookup"].T], 1),
        "proj_t": packed(x["L0_tok_proj_w"].T).reshape(P, KD, PCA), "fus_w": x["L0_tok_fus_w"],
        "proj_b": by_partition(x["L0_tok_proj_b"]), "fus_b": by_partition(x["L0_tok_fus_b"]), "tok_g": by_partition(x["L0_tok_ln_g"]), "tok_b": by_partition(x["L0_tok_ln_b"]),
        "l0_w": packed(np.concatenate([spread(x[f"L0_attn_w{c}"].T) for c in "qkv"], 1), spread(x["L0_attn_wo"]).T),
        "l0_a_in": np.stack([x[f"L0_attn_a{c}"] for c in "qkv"], 1),
        "l0_b_in": np.concatenate([spread(x[f"L0_attn_b{c}"].T) for c in "qkv"], 1),
        "l0_a_out": spread(x["L0_attn_ao"]), "l0_b_out": x["L0_attn_bo"].T,
        "w_gate": x["L0_ffn_w_gate"], "w_up": x["L0_ffn_w_up"], "w_down": x["L0_ffn_w_down"],
        "l1_w": packed(x["L1_attn_w_qkv"], x["L1_attn_w_out"]), "l1_b_qk": by_partition(x["L1_attn_b_qkv"][:2 * INNER]), "l1_b_v": x["L1_attn_b_qkv"][2 * INNER:],
        "l1_b_out": by_partition(x["L1_attn_b_out"]), "l1_g": by_partition(x["L1_attn_ln_gamma"]), "l1_b": by_partition(x["L1_attn_ln_beta"]),
    }
    for n in ("q_scale", "k_scale"):
        a[n] = x[f"L1_ffn_{n}"]
    for n in ("ln_g", "ln_b", "b2"):
        a[n] = by_partition(x[f"L1_ffn_{n}"])
    b1 = x["L1_ffn_b1"]
    a["b1"] = np.concatenate([by_partition(b1[:, :FF]), by_partition(b1[:, FF:])], -1)
    return a


def build(nc, arrays):
    dram = {n: nc.dram_tensor(f"in_{n}", a.shape, mybir.dt.from_np(a.dtype), kind="ExternalInput").ap()
            for n, a in arrays.items()}
    out = nc.dram_tensor("out_0", (D, B * S), F32, kind="ExternalOutput").ap()
    program(nc, dram, out)


def kernel(**inputs):
    import concourse.bacc as bacc
    from concourse.bass_utils import run_bass_kernel_spmd

    arrays = {n: np.ascontiguousarray(a) for n, a in {**laid_out({k: np.asarray(v) for k, v in inputs.items()}), **constants()}.items()}
    nc = bacc.Bacc("TRN2", target_bir_lowering=False, num_devices=1)
    build(nc, arrays)
    r = run_bass_kernel_spmd(nc, [{f"in_{n}": a for n, a in arrays.items()}], core_ids=[0])
    return np.ascontiguousarray(r.results[0]["out_0"].reshape(D, B, S).transpose(1, 2, 0))
```
